# Optimizing a Trainium2 kernel written in Bass

```python
import numpy as np
import jax
import jax.numpy as jnp

def _softmax(x, axis=-1):
    return jax.nn.softmax(x, axis=axis)

def _gelu(x):
    return jax.nn.gelu(x, approximate=True)

def _silu(x):
    return jax.nn.silu(x)

def _sigmoid(x):
    return jax.nn.sigmoid(x)

def _layernorm(x, axis=-1, eps=1e-05):
    m = jnp.mean(x, axis=axis, keepdims=True)
    v = jnp.var(x, axis=axis, keepdims=True)
    return (x - m) / jnp.sqrt(v + eps)

def _scatter_add(tgt, idx, src, axis=0):
    return tgt.at[idx].add(src)

def _segment_sum(src, seg, n):
    return jax.ops.segment_sum(src, seg, n)
kernel_name = 'mk_gnn_ffn_d2_gnn_r8_b38b88'

def setup_inputs(seed: int=0):
    np.random.seed(seed)
    _w = jnp.asarray

    def _rec_inputs():
        import jax
        import jax.numpy as jnp
        _gk = jax.random.key(seed)
        x = -0.0003713 + 1 * jax.random.normal(jax.random.fold_in(_gk, 1), (6250, 256), jnp.float32)
        _s = jax.random.randint(jax.random.fold_in(_gk, 2), (100000,), 0, 6250, jnp.int32)
        _d = jax.random.randint(jax.random.fold_in(_gk, 3), (100000,), 0, 6250, jnp.int32)
        _loop = jnp.arange(6250, dtype=jnp.int32)
        src = jnp.concatenate([_s, _d, _loop])
        dst = jnp.concatenate([_d, _s, _loop])
        _o = jnp.argsort(dst, stable=True)
        src = src[_o]
        dst = dst[_o]
        return (x, src, dst)
    x, src, dst = _rec_inputs()

    def _L0_gnn_setup():
        import jax, jax.numpy as jnp
        import numpy as np
        N = 6250
        E = 100000
        HIDDEN = 256
        HEADS = 8
        HEAD_DIM = HIDDEN // HEADS

        def _linear_params(key, fan_in, fan_out):
            k1, k2 = jax.random.split(key)
            s = 1.0 / np.sqrt(fan_in)
            W = jax.random.uniform(k1, (fan_in, fan_out), jnp.float32, -s, s)
            b = jax.random.uniform(k2, (fan_out,), jnp.float32, -s, s)
            return (W, b)
        key = jax.random.key(seed)
        ks = jax.random.split(key, 7)
        h = jax.random.normal(ks[0], (N, HIDDEN), jnp.float32)
        row = jnp.sort(jax.random.randint(ks[1], (E,), 0, N))
        col = jax.random.randint(ks[2], (E,), 0, N)
        Wq, bq = _linear_params(ks[3], HIDDEN, HIDDEN)
        Wk, bk = _linear_params(ks[4], HIDDEN, HIDDEN)
        Wv, bv = _linear_params(ks[5], HIDDEN, HIDDEN)
        Wo, bo = _linear_params(ks[6], HIDDEN, HIDDEN)
        return dict(h=h, row=row, col=col, Wq=Wq, bq=bq, Wk=Wk, bk=bk, Wv=Wv, bv=bv, Wo=Wo, bo=bo)
    _L0_gnn_all = _L0_gnn_setup()
    _L0_gnn_in = {k: v for k, v in _L0_gnn_all.items() if k in ('Wq', 'bq', 'Wk', 'bk', 'Wv', 'bv', 'Wo', 'bo')}
    del _L0_gnn_all

    def _L0_ffn_setup():
        import jax, jax.numpy as jnp
        import numpy as np
        E = 8
        K = 2
        D = 256
        H = 512
        DOUT = 256
        EPS = 1e-05
        key = jax.random.key(seed)
        ks = jax.random.split(key, 9)
        s = 0.02
        return {'x': jax.random.normal(ks[0], (4, 1024, D), jnp.float32), 'gamma': 1.0 + 0.05 * jax.random.normal(ks[1], (D,), jnp.float32), 'beta': 0.05 * jax.random.normal(ks[2], (D,), jnp.float32), 'Wr': 0.01 * jax.random.normal(ks[3], (D, E), jnp.float32), 'br': jnp.zeros((E,), jnp.float32), 'W1': s * jax.random.normal(ks[4], (E, D, H), jnp.float32), 'b1': s * jax.random.normal(ks[5], (E, H), jnp.float32), 'W2': s * jax.random.normal(ks[6], (E, H, DOUT), jnp.float32), 'b2': s * jax.random.normal(ks[7], (E, DOUT), jnp.float32)}
    _L0_ffn_all = _L0_ffn_setup()
    _L0_ffn_in = {k: v for k, v in _L0_ffn_all.items() if k in ('gamma', 'beta', 'Wr', 'br', 'W1', 'b1', 'W2', 'b2')}
    del _L0_ffn_all

    def _L1_gnn_setup():
        import jax, jax.numpy as jnp
        import numpy as np
        N_NODES = 12500
        N_EDGES = 400000
        CHANNEL = 256
        REDUCTION = 2
        N_GRAPHS = 64
        key = jax.random.key(seed)
        ks = jax.random.split(key, 10)
        C, R = (CHANNEL, CHANNEL // REDUCTION)
        x = jax.random.normal(ks[0], (N_NODES, C), dtype=jnp.float32)
        batch = jnp.sort(jax.random.randint(ks[1], (N_NODES,), 0, N_GRAPHS, dtype=jnp.int32))
        edge_index = jax.random.randint(ks[2], (2, N_EDGES), 0, N_NODES, dtype=jnp.int32)
        w1 = jax.random.normal(ks[3], (C, R), dtype=jnp.float32) / np.sqrt(C)
        b1 = jnp.zeros((R,), dtype=jnp.float32)
        w2 = jax.random.normal(ks[4], (R, C), dtype=jnp.float32) / np.sqrt(R)
        b2 = jnp.zeros((C,), dtype=jnp.float32)
        gcn_w = jax.random.normal(ks[5], (C, 1), dtype=jnp.float32) / np.sqrt(C)
        gcn_b = jnp.zeros((1,), dtype=jnp.float32)
        return {'x': x, 'batch': batch, 'edge_index': edge_index, 'num_graphs': N_GRAPHS, 'w1': w1, 'b1': b1, 'w2': w2, 'b2': b2, 'gcn_w': gcn_w, 'gcn_b': gcn_b}
    _L1_gnn_all = _L1_gnn_setup()
    _L1_gnn_in = {k: v for k, v in _L1_gnn_all.items() if k in ('w1', 'b1', 'w2', 'b2', 'gcn_w', 'gcn_b')}
    del _L1_gnn_all

    def _L1_ffn_setup():
        import jax, jax.numpy as jnp
        import numpy as np
        C = 256
        HID = 1024
        E = 8
        TEMP = 1.0
        key = jax.random.key(seed)
        ks = jax.random.split(key, 7)
        x = jax.random.normal(ks[0], (8, 2048, C), dtype=jnp.float32)
        W1 = jax.random.normal(ks[1], (C, HID), dtype=jnp.float32) * 0.02
        b1 = jnp.zeros((HID,), dtype=jnp.float32)
        Wg = jax.random.normal(ks[2], (HID, E), dtype=jnp.float32) * 0.02
        bg = jnp.zeros((E,), dtype=jnp.float32)
        Wd = jax.random.normal(ks[3], (E, HID, C), dtype=jnp.float32) * 0.02
        bd = jnp.zeros((E, C), dtype=jnp.float32)
        return {'x': x, 'W1': W1, 'b1': b1, 'Wg': Wg, 'bg': bg, 'Wd': Wd, 'bd': bd}
    _L1_ffn_all = _L1_ffn_setup()
    _L1_ffn_in = {k: v for k, v in _L1_ffn_all.items() if k in ('W1', 'b1', 'Wg', 'bg', 'Wd', 'bd')}
    del _L1_ffn_all
    return {'x': x, 'src': src, 'dst': dst, 'L0_gnn_Wq': _L0_gnn_in['Wq'], 'L0_gnn_bq': _L0_gnn_in['bq'], 'L0_gnn_Wk': _L0_gnn_in['Wk'], 'L0_gnn_bk': _L0_gnn_in['bk'], 'L0_gnn_Wv': _L0_gnn_in['Wv'], 'L0_gnn_bv': _L0_gnn_in['bv'], 'L0_gnn_Wo': _L0_gnn_in['Wo'], 'L0_gnn_bo': _L0_gnn_in['bo'], 'L0_ffn_gamma': _L0_ffn_in['gamma'], 'L0_ffn_beta': _L0_ffn_in['beta'], 'L0_ffn_Wr': _L0_ffn_in['Wr'], 'L0_ffn_br': _L0_ffn_in['br'], 'L0_ffn_W1': _L0_ffn_in['W1'], 'L0_ffn_b1': _L0_ffn_in['b1'], 'L0_ffn_W2': _L0_ffn_in['W2'], 'L0_ffn_b2': _L0_ffn_in['b2'], 'L1_gnn_w1': _L1_gnn_in['w1'], 'L1_gnn_b1': _L1_gnn_in['b1'], 'L1_gnn_w2': _L1_gnn_in['w2'], 'L1_gnn_b2': _L1_gnn_in['b2'], 'L1_gnn_gcn_w': _L1_gnn_in['gcn_w'], 'L1_gnn_gcn_b': _L1_gnn_in['gcn_b'], 'L1_ffn_W1': _L1_ffn_in['W1'], 'L1_ffn_b1': _L1_ffn_in['b1'], 'L1_ffn_Wg': _L1_ffn_in['Wg'], 'L1_ffn_bg': _L1_ffn_in['bg'], 'L1_ffn_Wd': _L1_ffn_in['Wd'], 'L1_ffn_bd': _L1_ffn_in['bd']}

def reference(x, src, dst, L0_gnn_Wq, L0_gnn_bq, L0_gnn_Wk, L0_gnn_bk, L0_gnn_Wv, L0_gnn_bv, L0_gnn_Wo, L0_gnn_bo, L0_ffn_gamma, L0_ffn_beta, L0_ffn_Wr, L0_ffn_br, L0_ffn_W1, L0_ffn_b1, L0_ffn_W2, L0_ffn_b2, L1_gnn_w1, L1_gnn_b1, L1_gnn_w2, L1_gnn_b2, L1_gnn_gcn_w, L1_gnn_gcn_b, L1_ffn_W1, L1_ffn_b1, L1_ffn_Wg, L1_ffn_bg, L1_ffn_Wd, L1_ffn_bd):
    import jax
    import jax.numpy as jnp

    def _L0_gnn_ref(h, row, col, Wq, bq, Wk, bk, Wv, bv, Wo, bo):
        import jax, jax.numpy as jnp
        import numpy as np
        N = 6250
        E = 100000
        HIDDEN = 256
        HEADS = 8
        HEAD_DIM = HIDDEN // HEADS

        def _linear_params(key, fan_in, fan_out):
            k1, k2 = jax.random.split(key)
            s = 1.0 / np.sqrt(fan_in)
            W = jax.random.uniform(k1, (fan_in, fan_out), jnp.float32, -s, s)
            b = jax.random.uniform(k2, (fan_out,), jnp.float32, -s, s)
            return (W, b)
        n = h.shape[0]
        scaling = HEAD_DIM ** (-0.5)
        q = (h @ Wq + bq).reshape(n, HEADS, HEAD_DIM) * scaling
        k = (h @ Wk + bk).reshape(n, HEADS, HEAD_DIM)
        v = (h @ Wv + bv).reshape(n, HEADS, HEAD_DIM)
        s = jnp.einsum('ehd,ehd->eh', q[row], k[col])
        m = jax.ops.segment_max(s, row, num_segments=n)
        p = jnp.exp(s - m[row])
        denom = jax.ops.segment_sum(p, row, num_segments=n)
        attn = p / denom[row]
        out = jax.ops.segment_sum(attn[:, :, None] * v[col], row, num_segments=n)
        return out.reshape(n, HIDDEN) @ Wo + bo

    def _L0_ffn_ref(x, gamma, beta, Wr, br, W1, b1, W2, b2):
        import jax, jax.numpy as jnp
        import numpy as np
        E = 8
        K = 2
        D = 256
        H = 512
        DOUT = 256
        EPS = 1e-05
        mu = jnp.mean(x, axis=-1, keepdims=True)
        var = jnp.mean(jnp.square(x - mu), axis=-1, keepdims=True)
        xn = (x - mu) * jax.lax.rsqrt(var + EPS) * gamma + beta
        logits = jnp.einsum('bsd,de->bse', xn, Wr) + br
        top_vals, top_idx = jax.lax.top_k(logits, K)
        w = jax.nn.softmax(top_vals, axis=-1)
        w_full = jnp.einsum('bsk,bske->bse', w, jax.nn.one_hot(top_idx, E, dtype=w.dtype))
        y = jnp.zeros(x.shape[:-1] + (DOUT,), x.dtype)
        for e in range(E):
            h = jax.nn.gelu(jnp.einsum('bsd,dh->bsh', xn, W1[e]) + b1[e], approximate=False)
            y_e = jnp.einsum('bsh,hd->bsd', h, W2[e]) + b2[e]
            y = y + y_e * w_full[..., e, None]
        return y

    def _L1_gnn_ref(x, batch, edge_index, num_graphs, w1, b1, w2, b2, gcn_w, gcn_b):
        import jax, jax.numpy as jnp
        import numpy as np
        N_NODES = 12500
        N_EDGES = 400000
        CHANNEL = 256
        REDUCTION = 2
        N_GRAPHS = 64
        N, C = x.shape
        seg_sum = jax.ops.segment_sum(x, batch, num_segments=num_graphs)
        cnt = jax.ops.segment_sum(jnp.ones((N,), x.dtype), batch, num_segments=num_graphs)
        chn_mean = seg_sum / jnp.maximum(cnt, 1.0)[:, None]
        gate = jax.nn.sigmoid(jax.nn.relu(chn_mean @ w1 + b1) @ w2 + b2)
        chn_se = x * gate[batch]
        h = x @ gcn_w
        loop = jnp.arange(N, dtype=edge_index.dtype)
        src = jnp.concatenate([edge_index[0], loop])
        dst = jnp.concatenate([edge_index[1], loop])
        deg = jax.ops.segment_sum(jnp.ones_like(src, dtype=x.dtype), dst, num_segments=N)
        dis = jnp.where(deg > 0, jax.lax.rsqrt(jnp.maximum(deg, 1e-12)), 0.0)
        msg = h[src] * (dis[src] * dis[dst])[:, None]
        spa = jax.nn.sigmoid(jax.ops.segment_sum(msg, dst, num_segments=N) + gcn_b)
        return x * spa + x + chn_se

    def _L1_ffn_ref(x, W1, b1, Wg, bg, Wd, bd):
        import jax, jax.numpy as jnp
        import numpy as np
        C = 256
        HID = 1024
        E = 8
        TEMP = 1.0
        orig_shape = x.shape
        xf = x.reshape(-1, orig_shape[-1])
        H = jax.nn.gelu(xf @ W1 + b1, approximate=False)
        probs = jax.nn.softmax((H @ Wg + bg) / TEMP, axis=-1)
        assign = jnp.argmax(probs, axis=-1)
        out = jnp.zeros_like(xf)
        for e in range(Wd.shape[0]):
            y = H @ Wd[e] + bd[e]
            sel = (assign == e)[:, None]
            out = out + jnp.where(sel, probs[:, e:e + 1] * y, 0.0)
        return out.reshape(orig_shape)
    edge_index = jnp.stack([src, dst])
    batch0 = jnp.zeros((6250,), jnp.int32)
    x = x + _L0_gnn_ref(_layernorm(x, axis=-1), src, dst, L0_gnn_Wq, L0_gnn_bq, L0_gnn_Wk, L0_gnn_bk, L0_gnn_Wv, L0_gnn_bv, L0_gnn_Wo, L0_gnn_bo)
    x = x + _L0_ffn_ref(_layernorm(x, axis=-1)[None], L0_ffn_gamma, L0_ffn_beta, L0_ffn_Wr, L0_ffn_br, L0_ffn_W1, L0_ffn_b1, L0_ffn_W2, L0_ffn_b2)[0]
    x = x + _L1_gnn_ref(_layernorm(x, axis=-1), batch0, edge_index, 64, L1_gnn_w1, L1_gnn_b1, L1_gnn_w2, L1_gnn_b2, L1_gnn_gcn_w, L1_gnn_gcn_b)
    x = x + _L1_ffn_ref(_layernorm(x, axis=-1)[None], L1_ffn_W1, L1_ffn_b1, L1_ffn_Wg, L1_ffn_bg, L1_ffn_Wd, L1_ffn_bd)[0]
    return x

_drawn_inputs = setup_inputs


def setup_inputs(seed=0):
    import zlib

    import numpy as np

    out = dict(_drawn_inputs(seed))
    spreads = {'L0_ffn_br': (0.0, 0.1),
     'L1_gnn_b1': (0.0, 0.8),
     'L1_gnn_b2': (0.0, 0.8),
     'L1_ffn_b1': (0.0, 0.8),
     'L1_ffn_bg': (0.0, 0.8),
     'L1_ffn_bd': (0.0, 0.8)}
    factors = {'L0_gnn_bq': 8.0,
     'L0_gnn_bk': 8.0,
     'L0_gnn_bv': 2.847,
     'L0_ffn_gamma': 5.969,
     'L0_ffn_beta': 4.98,
     'L0_ffn_b1': 8.0,
     'L0_ffn_b2': 4.214,
     'L1_gnn_w1': 8.0,
     'L1_gnn_w2': 7.742,
     'L1_gnn_gcn_w': 3.612,
     'L1_ffn_W1': 7.876,
     'L1_ffn_Wg': 8.0,
     'L1_ffn_Wd': 8.0}
    for name, (base, spread) in spreads.items():
        noise = np.random.default_rng([zlib.crc32(name.encode()), seed]).standard_normal(out[name].shape)
        drawn = base * np.exp(spread * noise) if base else spread * noise
        out[name] = jnp.asarray(drawn.astype(out[name].dtype))
    for name, factor in factors.items():
        out[name] = (out[name] * factor).astype(out[name].dtype)
    return out
```

```python
from contextlib import ExitStack

import concourse.bass as bass
from concourse import mybir

F32 = mybir.dt.float32
BF16 = mybir.dt.bfloat16
I32 = mybir.dt.int32
I16 = mybir.dt.int16
ALU = mybir.AluOpType
ACT = mybir.ActivationFunctionType
AX = mybir.AxisListType

P = 128
N = 6250
D = 256
DC = D // P
HEADS, HD = 8, 32
E = 206250
NB = 50
FULL = N // P
TAIL = N - FULL * P
ET = -(-E // P)
ETAIL = E - (ET - 1) * P
CH = 16
CI = 104
NI = CH * CI
IG = NI // P
assert NI >= ET + FULL + 1
PAD_ROW = 8192
BIG = 1.0e38
CL = CI * P
EPS = 1e-5
EX = 8
QUAD = 4
RING = 4
AW = D + HEADS + 1


class Stage:

    def __init__(self, nc):
        self.nc = nc
        self.keep = ExitStack()
        self.taken = []

    def sem(self, name):
        self.taken.append(self.nc.alloc_semaphore(name=name))
        return self.taken[-1]

    def hand_back(self):
        self.nc.all_engine_barrier()
        self.nc.clear_and_free_semaphores(self.taken)
        self.nc.all_engine_barrier()
        self.taken = []


def chained(engine, sem, start=0):
    count = [start]

    def link(instruction):
        count[0] += 1
        instruction.then_inc(sem, 1)
        engine.wait_ge(sem, count[0])

    return link


def constants(nc, st, ident, identb, iota_free, iota_part, ones, order):
    made = st.sem("const_made")
    with nc.Block() as block:
        @block.gpsimd
        def _(pool):
            link = chained(pool, made)
            link(nc.gpsimd.memset(ones[:], 1.0))
            link(nc.gpsimd.iota(iota_free[:], pattern=[[1, P]], base=0, channel_multiplier=0,
                                allow_small_or_imprecise_dtypes=True))
            link(nc.gpsimd.iota(iota_part[:], pattern=[[0, 1]], base=0, channel_multiplier=1,
                                allow_small_or_imprecise_dtypes=True))
            link(nc.gpsimd.tensor_scalar(ident[:], iota_free[:], iota_part[:, 0:1], None, ALU.is_equal))
            link(nc.gpsimd.tensor_copy(identb[:], ident[:]))
            link(nc.gpsimd.iota(order[:], pattern=[[-1, EX]], base=EX, channel_multiplier=0,
                                allow_small_or_imprecise_dtypes=True))


def layernorm_stats(nc, st, name, x, stats, mean, rstd, tmp, inner=None):
    inner_done = st.sem(f"{name}_inner_done")
    stat_done = st.sem(f"{name}_stat_done")
    chain = st.sem(f"{name}_chain")
    var_ready = st.sem(f"{name}_var_ready")
    root_ready = st.sem(f"{name}_root_ready")
    with nc.Block() as block:
        @block.vector
        def _(dve):
            with dve.Fori(0, NB) as b:
                of = x[:, bass.ds(b, 1), :].rearrange("p a d -> p (a d)")
                if inner:
                    nc.vector.tensor_scalar(inner[2][:], of, inner[0][:, bass.ds(b, 1)], inner[1][:, bass.ds(b, 1)],
                                            ALU.subtract, ALU.mult).then_inc(inner_done, 1)
                    dve.wait_ge(inner_done, b + 1)
                    of = inner[2][:]
                nc.vector.bn_stats(stats[:, bass.ds(b, 1), :].rearrange("p a s -> p (a s)"), of).then_inc(stat_done, 1)
                if inner:
                    dve.wait_ge(stat_done, b + 1)
            dve.wait_ge(stat_done, NB)
            link = chained(dve, chain)
            link(nc.vector.tensor_tensor(mean[:], stats[:, :, 1], stats[:, :, 4], ALU.add))
            link(nc.vector.tensor_scalar(mean[:], mean[:], 0.5, None, ALU.mult))
            link(nc.vector.tensor_tensor(tmp[:], stats[:, :, 1], stats[:, :, 4], ALU.subtract))
            link(nc.vector.tensor_tensor(tmp[:], tmp[:], tmp[:], ALU.mult))
            link(nc.vector.tensor_tensor(rstd[:], stats[:, :, 2], stats[:, :, 5], ALU.add))
            link(nc.vector.tensor_scalar(rstd[:], rstd[:], 1.0 / D, EPS, ALU.mult, ALU.add))
            link(nc.vector.scalar_tensor_tensor(out=rstd[:], in0=tmp[:], scalar=0.25, in1=rstd[:],
                                                op0=ALU.mult, op1=ALU.add))
            nc.vector.memset(tmp[:, 0:1], 0.0).then_inc(var_ready, 1)
            dve.wait_ge(root_ready, 1)
            link(nc.vector.reciprocal(rstd[:], tmp[:]))

        @block.scalar
        def _(act):
            act.wait_ge(var_ready, 1)
            nc.scalar.activation(tmp[:], rstd[:], ACT.Sqrt).then_inc(root_ready, 1)


def load_x(nc, st, name, x_dram, x):
    zeroed = st.sem(f"{name}_zeroed")
    loaded = st.sem(f"{name}_loaded")
    with nc.Block() as block:
        @block.vector
        def _(dve):
            nc.vector.memset(x[:, FULL:NB, :], 0.0).then_inc(zeroed, 1)

        @block.sync
        def _(sp):
            sp.dma_start(x[:, 0:FULL, :], x_dram[0:FULL * P, :].rearrange("(b p) d -> p b d", p=P)).then_inc(loaded, 16)
            sp.wait_ge(zeroed, 1)
            sp.dma_start(x[0:TAIL, FULL, :], x_dram[FULL * P:N, :]).then_inc(loaded, 16)
            sp.wait_ge(loaded, 32)


def project_qkv(nc, st, x, mean, rstd, ident, ones, weights, biases, q_all, kv_dram):
    with ExitStack() as ctx:
        w = ctx.enter_context(nc.sbuf_tensor("wqkv", [P, DC, 3 * D], F32))
        bias = ctx.enter_context(nc.sbuf_tensor("bqkv", [1, 3 * D], F32))
        xn = ctx.enter_context(nc.sbuf_tensor("qkv_xn", [P, 2, D], F32))
        xt = ctx.enter_context(nc.sbuf_tensor("qkv_xt", [P, 2, D], F32))
        kv = ctx.enter_context(nc.sbuf_tensor("qkv_kv", [P, 2, 2 * D], F32))
        pt = ctx.enter_context(nc.psum_tensor("qkv_pt", [P, 2, 512], F32))
        pq = ctx.enter_context(nc.psum_tensor("qkv_pq", [P, 2, 512], F32))
        pkv = ctx.enter_context(nc.psum_tensor("qkv_pkv", [P, 2, 512], F32))
        w_loaded = st.sem("qkv_w_loaded")
        xn_ready = st.sem("qkv_xn_ready")
        xt_psum = st.sem("qkv_xt_psum")
        xt_ready = st.sem("qkv_xt_ready")
        products = st.sem("qkv_products")
        q_out = st.sem("qkv_q_out")
        kv_out = st.sem("qkv_kv_out")
        stored = [st.sem(f"qkv_stored{k}") for k in range(2)]
        with nc.Block() as block:
            @block.sync
            def _(sp):
                for j, (wm, bm) in enumerate(zip(weights, biases)):
                    sp.dma_start(w[:, :, j * D:(j + 1) * D], wm.rearrange("(c p) n -> p c n", p=P)).then_inc(w_loaded, 16)
                    sp.dma_start(bias[0:1, j * D:(j + 1) * D], bm.rearrange("(a n) -> a n", a=1)).then_inc(w_loaded, 16)
                with sp.Fori(0, NB // 2) as h:
                    b = h * 2
                    for k in range(2):
                        sp.wait_ge(kv_out, b + k + 1)
                        for j in range(2):
                            sp.dma_start(kv_dram[j][bass.ds((b + k) * P, P), :],
                                         kv[:, k, j * D:(j + 1) * D]).then_inc(stored[k], 16)
                for k in range(2):
                    sp.wait_ge(stored[k], 32 * (NB // 2))

            @block.vector
            def _(dve):
                with dve.Fori(0, NB // 2) as h:
                    b = h * 2
                    for k in range(2):
                        dve.wait_ge(xt_psum, b)
                        nc.vector.tensor_scalar(xn[:, k, :], x[:, bass.ds(b + k, 1), :].rearrange("p a d -> p (a d)"),
                                                mean[:, bass.ds(b + k, 1)], rstd[:, bass.ds(b + k, 1)],
                                                ALU.subtract, ALU.mult).then_inc(xn_ready, 1)
                    for k in range(2):
                        dve.wait_ge(products, b + k + 1)
                        dve.wait_ge(stored[k], b * 16)
                        nc.vector.tensor_copy(kv[:, k, :], pkv[:, k, :]).then_inc(kv_out, 1)

            @block.tensor
            def _(pe):
                pe.wait_ge(w_loaded, 96)
                with pe.Fori(0, NB // 2) as h:
                    b = h * 2
                    for k in range(2):
                        pe.wait_ge(xn_ready, b + k + 1)
                        pe.wait_ge(xt_ready, b)
                        for c in range(DC):
                            last = nc.tensor.transpose(pt[:, k, c * P:(c + 1) * P], xn[:, k, c * P:(c + 1) * P], ident[:])
                        last.then_inc(xt_psum, 1)
                    for k in range(2):
                        pe.wait_ge(xt_ready, b + k + 1)
                        pe.wait_ge(q_out, b)
                        pe.wait_ge(kv_out, b)
                        for out, lo, hi in ((pq[:, k, 0:D], 0, D), (pkv[:, k, :], D, 3 * D)):
                            for c in range(DC):
                                nc.tensor.matmul(out, xt[:, k, c * P:(c + 1) * P], w[:, c, lo:hi], start=(c == 0), stop=False)
                            last = nc.tensor.matmul(out, ones[0:1, :], bias[0:1, lo:hi], start=False, stop=True)
                        last.then_inc(products, 1)

            @block.scalar
            def _(act):
                with act.Fori(0, NB // 2) as h:
                    b = h * 2
                    for k in range(2):
                        act.wait_ge(xt_psum, b + k + 1)
                        act.wait_ge(products, b)
                        nc.scalar.copy(xt[:, k, :], pt[:, k, 0:D]).then_inc(xt_ready, 1)
                    for k in range(2):
                        act.wait_ge(products, b + k + 1)
                        nc.scalar.activation(q_all[:, bass.ds(b + k, 1), :].rearrange("p a d -> p (a d)"), pq[:, k, 0:D], ACT.Copy, scale=float(HD) ** -0.5).then_inc(q_out, 1)


def item_tables(nc, st, row_in, col_in, scratch, ident, ones, rel, col):
    RP = 125
    RE = E // RP
    assert RP * RE == E
    with ExitStack() as ctx:
        def sb(name, shape, dt=F32):
            return ctx.enter_context(nc.sbuf_tensor(f"it_{name}", shape, dt))

        raw = sb("raw", [RP, RE], I32)
        rows = sb("rows", [RP, RE])
        below = sb("below", [RP, RE])
        bound = sb("bound", [P, NB])
        count = sb("count", [P, NB])
        padding = sb("padding", [1, 2 * P], I32)
        ptr = sb("ptr", [P, NB], I32)
        up = sb("up", [P, NB], I32)
        first = sb("first", [P, NB])
        behind = sb("behind", [P, NB])
        many = sb("many", [P, FULL + 1])
        ends = sb("ends", [P, FULL + 1])
        shift = sb("shift", [P, FULL + 1])
        item = sb("item", [P, IG])
        block_of = sb("block_of", [P, IG])
        block_int = sb("block_int", [P, IG], I32)
        tile_of = sb("tile_of", [P, IG])
        tile_int = sb("tile_int", [P, IG], I32)
        table = sb("table", [P, IG, FULL + 1])
        got_row = sb("got_row", [P, IG, P], I32)
        got_col = sb("got_col", [P, IG, P], I32)
        rowf = sb("rowf", [P, IG, P])
        key = sb("key", [P, IG, P], I16)
        colf = sb("colf", [P, IG, P])
        total = ctx.enter_context(nc.psum_tensor("it_total", [P, 512], F32))
        turned = ctx.enter_context(nc.psum_tensor("it_turned", [P, 2, 512], F32))
        loaded = st.sem("it_loaded")
        pad_made = st.sem("it_pad_made")
        padded = st.sem("it_padded")
        made = st.sem("it_made")
        counted = st.sem("it_counted")
        chain = st.sem("it_chain")
        counts_done = st.sem("it_counts_done")
        summed = st.sem("it_summed")
        tiles_ready = st.sem("it_tiles_ready")
        gathered = st.sem("it_gathered")
        tables_ready = st.sem("it_tables_ready")
        turned_ready = st.sem("it_turned_ready")
        turned_out = st.sem("it_turned_out")
        stored = st.sem("it_stored")
        NBLK = FULL + 1
        with nc.Block() as block:
            @block.sync
            def _(sp):
                sp.dma_start(raw[:], row_in.rearrange("(p e) -> p e", p=RP)).then_inc(loaded, 16)
                for n, (src, dst) in enumerate(((row_in, scratch["rows"]), (col_in, scratch["cols"]))):
                    flat = dst.rearrange("t e -> (t e)")
                    sp.dma_start(flat[0:E].rearrange("(a e) -> a e", a=50), src.rearrange("(a e) -> a e", a=50)).then_inc(padded, 16)
                    if n == 0:
                        sp.wait_ge(pad_made, 2)
                    sp.dma_start(dst[ET - 1:ET, ETAIL:P], padding[0:1, n * P + ETAIL:(n + 1) * P]).then_inc(padded, 16)
                sp.wait_ge(tables_ready, 1)
                sp.dma_start(scratch["item_block"].rearrange("(g p) -> p g", p=P), block_int[:], allow_slow_non_contiguous=True).then_inc(stored, 16)
                sp.dma_start(scratch["keys"].rearrange("(g p) e -> p g e", p=P), key[:]).then_inc(stored, 16)
                sp.wait_ge(stored, 32)

            @block.gpsimd
            def _(pool):
                nc.gpsimd.memset(padding[0:1, 0:P], PAD_ROW - 1).then_inc(pad_made, 1)
                nc.gpsimd.memset(padding[0:1, P:2 * P], 0).then_inc(pad_made, 1)
                nc.gpsimd.iota(bound[:], pattern=[[P, NB]], base=0, channel_multiplier=0,
                               allow_small_or_imprecise_dtypes=True).then_inc(made, 1)
                nc.gpsimd.iota(item[:], pattern=[[P, IG]], base=0, channel_multiplier=1,
                               allow_small_or_imprecise_dtypes=True).then_inc(made, 1)
                pool.wait_ge(padded, 64)
                pool.wait_ge(tiles_ready, 1)
                for g in range(IG):
                    for got, name in ((got_row, "rows"), (got_col, "cols")):
                        nc.gpsimd.indirect_dma_start(got[:, g, :], None, scratch[name],
                                                     bass.IndirectOffsetOnAxis(ap=tile_int[:, g:g + 1], axis=0)).then_inc(gathered, 16)

            @block.tensor
            def _(pe):
                pe.wait_ge(counts_done, 1)
                nc.tensor.matmul(total[:, 0:NB], ones[0:RP, :], count[0:RP, :], start=True, stop=True).then_inc(summed, 1)
                pe.wait_ge(tables_ready, 1)
                for n in range(2 * IG):
                    if n >= 2:
                        pe.wait_ge(turned_out, n - 1)
                    of = rowf if n % 2 == 0 else colf
                    nc.tensor.transpose(turned[:, n % 2, 0:P], of[:, n // 2, :], ident[:]).then_inc(turned_ready, 1)

            @block.vector
            def _(dve):
                link = chained(dve, chain)
                dve.wait_ge(made, 2)
                dve.wait_ge(loaded, 16)
                link(nc.vector.tensor_copy(rows[:], raw[:]))
                with dve.Fori(0, NB) as b:
                    nc.vector.tensor_scalar(below[:], rows[:], bound[0:RP, bass.ds(b, 1)], None, ALU.is_lt).then_inc(counted, 1)
                    dve.wait_ge(counted, 2 * b + 1)
                    nc.vector.tensor_reduce(count[0:RP, bass.ds(b, 1)], below[:], AX.X, ALU.add).then_inc(counted, 1)
                    dve.wait_ge(counted, 2 * b + 2)
                nc.vector.memset(many[:], 0.0).then_inc(counts_done, 1)
                dve.wait_ge(summed, 1)
                link(nc.vector.tensor_copy(ptr[:], total[:, 0:NB]))
                link(nc.vector.tensor_scalar(behind[:], total[:, 0:NB], float(P - 1), None, ALU.add))
                link(nc.vector.tensor_copy(up[:], behind[:]))
                link(nc.vector.tensor_scalar(ptr[:], ptr[:], 7, None, ALU.arith_shift_right))
                link(nc.vector.tensor_scalar(up[:], up[:], 7, None, ALU.arith_shift_right))
                link(nc.vector.tensor_copy(first[:], ptr[:]))
                link(nc.vector.tensor_copy(behind[:], up[:]))
                link(nc.vector.tensor_copy(count[:], total[:, 0:NB]))
                link(nc.vector.tensor_tensor(many[:], behind[:, 1:NBLK + 1], first[:, 0:NBLK], ALU.subtract))
                link(nc.vector.tensor_tensor(shift[:], count[:, 1:NBLK + 1], count[:, 0:NBLK], ALU.is_gt))
                link(nc.vector.tensor_tensor(many[:], many[:], shift[:], ALU.mult))
                link(nc.vector.tensor_tensor_scan(ends[:], ones[:, 0:NBLK], many[:], 0.0, ALU.mult, ALU.add))
                link(nc.vector.tensor_tensor(shift[:], first[:, 0:NBLK], ends[:], ALU.subtract))
                link(nc.vector.tensor_tensor(shift[:], shift[:], many[:], ALU.add))
                wide = [P, IG, NBLK]
                ends_b = ends[:].unsqueeze(1).to_broadcast(wide)
                shift_b = shift[:].unsqueeze(1).to_broadcast(wide)
                link(nc.vector.tensor_tensor(table[:], ends_b, item[:].unsqueeze(2).to_broadcast(wide), ALU.is_le))
                link(nc.vector.tensor_reduce(block_of[:], table[:], AX.X, ALU.add))
                link(nc.vector.tensor_scalar(tile_of[:], block_of[:], float(P), None, ALU.mult))
                link(nc.vector.tensor_tensor(table[:], bound[:, 0:NBLK].unsqueeze(1).to_broadcast(wide),
                                             tile_of[:].unsqueeze(2).to_broadcast(wide), ALU.is_equal))
                link(nc.vector.tensor_tensor(table[:], table[:], shift_b, ALU.mult))
                link(nc.vector.tensor_reduce(tile_of[:], table[:], AX.X, ALU.add))
                link(nc.vector.tensor_tensor(tile_of[:], tile_of[:], item[:], ALU.add))
                link(nc.vector.tensor_scalar(tile_of[:], tile_of[:], float(ET - 1), None, ALU.min))
                link(nc.vector.tensor_copy(block_int[:], block_of[:]))
                nc.vector.tensor_copy(tile_int[:], tile_of[:]).then_inc(tiles_ready, 1)
                dve.wait_ge(gathered, 16 * 2 * IG)
                link(nc.vector.tensor_copy(rowf[:], got_row[:]))
                link(nc.vector.tensor_copy(colf[:], got_col[:]))
                link(nc.vector.tensor_scalar(tile_of[:], block_of[:], float(NBLK), float(PAD_ROW), ALU.is_equal, ALU.mult))
                link(nc.vector.tensor_tensor(key[:], rowf[:], tile_of[:].unsqueeze(2).to_broadcast([P, IG, P]), ALU.add))
                link(nc.vector.tensor_scalar(tile_of[:], block_of[:], float(P), None, ALU.mult))
                nc.vector.tensor_tensor(rowf[:], rowf[:], tile_of[:].unsqueeze(2).to_broadcast([P, IG, P]),
                                        ALU.subtract).then_inc(tables_ready, 1)
                for n in range(2 * IG):
                    dve.wait_ge(turned_ready, n + 1)
                    to = rel if n % 2 == 0 else col
                    nc.vector.tensor_copy(to[:, (n // 2) * P:(n // 2 + 1) * P], turned[:, n % 2, 0:P]).then_inc(turned_out, 1)




def load_blocks(nc, item_block, q, engine):
    _, values = nc.values_load_multi_w_load_instructions(
        item_block[0:1, bass.ds(q * QUAD, QUAD)], engines=[engine], min_val=0, max_val=NB - 1,
        skip_runtime_bounds_check_because="item_tables counts at most FULL + 1 block ends before an item")
    return values


def edge_scores(nc, st, q_all, k_dram, rel, col, item_block, iota_free, ident, scores):
    with ExitStack() as ctx:
        def sb(name, shape, dt=F32):
            return ctx.enter_context(nc.sbuf_tensor(f"sc_{name}", shape, dt))

        kg = sb("kg", [P, RING, QUAD, D])
        index = sb("index", [P, RING, QUAD], I32)
        hot = sb("hot", [P, 2, QUAD, P])
        hot_t = sb("hot_t", [P, 2, QUAD, P])
        product = sb("product", [P, QUAD, D])
        pt = ctx.enter_context(nc.psum_tensor("sc_pt", [P, 2, 512], F32))
        pq = ctx.enter_context(nc.psum_tensor("sc_pq", [P, 2, 2, 512], F32))
        gathered = [st.sem(f"sc_gathered{k}") for k in range(RING * QUAD)]
        index_ready = st.sem("sc_index_ready")
        hot_ready = st.sem("sc_hot_ready")
        hot_turned = st.sem("sc_hot_turned")
        hot_t_ready = st.sem("sc_hot_t_ready")
        q_expanded = st.sem("sc_q_expanded")
        product_ready = st.sem("sc_product_ready")
        reduced = st.sem("sc_reduced")
        QUADS = NI // QUAD
        with nc.Block() as block:
            @block.gpsimd
            def _(pool):
                nc.gpsimd.memset(col[:, NI:NI + QUAD], 0).then_inc(index_ready, 1)
                nc.gpsimd.tensor_copy(index[:, 0, :], col[:, 0:QUAD]).then_inc(index_ready, 1)
                with pool.Fori(0, QUADS // RING) as s:
                    for u in range(RING):
                        q = s * RING + u
                        pool.wait_ge(product_ready, q * 2)
                        pool.wait_ge(index_ready, q + 2)
                        nc.gpsimd.tensor_copy(index[:, (u + 1) % RING, :],
                                              col[:, bass.ds((q + 1) * QUAD, QUAD)]).then_inc(index_ready, 1)
                        for j in range(QUAD):
                            nc.gpsimd.indirect_dma_start(
                                kg[:, u, j, :], None, k_dram,
                                bass.IndirectOffsetOnAxis(ap=index[:, u, j:j + 1], axis=0)).then_inc(gathered[u * QUAD + j], 16)

            @block.tensor
            def _(pe):
                def turn(u):
                    for j in range(QUAD):
                        last = nc.tensor.transpose(pt[:, u, j * P:(j + 1) * P], hot[:, u, j, :], ident[:])
                    last.then_inc(hot_turned, 1)

                pe.wait_ge(hot_ready, 1)
                turn(0)
                with pe.Fori(0, QUADS // 2) as s:
                    for u in range(2):
                        q = s * 2 + u
                        blk = load_blocks(nc, item_block, q, mybir.EngineType.PE)
                        pe.wait_ge(hot_t_ready, q + 1)
                        for half in range(2):
                            pe.wait_ge(product_ready, q * 2 + half + 1)
                            for j in (2 * half, 2 * half + 1):
                                last = nc.tensor.matmul(pq[:, u, half, (j % 2) * D:(j % 2 + 1) * D], hot_t[:, u, j, :],
                                                        q_all[:, bass.ds(blk[j], 1), :].rearrange("p a d -> p (a d)"),
                                                        start=True, stop=True)
                            last.then_inc(q_expanded, 1)
                            if half == 0:
                                pe.wait_ge(hot_ready, q + 2)
                                turn(1 - u)

            @block.scalar
            def _(act):
                def copy_turned(u):
                    nc.scalar.copy(hot_t[:, u, :, :].rearrange("p j n -> p (j n)"), pt[:, u, 0:QUAD * P]).then_inc(hot_t_ready, 1)

                act.wait_ge(hot_turned, 1)
                copy_turned(0)
                with act.Fori(0, QUADS // 2) as s:
                    for u in range(2):
                        q = s * 2 + u
                        act.wait_ge(q_expanded, q * 2)
                        act.wait_ge(hot_turned, q + 2)
                        copy_turned(1 - u)

            @block.vector
            def _(dve):
                def one_hots(q, u):
                    for j in range(QUAD):
                        last = nc.vector.tensor_scalar(hot[:, u, j, :], iota_free[:], rel[:, bass.ds(q * QUAD + j, 1)], None, ALU.is_equal)
                    last.then_inc(hot_ready, 1)

                nc.vector.memset(rel[:, NI:NI + QUAD], float(P)).then_inc(product_ready, 4)
                nc.vector.memset(product[:], 0.0).then_inc(reduced, 2)
                one_hots(0, 0)
                with dve.Fori(0, QUADS // RING) as s:
                    for v in range(RING):
                        q, u = s * RING + v, v % 2
                        dve.wait_ge(hot_turned, q)
                        one_hots(q + 1, 1 - u)
                        for half in range(2):
                            pair = slice(2 * half, 2 * half + 2)
                            dve.wait_ge(q_expanded, q * 2 + half + 1)
                            for j in (2 * half, 2 * half + 1):
                                dve.wait_ge(gathered[v * QUAD + j], s * 16 + 16)
                            dve.wait_ge(reduced, q * 2 + half + 1)
                            nc.vector.tensor_tensor(product[:, pair, :].rearrange("p j d -> p (j d)"),
                                                    kg[:, v, pair, :].rearrange("p j d -> p (j d)"),
                                                    pq[:, u, half, :], ALU.mult).then_inc(product_ready, 1)
                            dve.wait_ge(product_ready, q * 2 + half + 5)
                            nc.vector.tensor_reduce(
                                scores[:, bass.ds(q * QUAD + 2 * half, 2), :].rearrange("p j h -> p (j h)"),
                                product[:, pair, :].rearrange("p j (h d) -> p (j h) d", h=HEADS),
                                AX.X, ALU.add).then_inc(reduced, 1)


def softmax_over_rows(nc, st, scores, keys, bounce, ident):
    view = scores[:].rearrange("p (c g) h -> p g c h", c=CH)
    largest = scores[:].rearrange("p i h -> p (i h)")
    keys_flat = keys.rearrange("i e -> (i e)")
    GROUPS = CI // QUAD
    with ExitStack() as ctx:
        def sb(name, shape, dt=F32):
            return ctx.enter_context(nc.sbuf_tensor(f"sm_{name}", shape, dt))

        line = sb("line", [P, CL])
        key = sb("key", [P, CL], I16)
        cut = sb("cut", [P, CL + 1], BF16)
        part = sb("part", [P, 2, QUAD * P])
        end_keys = sb("end_keys", [HEADS, 2, CH], I16)
        end_keyf = sb("end_keyf", [HEADS, 2, CH])
        same = sb("same", [HEADS, CH])
        forth = sb("forth", [HEADS, CH])
        back = sb("back", [HEADS, CH])
        ends = sb("ends", [HEADS, CH])
        reach = sb("reach", [HEADS, CH])
        carried = sb("carried", [HEADS, CH])
        carry = sb("carry", [P, 2])
        turned = ctx.enter_context(nc.psum_tensor("sm_turned", [P, 2, 512], F32))
        part_ready = st.sem("sm_part_ready")
        turned_ready = st.sem("sm_turned_ready")
        turned_out = st.sem("sm_turned_out")
        keys_loaded = st.sem("sm_keys_loaded")
        chain = st.sem("sm_chain")
        bounced = st.sem("sm_bounced")
        to_bounce = st.sem("sm_to_bounce")
        differences = st.sem("sm_differences")
        with nc.Block() as block:
            @block.sync
            def _(sp):
                for c in range(CH):
                    sp.dma_start(key[c * HEADS:(c + 1) * HEADS, :],
                                 keys_flat[c * CL:(c + 1) * CL].unsqueeze(0).to_broadcast([HEADS, CL])).then_inc(keys_loaded, 16)
                for n, at in enumerate((0, CL - 1)):
                    ends_of = keys_flat.rearrange("(c l) -> c l", c=CH)[:, at:at + 1].rearrange("c o -> o c")
                    sp.dma_start(end_keys[:, n, :], ends_of.to_broadcast([HEADS, CH]),
                                 allow_slow_non_contiguous=True).then_inc(keys_loaded, 16)
                for n, at in enumerate((CL - 1, 0)):
                    sp.wait_ge(to_bounce, 2 * n + 1)
                    sp.dma_start(bounce[0], largest[:, at:at + 1]).then_inc(bounced, 16)
                    sp.wait_ge(bounced, 16 * (4 * n + 1))
                    sp.dma_start(ends[:], bounce[0].rearrange("(c h) o -> h (c o)", h=HEADS),
                                 allow_slow_non_contiguous=True).then_inc(bounced, 16)
                    sp.wait_ge(to_bounce, 2 * n + 2)
                    sp.wait_ge(bounced, 16 * (4 * n + 2))
                    sp.dma_start(bounce[1].rearrange("(c h) o -> h (c o)", h=HEADS), carried[:],
                                 allow_slow_non_contiguous=True).then_inc(bounced, 16)
                    sp.wait_ge(bounced, 16 * (4 * n + 3))
                    sp.dma_start(carry[:, n:n + 1], bounce[1]).then_inc(bounced, 16)

            @block.scalar
            def _(act):
                with act.Fori(0, GROUPS // 2) as s:
                    for u in range(2):
                        g = s * 2 + u
                        act.wait_ge(turned_ready, s * 2)
                        nc.scalar.copy(part[:, u, :].rearrange("p (g c h) -> p g c h", g=QUAD, c=CH),
                                       view[:, bass.ds(g * QUAD, QUAD), :, :]).then_inc(part_ready, 1)
                act.wait_ge(differences, 1)
                with act.Fori(0, GROUPS // 2) as s:
                    for u in range(2):
                        g = s * 2 + u
                        act.wait_ge(turned_ready, s * 2 + GROUPS)
                        nc.scalar.activation(part[:, u, :], line[:, bass.ds(g * QUAD * P, QUAD * P)], ACT.Exp).then_inc(part_ready, 1)

            @block.tensor
            def _(pe):
                with pe.Fori(0, GROUPS) as s:
                    for u in range(2):
                        pe.wait_ge(part_ready, s * 2 + u + 1)
                        pe.wait_ge(turned_out, s * 2)
                        for j in range(QUAD):
                            last = nc.tensor.transpose(turned[:, u, j * P:(j + 1) * P], part[:, u, j * P:(j + 1) * P], ident[:])
                        last.then_inc(turned_ready, 1)

            @block.vector
            def _(dve):
                link = chained(dve, chain)
                dve.wait_ge(keys_loaded, 16 * (CH + 2))
                link(nc.vector.memset(cut[:, 0:1], 0.0))
                link(nc.vector.memset(cut[:, CL:CL + 1], 0.0))
                link(nc.vector.tensor_tensor(cut[:, 1:CL], key[:, 1:CL], key[:, 0:CL - 1], ALU.not_equal))
                link(nc.vector.tensor_scalar(cut[:, 1:CL], cut[:, 1:CL], -BIG, None, ALU.mult))
                link(nc.vector.tensor_copy(end_keyf[:], end_keys[:]))
                link(nc.vector.memset(same[:], 1.0))
                link(nc.vector.tensor_tensor(same[:, 0:CH - 1], end_keyf[:, 0, 1:CH], end_keyf[:, 1, 0:CH - 1], ALU.not_equal))
                link(nc.vector.tensor_tensor(reach[:], end_keyf[:, 0, :], end_keyf[:, 1, :], ALU.not_equal))
                link(nc.vector.tensor_tensor(back[:], same[:], reach[:], ALU.max))
                link(nc.vector.memset(forth[:], 1.0))
                link(nc.vector.tensor_tensor(forth[:, 1:CH], same[:, 0:CH - 1], reach[:, 1:CH], ALU.max))
                for flags in (same, forth, back):
                    link(nc.vector.tensor_scalar(flags[:], flags[:], -BIG, None, ALU.mult))
                with dve.Fori(0, GROUPS // 2) as s:
                    for u in range(2):
                        g = s * 2 + u
                        dve.wait_ge(turned_ready, g + 1)
                        nc.vector.tensor_copy(line[:, bass.ds(g * QUAD * P, QUAD * P)], turned[:, u, :]).then_inc(turned_out, 1)
                dve.wait_ge(turned_out, GROUPS)

                link(nc.vector.tensor_tensor_scan(largest, cut[:, 0:CL], line[:], -BIG, ALU.add, ALU.max))
                nc.vector.memset(carried[:], -BIG).then_inc(to_bounce, 1)
                dve.wait_ge(bounced, 32)
                link(nc.vector.tensor_tensor_scan(reach[:], forth[:], ends[:], -BIG, ALU.add, ALU.max))
                nc.vector.tensor_tensor(carried[:, 1:CH], reach[:, 0:CH - 1], same[:, 0:CH - 1], ALU.add).then_inc(to_bounce, 1)
                dve.wait_ge(bounced, 64)
                link(nc.vector.tensor_tensor_scan(largest, cut[:, 0:CL], line[:], carry[:, 0:1], ALU.add, ALU.max))
                link(nc.vector.tensor_tensor_scan(largest[:, ::-1], cut[:, :0:-1], largest[:, ::-1], -BIG, ALU.add, ALU.max))
                nc.vector.memset(carried[:], -BIG).then_inc(to_bounce, 1)
                dve.wait_ge(bounced, 96)
                link(nc.vector.tensor_tensor_scan(reach[:, ::-1], back[:, ::-1], ends[:, ::-1], -BIG, ALU.add, ALU.max))
                nc.vector.tensor_tensor(carried[:, 0:CH - 1], reach[:, 1:CH], same[:, 0:CH - 1], ALU.add).then_inc(to_bounce, 1)
                dve.wait_ge(bounced, 128)
                link(nc.vector.tensor_tensor_scan(largest[:, ::-1], cut[:, :0:-1], largest[:, ::-1], carry[:, 1:2], ALU.add, ALU.max))
                nc.vector.tensor_tensor(line[:], line[:], largest, ALU.subtract).then_inc(differences, 1)
                dve.wait_ge(differences, 1)
                with dve.Fori(0, GROUPS // 2) as s:
                    for u in range(2):
                        g = s * 2 + u
                        dve.wait_ge(turned_ready, g + GROUPS + 1)
                        nc.vector.tensor_copy(view[:, bass.ds(g * QUAD, QUAD), :, :],
                                              turned[:, u, :].rearrange("p (g c h) -> p g c h", g=QUAD, c=CH)).then_inc(turned_out, 1)
                dve.wait_ge(turned_out, 2 * GROUPS)


def aggregate(nc, st, probs, v_dram, rel, col, item_block, iota_free, acc):
    with ExitStack() as ctx:
        def sb(name, shape, dt=F32):
            return ctx.enter_context(nc.sbuf_tensor(f"ag_{name}", shape, dt))

        vg = sb("vg", [P, RING, QUAD, D])
        index = sb("index", [P, RING, QUAD], I32)
        hot = sb("hot", [P, 2, QUAD, P])
        weighted = sb("weighted", [P, 2, QUAD, AW])
        sums = ctx.enter_context(nc.psum_tensor("ag_sums", [P, 2, QUAD, 512], F32))
        gathered = [st.sem(f"ag_gathered{k}") for k in range(RING * QUAD)]
        index_ready = st.sem("ag_index_ready")
        hot_ready = st.sem("ag_hot_ready")
        p_ready = st.sem("ag_p_ready")
        weighted_ready = st.sem("ag_weighted_ready")
        summed = st.sem("ag_summed")
        added = st.sem("ag_added")
        QUADS = NI // QUAD
        with nc.Block() as block:
            @block.gpsimd
            def _(pool):
                nc.gpsimd.memset(col[:, NI:NI + QUAD], 0).then_inc(index_ready, 1)
                nc.gpsimd.tensor_copy(index[:, 0, :], col[:, 0:QUAD]).then_inc(index_ready, 1)
                with pool.Fori(0, QUADS // RING) as s:
                    for u in range(RING):
                        q = s * RING + u
                        pool.wait_ge(weighted_ready, q * 2)
                        pool.wait_ge(index_ready, q + 2)
                        nc.gpsimd.tensor_copy(index[:, (u + 1) % RING, :],
                                              col[:, bass.ds((q + 1) * QUAD, QUAD)]).then_inc(index_ready, 1)
                        for j in range(QUAD):
                            nc.gpsimd.indirect_dma_start(
                                vg[:, u, j, :], None, v_dram,
                                bass.IndirectOffsetOnAxis(ap=index[:, u, j:j + 1], axis=0)).then_inc(gathered[u * QUAD + j], 16)

            @block.scalar
            def _(act):
                with act.Fori(0, QUADS // 2) as s:
                    for u in range(2):
                        q = s * 2 + u
                        act.wait_ge(added, q * 4)
                        nc.scalar.copy(weighted[:, u, :, D:D + HEADS], probs[:, bass.ds(q * QUAD, QUAD), :]).then_inc(p_ready, 1)

            @block.tensor
            def _(pe):
                with pe.Fori(0, QUADS // 2) as s:
                    for u in range(2):
                        q = s * 2 + u
                        pe.wait_ge(added, q * 4)
                        pe.wait_ge(hot_ready, q + 1)
                        pe.wait_ge(p_ready, q + 1)
                        for half in range(2):
                            pe.wait_ge(weighted_ready, q * 2 + half + 5)
                            for j in (2 * half, 2 * half + 1):
                                last = nc.tensor.matmul(sums[:, u, j, 0:AW], hot[:, u, j, :], weighted[:, u, j, :], start=True, stop=True)
                            last.then_inc(summed, 1)

            @block.vector
            def _(dve):
                def weigh(q, v, s):
                    u = v % 2
                    for j in range(QUAD):
                        last = nc.vector.tensor_scalar(hot[:, u, j, :], iota_free[:], rel[:, bass.ds(q * QUAD + j, 1)], None, ALU.is_equal)
                    last.then_inc(hot_ready, 1)
                    for half in range(2):
                        pair = slice(2 * half, 2 * half + 2)
                        for j in (2 * half, 2 * half + 1):
                            dve.wait_ge(gathered[v * QUAD + j], s * 16 + 16)
                        nc.vector.tensor_tensor(
                            weighted[:, u, pair, 0:D].rearrange("p j (h d) -> p j h d", h=HEADS),
                            vg[:, v, pair, :].rearrange("p j (h d) -> p j h d", h=HEADS),
                            probs[:, bass.ds(q * QUAD + 2 * half, 2), :].unsqueeze(3).to_broadcast([P, 2, HEADS, HD]),
                            ALU.mult).then_inc(weighted_ready, 1)

                def add(q, v):
                    u = v % 2
                    blk = load_blocks(nc, item_block, q, mybir.EngineType.DVE)
                    for j in range(QUAD):
                        dve.wait_ge(summed, q * 2 + j // 2 + 1)
                        dve.wait_ge(added, q * 4 + j + 4)
                        to = acc[:, bass.ds(blk[j], 1), :].rearrange("p a d -> p (a d)")
                        nc.vector.tensor_tensor(to, to, sums[:, u, j, 0:AW], ALU.add).then_inc(added, 1)

                nc.vector.memset(acc[:], 0.0).then_inc(added, 4)
                nc.vector.memset(weighted[:, :, :, AW - 1], 1.0).then_inc(weighted_ready, 4)
                weigh(0, 0, 0)
                with dve.Fori(0, QUADS // RING - 1) as s:
                    for v in range(RING):
                        q = s * RING + v
                        weigh(q + 1, (v + 1) % RING, s + (v + 1) // RING)
                        add(q, v)
                for v in range(RING):
                    q = QUADS - RING + v
                    if v + 1 < RING:
                        weigh(q + 1, v + 1, QUADS // RING - 1)
                    add(q, v)


def attention_output(nc, st, acc, x, wo, bo, ident, ones):
    with ExitStack() as ctx:
        w = ctx.enter_context(nc.sbuf_tensor("ao_w", [P, DC, D], F32))
        bias = ctx.enter_context(nc.sbuf_tensor("ao_b", [1, D], F32))
        share = ctx.enter_context(nc.sbuf_tensor("ao_share", [P, NB, HEADS], F32))
        rows = ctx.enter_context(nc.sbuf_tensor("ao_rows", [P, 2, D], F32))
        turned = ctx.enter_context(nc.sbuf_tensor("ao_turned", [P, 2, D], F32))
        pt = ctx.enter_context(nc.psum_tensor("ao_pt", [P, 2, 512], F32))
        po = ctx.enter_context(nc.psum_tensor("ao_po", [P, 2, 512], F32))
        w_loaded = st.sem("ao_w_loaded")
        chain = st.sem("ao_chain")
        rows_ready = st.sem("ao_rows_ready")
        pt_ready = st.sem("ao_pt_ready")
        turned_ready = st.sem("ao_turned_ready")
        po_ready = st.sem("ao_po_ready")
        added = st.sem("ao_added")
        with nc.Block() as block:
            @block.sync
            def _(sp):
                sp.dma_start(w[:], wo.rearrange("(c p) n -> p c n", p=P)).then_inc(w_loaded, 16)
                sp.dma_start(bias[:], bo.rearrange("(a n) -> a n", a=1)).then_inc(w_loaded, 16)

            @block.vector
            def _(dve):
                link = chained(dve, chain)
                link(nc.vector.tensor_scalar(share[:], acc[:, :, D:D + HEADS], 1e-30, None, ALU.max))
                link(nc.vector.reciprocal(share[:], share[:]))
                with dve.Fori(0, NB // 2) as h:
                    b = h * 2
                    for k in range(2):
                        dve.wait_ge(pt_ready, b)
                        nc.vector.tensor_tensor(
                            rows[:, k, :].rearrange("p (h d) -> p h d", h=HEADS),
                            acc[:, bass.ds(b + k, 1), 0:D].rearrange("p a (h d) -> p (a h) d", h=HEADS),
                            share[:, bass.ds(b + k, 1), :].rearrange("p a h -> p (a h)").unsqueeze(2).to_broadcast([P, HEADS, HD]),
                            ALU.mult).then_inc(rows_ready, 1)
                    for k in range(2):
                        dve.wait_ge(po_ready, b + k + 1)
                        to = x[:, bass.ds(b + k, 1), :].rearrange("p a d -> p (a d)")
                        nc.vector.tensor_tensor(to, to, po[:, k, 0:D], ALU.add).then_inc(added, 1)

            @block.scalar
            def _(act):
                with act.Fori(0, NB // 2) as h:
                    b = h * 2
                    for k in range(2):
                        act.wait_ge(po_ready, b)
                        act.wait_ge(pt_ready, b + k + 1)
                        nc.scalar.copy(turned[:, k, :], pt[:, k, 0:D]).then_inc(turned_ready, 1)

            @block.tensor
            def _(pe):
                pe.wait_ge(w_loaded, 32)
                with pe.Fori(0, NB // 2) as h:
                    b = h * 2
                    for k in range(2):
                        pe.wait_ge(turned_ready, b)
                        pe.wait_ge(rows_ready, b + k + 1)
                        for c in range(DC):
                            last = nc.tensor.transpose(pt[:, k, c * P:(c + 1) * P], rows[:, k, c * P:(c + 1) * P], ident[:])
                        last.then_inc(pt_ready, 1)
                    for k in range(2):
                        pe.wait_ge(added, b)
                        pe.wait_ge(turned_ready, b + k + 1)
                        for c in range(DC):
                            nc.tensor.matmul(po[:, k, 0:D], turned[:, k, c * P:(c + 1) * P], w[:, c, :], start=(c == 0), stop=False)
                        nc.tensor.matmul(po[:, k, 0:D], ones[0:1, :], bias[:], start=False, stop=True).then_inc(po_ready, 1)


def turn(nc, st, name, x, affine, xt, ident, scale=None, shift=None):
    with ExitStack() as ctx:
        rows = ctx.enter_context(nc.sbuf_tensor(f"{name}_rows", [P, 2, D], F32))
        pt = ctx.enter_context(nc.psum_tensor(f"{name}_pt", [P, 2, 512], F32))
        rows_step = st.sem(f"{name}_rows_step")
        pt_ready = st.sem(f"{name}_pt_ready")
        out = st.sem(f"{name}_out")
        steps = len(affine)
        with nc.Block() as block:
            @block.vector
            def _(dve):
                with dve.Fori(0, NB // 2) as h:
                    b = h * 2
                    for k in range(2):
                        dve.wait_ge(pt_ready, b)
                        of = x[:, bass.ds(b + k, 1), :].rearrange("p a d -> p (a d)")
                        for n, (mean, rstd) in enumerate(affine):
                            if n:
                                dve.wait_ge(rows_step, (b + k) * steps + n)
                            nc.vector.tensor_scalar(rows[:, k, :], of, mean[:, bass.ds(b + k, 1)], rstd[:, bass.ds(b + k, 1)],
                                                    ALU.subtract, ALU.mult).then_inc(rows_step, 1)
                            of = rows[:, k, :]

            @block.tensor
            def _(pe):
                with pe.Fori(0, NB // 2) as h:
                    b = h * 2
                    for k in range(2):
                        pe.wait_ge(out, b)
                        pe.wait_ge(rows_step, (b + k + 1) * steps)
                        for c in range(DC):
                            last = nc.tensor.transpose(pt[:, k, c * P:(c + 1) * P], rows[:, k, c * P:(c + 1) * P], ident[:])
                        last.then_inc(pt_ready, 1)

            @block.scalar
            def _(act):
                with act.Fori(0, NB // 2) as h:
                    b = h * 2
                    for k in range(2):
                        act.wait_ge(pt_ready, b + k + 1)
                        if scale is None:
                            nc.scalar.copy(xt[:, :, bass.ds((b + k) * P, P)],
                                           pt[:, k, 0:D].rearrange("p (c n) -> p c n", c=DC)).then_inc(out, 1)
                        else:
                            for c in range(DC):
                                last = nc.scalar.activation(xt[:, c, bass.ds((b + k) * P, P)], pt[:, k, c * P:(c + 1) * P],
                                                            ACT.Identity, bias=shift[:, c:c + 1], scale=scale[:, c:c + 1])
                            last.then_inc(out, 1)


def first_largest(dve, nc, link, values, mask, best, tmp, order, shape):
    link(nc.vector.tensor_reduce(best, values, AX.X, ALU.max))
    link(nc.vector.tensor_tensor(mask, values, best.unsqueeze(len(shape) - 1).to_broadcast(shape), ALU.is_equal))
    link(nc.vector.tensor_tensor(mask, mask, order, ALU.mult))
    link(nc.vector.tensor_reduce(tmp, mask, AX.X, ALU.max))
    link(nc.vector.tensor_tensor(mask, order, tmp.unsqueeze(len(shape) - 1).to_broadcast(shape), ALU.is_equal))


def route_two(nc, st, xt, wr, br, x, b2, order, ident, share):
    with ExitStack() as ctx:
        def sb(name, shape, dt=F32):
            return ctx.enter_context(nc.sbuf_tensor(f"ro_{name}", shape, dt))

        w = sb("w", [P, DC, EX])
        bias = sb("bias", [EX, 1])
        b2_sb = sb("b2", [EX, D])
        lines = sb("lines", [EX, 2, 2 * P])
        logits = sb("logits", [P, NB, EX])
        second = sb("second", [P, NB, EX])
        best = sb("best", [P, NB])
        next_best = sb("next_best", [P, NB])
        tmp = sb("tmp", [P, NB])
        part = sb("part", [P, 2, 2, EX])
        turned = sb("turned", [EX, 2, 2 * P])
        pl = ctx.enter_context(nc.psum_tensor("ro_pl", [EX, 2, 512], F32))
        pt = ctx.enter_context(nc.psum_tensor("ro_pt", [P, 2, 512], F32))
        po = ctx.enter_context(nc.psum_tensor("ro_po", [P, 2, 512], F32))
        loaded = st.sem("ro_loaded")
        product = st.sem("ro_product")
        line_ready = st.sem("ro_line_ready")
        line_turned = st.sem("ro_line_turned")
        logits_out = st.sem("ro_logits_out")
        chain = st.sem("ro_chain")
        gap_ready = st.sem("ro_gap_ready")
        ratio_ready = st.sem("ro_ratio_ready")
        part_ready = st.sem("ro_part_ready")
        part_turned = st.sem("ro_part_turned")
        turned_ready = st.sem("ro_turned_ready")
        bias_ready = st.sem("ro_bias_ready")
        bias_added = st.sem("ro_bias_added")
        with nc.Block() as block:
            @block.sync
            def _(sp):
                sp.dma_start(w[:], wr.rearrange("(c p) e -> p c e", p=P)).then_inc(loaded, 16)
                sp.dma_start(bias[:], br.rearrange("(e a) -> e a", a=1)).then_inc(loaded, 16)
                sp.dma_start(b2_sb[:], b2).then_inc(loaded, 16)

            @block.tensor
            def _(pe):
                pe.wait_ge(loaded, 48)

                def turn_lines(s):
                    pe.wait_ge(line_ready, s + 1)
                    pe.wait_ge(logits_out, s)
                    for j in range(2):
                        last = nc.tensor.matmul(pt[:, 0, j * EX:(j + 1) * EX], lines[:, 0, j * P:(j + 1) * P], ident[0:EX, 0:EX],
                                                start=True, stop=True)
                    last.then_inc(line_turned, 1)

                with pe.Fori(0, NB // 2) as s:
                    pe.wait_ge(line_ready, s)
                    for c in range(DC):
                        last = nc.tensor.matmul(pl[:, 0, 0:2 * P], w[:, c, :], xt[:, c, bass.ds(s * 2 * P, 2 * P)],
                                                start=(c == 0), stop=(c == DC - 1))
                    last.then_inc(product, 1)
                    turn_lines(s)
                with pe.Fori(0, NB // 2) as s:
                    pe.wait_ge(part_ready, s + 1)
                    for j in range(2):
                        last = nc.tensor.transpose(pt[0:EX, 1, j * P:(j + 1) * P], part[:, 0, j, :], ident[:])
                    last.then_inc(part_turned, 1)
                    pe.wait_ge(turned_ready, s + 1)
                    pe.wait_ge(bias_added, s)
                    for j in range(2):
                        last = nc.tensor.matmul(po[:, 0, j * D:(j + 1) * D], turned[:, 0, j * P:(j + 1) * P], b2_sb[:], start=True, stop=True)
                    last.then_inc(bias_ready, 1)

            @block.scalar
            def _(act):
                act.wait_ge(loaded, 48)
                with act.Fori(0, NB // 2) as s:
                    act.wait_ge(product, s + 1)
                    act.wait_ge(line_turned, s)
                    nc.scalar.activation(lines[:, 0, :], pl[:, 0, 0:2 * P], ACT.Identity, bias=bias[:, 0:1]).then_inc(line_ready, 1)
                act.wait_ge(gap_ready, 1)
                nc.scalar.activation(tmp[:], next_best[:], ACT.Exp).then_inc(ratio_ready, 1)
                with act.Fori(0, NB // 2) as s:
                    act.wait_ge(part_turned, s + 1)
                    act.wait_ge(bias_ready, s)
                    nc.scalar.copy(turned[:, 0, :], pt[0:EX, 1, 0:2 * P]).then_inc(turned_ready, 1)

            @block.vector
            def _(dve):
                with dve.Fori(0, NB // 2) as s:
                    dve.wait_ge(line_turned, s + 1)
                    nc.vector.tensor_copy(logits[:, bass.ds(s * 2, 2), :], pt[:, 0, 0:2 * EX].rearrange("p (j e) -> p j e", e=EX)).then_inc(logits_out, 1)
                dve.wait_ge(logits_out, NB // 2)
                link = chained(dve, chain)
                shape = [P, NB, EX]
                order_b = order[:].unsqueeze(1).to_broadcast(shape)
                first_largest(dve, nc, link, logits[:], share[:], best[:], tmp[:], order_b, shape)
                link(nc.vector.scalar_tensor_tensor(out=logits[:], in0=share[:], scalar=-BIG, in1=logits[:], op0=ALU.mult, op1=ALU.add))
                first_largest(dve, nc, link, logits[:], second[:], next_best[:], tmp[:], order_b, shape)
                nc.vector.tensor_tensor(next_best[:], next_best[:], best[:], ALU.subtract).then_inc(gap_ready, 1)
                dve.wait_ge(ratio_ready, 1)
                link(nc.vector.tensor_scalar(best[:], tmp[:], 1.0, None, ALU.add))
                link(nc.vector.reciprocal(best[:], best[:]))
                link(nc.vector.tensor_tensor(next_best[:], tmp[:], best[:], ALU.mult))
                link(nc.vector.tensor_tensor(share[:], share[:], best[:].unsqueeze(2).to_broadcast(shape), ALU.mult))
                link(nc.vector.tensor_tensor(second[:], second[:], next_best[:].unsqueeze(2).to_broadcast(shape), ALU.mult))
                link(nc.vector.tensor_tensor(share[:], share[:], second[:], ALU.add))
                with dve.Fori(0, NB // 2) as s:
                    dve.wait_ge(part_turned, s)
                    nc.vector.tensor_copy(part[:, 0, :, :], share[:, bass.ds(s * 2, 2), :]).then_inc(part_ready, 1)
                    dve.wait_ge(bias_ready, s + 1)
                    to = x[:, bass.ds(s * 2, 2), :].rearrange("p a d -> p (a d)")
                    nc.vector.tensor_tensor(to, to, po[:, 0, :], ALU.add).then_inc(bias_added, 1)


NX = FULL + 1
GB = 7
HALF = GB * P // 2
assert NX % GB == 0


def mixture_ffn(nc, st, xt, w1, b1, w2, share, x):
    H = w1.shape[2]
    HC = H // P
    with ExitStack() as ctx:
        def sb(name, shape, dt=F32):
            return ctx.enter_context(nc.sbuf_tensor(f"mx_{name}", shape, dt))

        w1_sb = sb("w1", [P, EX, DC, H])
        w2_sb = sb("w2", [P, EX, HC, D])
        b1_sb = sb("b1", [P, EX, HC])
        hidden = sb("hidden", [P, 2, HC, GB * P])
        ph = ctx.enter_context(nc.psum_tensor("mx_ph", [P, 4, 512], F32))
        py = ctx.enter_context(nc.psum_tensor("mx_py", [P, 4, 512], F32))
        loaded = st.sem("mx_loaded")
        h_product = st.sem("mx_h_product")
        h_ready = st.sem("mx_h_ready")
        y_product = st.sem("mx_y_product")
        y_added = st.sem("mx_y_added")
        HP, YP = EX * HC * 2, EX * GB
        with nc.Block() as block:
            @block.sync
            def _(sp):
                for e in range(EX):
                    sp.dma_start(w1_sb[:, e, :, :], w1[e].rearrange("(c p) h -> p c h", p=P)).then_inc(loaded, 16)
                    sp.dma_start(w2_sb[:, e, :, :], w2[e].rearrange("(c p) d -> p c d", p=P)).then_inc(loaded, 16)
                sp.dma_start(b1_sb[:], b1.rearrange("e (c p) -> p e c", p=P), allow_slow_non_contiguous=True).then_inc(loaded, 16)

            @block.tensor
            def _(pe):
                def hidden_parts(g, e):
                    for i in range(2 * HC):
                        hc, half, n = i // 2, i % 2, g * HP + e * 2 * HC + i
                        pe.wait_ge(h_ready, n + 1)
                        for c in range(DC):
                            last = nc.tensor.matmul(ph[:, i % 4, 0:HALF], w1_sb[:, e, c, hc * P:(hc + 1) * P],
                                                    xt[:, c, bass.ds(g * GB * P + half * HALF, HALF)],
                                                    start=(c == 0), stop=(c == DC - 1))
                        last.then_inc(h_product, 1)

                def output_parts(g, e):
                    pe.wait_ge(h_ready, g * HP + (e + 1) * 2 * HC + 4)
                    for j in range(GB):
                        m = g * YP + e * GB + j
                        pe.wait_ge(y_added, m + 1)
                        for hc in range(HC):
                            last = nc.tensor.matmul(py[:, (e * GB + j) % 4, 0:D], hidden[:, e % 2, hc, j * P:(j + 1) * P],
                                                    w2_sb[:, e, hc, :], start=(hc == 0), stop=(hc == HC - 1))
                        last.then_inc(y_product, 1)

                pe.sem_inc(y_product, GB)
                pe.wait_ge(loaded, 16 * (2 * EX + 1))
                with pe.Fori(0, NX // GB) as g:
                    hidden_parts(g, 0)
                    for e in range(EX):
                        if e + 1 < EX:
                            hidden_parts(g, e + 1)
                        output_parts(g, e)

            @block.scalar
            def _(act):
                act.sem_inc(h_ready, 4)
                act.wait_ge(loaded, 16 * (2 * EX + 1))
                with act.Fori(0, NX // GB) as g:
                    for e in range(EX):
                        act.wait_ge(y_product, g * YP + e * GB)
                        for i in range(2 * HC):
                            hc, half, n = i // 2, i % 2, g * HP + e * 2 * HC + i
                            act.wait_ge(h_product, n + 1)
                            nc.scalar.activation(hidden[:, e % 2, hc, half * HALF:(half + 1) * HALF], ph[:, i % 4, 0:HALF],
                                                 ACT.Gelu, bias=b1_sb[:, e, hc:hc + 1]).then_inc(h_ready, 1)

            @block.vector
            def _(dve):
                dve.sem_inc(y_added, 4)
                with dve.Fori(0, NX // GB) as g:
                    for e in range(EX):
                        for j in range(GB):
                            m = g * YP + e * GB + j
                            dve.wait_ge(y_product, m + GB + 1)
                            b = g * GB + j
                            to = x[:, bass.ds(b, 1), :].rearrange("p a d -> p (a d)")
                            nc.vector.scalar_tensor_tensor(
                                out=to, in0=py[:, (e * GB + j) % 4, 0:D],
                                scalar=share[:, bass.ds(b, 1), e:e + 1].rearrange("p a e -> p (a e)"),
                                in1=to, op0=ALU.mult, op1=ALU.add).then_inc(y_added, 1)


def gate_and_values(nc, st, xt, w1, b1, w2, b2, gcn_w, h_dram, ident, gate, h):
    R = w1.shape[1]
    assert R == P
    with ExitStack() as ctx:
        def sb(name, shape, dt=F32):
            return ctx.enter_context(nc.sbuf_tensor(f"ga_{name}", shape, dt))

        w1_sb, w2_sb, gw = sb("w1", [P, DC, R]), sb("w2", [R, D]), sb("gw", [P, DC])
        b1_sb, b2_sb = sb("b1", [P, 1]), sb("b2", [P, DC])
        total = sb("total", [P, DC])
        squeezed = sb("squeezed", [P, 1])
        gate_t = sb("gate_t", [P, DC])
        h_line = sb("h_line", [1, 2, 2 * P])
        h_rows = sb("h_rows", [NB, P])
        ph = ctx.enter_context(nc.psum_tensor("ga_ph", [1, 2, 512], F32))
        pg = ctx.enter_context(nc.psum_tensor("ga_pg", [P, 3, 512], F32))
        loaded = st.sem("ga_loaded")
        product = st.sem("ga_product")
        line_ready = st.sem("ga_line_ready")
        line_stored = [st.sem(f"ga_line_stored{k}") for k in range(2)]
        h_loaded = st.sem("ga_h_loaded")
        chain = st.sem("ga_chain")
        mean_ready = st.sem("ga_mean_ready")
        gate_psum = st.sem("ga_gate_psum")
        gate_step = st.sem("ga_gate_step")
        h_flat = h_dram.rearrange("n a -> (n a)")
        with nc.Block() as block:
            @block.sync
            def _(sp):
                sp.dma_start(w1_sb[:], w1.rearrange("(c p) r -> p c r", p=P)).then_inc(loaded, 16)
                sp.dma_start(w2_sb[:], w2).then_inc(loaded, 16)
                sp.dma_start(gw[:], gcn_w.rearrange("(c p) a -> p (c a)", p=P), allow_slow_non_contiguous=True).then_inc(loaded, 16)
                sp.dma_start(b1_sb[:], b1.rearrange("(p a) -> p a", a=1)).then_inc(loaded, 16)
                sp.dma_start(b2_sb[:], b2.rearrange("(c p) -> p c", p=P), allow_slow_non_contiguous=True).then_inc(loaded, 16)
                with sp.Fori(0, NB // 2) as s:
                    sp.wait_ge(line_ready, s + 1)
                    sp.dma_start(h_flat[bass.ds(s * 2 * P, 2 * P)].rearrange("(a n) -> a n", a=1), h_line[:, 0, :]).then_inc(line_stored[0], 16)
                sp.wait_ge(line_stored[0], 16 * (NB // 2))
                sp.dma_start(h_rows[:], h_flat.rearrange("(b n) -> b n", b=NB)).then_inc(h_loaded, 16)

            @block.tensor
            def _(pe):
                pe.wait_ge(loaded, 80)
                with pe.Fori(0, NB // 2) as s:
                    pe.wait_ge(line_ready, s)
                    for c in range(DC):
                        last = nc.tensor.matmul(ph[:, 0, 0:2 * P], gw[:, c:c + 1], xt[:, c, bass.ds(s * 2 * P, 2 * P)],
                                                start=(c == 0), stop=(c == DC - 1))
                    last.then_inc(product, 1)
                pe.wait_ge(mean_ready, 1)
                for c in range(DC):
                    last = nc.tensor.matmul(pg[:, 0, 0:1], w1_sb[:, c, :], total[:, c:c + 1], start=(c == 0), stop=(c == DC - 1))
                last.then_inc(gate_psum, 1)
                pe.wait_ge(gate_step, 1)
                for c in range(DC):
                    last = nc.tensor.matmul(pg[:, 1, c:c + 1], w2_sb[:, c * P:(c + 1) * P], squeezed[:], start=True, stop=True)
                last.then_inc(gate_psum, 1)
                pe.wait_ge(gate_step, 2)
                for c in range(DC):
                    last = nc.tensor.matmul(pg[:, 2, c * P:(c + 1) * P], gate_t[:, c:c + 1].to_broadcast([P, P]), ident[:], start=True, stop=True)
                last.then_inc(gate_psum, 1)
                pe.wait_ge(h_loaded, 16)
                pe.wait_ge(gate_step, 3)
                nc.tensor.transpose(pg[:, 0, 0:NB], h_rows[:], ident[0:NB, 0:NB]).then_inc(gate_psum, 1)

            @block.scalar
            def _(act):
                with act.Fori(0, NB // 2) as s:
                    act.wait_ge(line_stored[0], s * 16)
                    act.wait_ge(product, s + 1)
                    nc.scalar.copy(h_line[:, 0, :], ph[:, 0, 0:2 * P]).then_inc(line_ready, 1)
                act.wait_ge(loaded, 80)
                act.wait_ge(gate_psum, 1)
                nc.scalar.activation(squeezed[:], pg[:, 0, 0:1], ACT.Relu, bias=b1_sb[:, 0:1]).then_inc(gate_step, 1)
                act.wait_ge(gate_psum, 2)
                for c in range(DC):
                    last = nc.scalar.activation(gate_t[:, c:c + 1], pg[:, 1, c:c + 1], ACT.Sigmoid, bias=b2_sb[:, c:c + 1])
                last.then_inc(gate_step, 1)

            @block.vector
            def _(dve):
                link = chained(dve, chain)
                link(nc.vector.tensor_reduce(total[:], xt[:, :, 0:N], AX.X, ALU.add))
                nc.vector.tensor_scalar(total[:], total[:], 1.0 / N, None, ALU.mult).then_inc(mean_ready, 1)
                dve.wait_ge(gate_psum, 3)
                nc.vector.tensor_scalar(gate[:], pg[:, 2, 0:D], 1.0, None, ALU.add).then_inc(gate_step, 1)
                dve.wait_ge(gate_psum, 4)
                link(nc.vector.tensor_copy(h[:], pg[:, 0, 0:NB]))


def graph_values(nc, st, h, degree, dis, g, g_dram, ident):
    with ExitStack() as ctx:
        g_rows = ctx.enter_context(nc.sbuf_tensor("gv_rows", [NB, P], F32))
        root = ctx.enter_context(nc.sbuf_tensor("gv_root", [P, NB], F32))
        pt = ctx.enter_context(nc.psum_tensor("gv_pt", [P, 512], F32))
        chain = st.sem("gv_chain")
        more = st.sem("gv_more")
        rooted = st.sem("gv_rooted")
        g_ready = st.sem("gv_g_ready")
        turned = st.sem("gv_turned")
        rows_ready = st.sem("gv_rows_ready")
        stored = st.sem("gv_stored")
        with nc.Block() as block:
            @block.vector
            def _(dve):
                nc.vector.tensor_scalar(dis[:], degree[:], 1.0, None, ALU.add).then_inc(more, 1)
                dve.wait_ge(rooted, 1)
                link = chained(dve, chain)
                link(nc.vector.reciprocal(dis[:], root[:]))
                nc.vector.tensor_tensor(g[:], h[:], dis[:], ALU.mult).then_inc(g_ready, 1)
                dve.wait_ge(turned, 1)
                nc.vector.tensor_copy(g_rows[:], pt[0:NB, 0:P]).then_inc(rows_ready, 1)

            @block.scalar
            def _(act):
                act.wait_ge(more, 1)
                nc.scalar.activation(root[:], dis[:], ACT.Sqrt).then_inc(rooted, 1)

            @block.tensor
            def _(pe):
                pe.wait_ge(g_ready, 1)
                nc.tensor.transpose(pt[0:NB, 0:P], g[:], ident[:]).then_inc(turned, 1)

            @block.sync
            def _(sp):
                sp.wait_ge(rows_ready, 1)
                sp.dma_start(g_dram.rearrange("(b n) a -> b (n a)", b=NB), g_rows[:]).then_inc(stored, 16)
                sp.wait_ge(stored, 16)


def aggregate_values(nc, st, g_dram, rel, col, item_block, iota_free, acc):
    with ExitStack() as ctx:
        def sb(name, shape, dt=F32):
            return ctx.enter_context(nc.sbuf_tensor(f"av_{name}", shape, dt))

        got = sb("got", [P, RING, QUAD])
        index = sb("index", [P, RING, QUAD], I32)
        hot = sb("hot", [P, 2, QUAD, P])
        sums = ctx.enter_context(nc.psum_tensor("av_sums", [P, 2, 512], F32))
        gathered = [st.sem(f"av_gathered{k}") for k in range(RING * QUAD)]
        index_ready = st.sem("av_index_ready")
        hot_ready = st.sem("av_hot_ready")
        summed = st.sem("av_summed")
        added = st.sem("av_added")
        QUADS = NI // QUAD
        with nc.Block() as block:
            @block.gpsimd
            def _(pool):
                nc.gpsimd.memset(col[:, NI:NI + QUAD], 0).then_inc(index_ready, 1)
                nc.gpsimd.tensor_copy(index[:, 0, :], col[:, 0:QUAD]).then_inc(index_ready, 1)
                with pool.Fori(0, QUADS // RING) as s:
                    for u in range(RING):
                        q = s * RING + u
                        pool.wait_ge(summed, q + 1)
                        pool.wait_ge(index_ready, q + 2)
                        nc.gpsimd.tensor_copy(index[:, (u + 1) % RING, :],
                                              col[:, bass.ds((q + 1) * QUAD, QUAD)]).then_inc(index_ready, 1)
                        for j in range(QUAD):
                            nc.gpsimd.indirect_dma_start(
                                got[:, u, j:j + 1], None, g_dram,
                                bass.IndirectOffsetOnAxis(ap=index[:, u, j:j + 1], axis=0)).then_inc(gathered[u * QUAD + j], 16)

            @block.tensor
            def _(pe):
                pe.sem_inc(summed, 3)
                with pe.Fori(0, QUADS // RING) as s:
                    for v in range(RING):
                        q, u = s * RING + v, v % 2
                        pe.wait_ge(added, q * 4 + 4)
                        pe.wait_ge(hot_ready, q + 1)
                        for j in range(QUAD):
                            pe.wait_ge(gathered[v * QUAD + j], s * 16 + 16)
                        for j in range(QUAD):
                            last = nc.tensor.matmul(sums[:, u, j:j + 1], hot[:, u, j, :], got[:, v, j:j + 1], start=True, stop=True)
                        last.then_inc(summed, 1)

            @block.vector
            def _(dve):
                def one_hots(q, u):
                    for j in range(QUAD):
                        last = nc.vector.tensor_scalar(hot[:, u, j, :], iota_free[:], rel[:, bass.ds(q * QUAD + j, 1)], None, ALU.is_equal)
                    last.then_inc(hot_ready, 1)

                nc.vector.memset(rel[:, NI:NI + QUAD], float(P)).then_inc(added, 4)
                nc.vector.memset(acc[:], 0.0).then_inc(added, 4)
                dve.wait_ge(added, 8)
                one_hots(0, 0)
                with dve.Fori(0, QUADS // 2) as s:
                    for u in range(2):
                        q = s * 2 + u
                        dve.wait_ge(summed, q + 3)
                        one_hots(q + 1, 1 - u)
                        blk = load_blocks(nc, item_block, q, mybir.EngineType.DVE)
                        dve.wait_ge(summed, q + 4)
                        for j in range(QUAD):
                            dve.wait_ge(added, q * 4 + j + 8)
                            to = acc[:, bass.ds(blk[j], 1)]
                            nc.vector.tensor_tensor(to, to, sums[:, u, j:j + 1], ALU.add).then_inc(added, 1)


def gated_update(nc, st, x, mean, rstd, dis, g, sums, gcn_b, gate):
    with ExitStack() as ctx:
        def sb(name, shape, dt=F32):
            return ctx.enter_context(nc.sbuf_tensor(f"gu_{name}", shape, dt))

        bias = sb("bias", [P, 1])
        pre = sb("pre", [P, NB])
        spatial = sb("spatial", [P, NB])
        rows = sb("rows", [P, 2, D])
        factor = sb("factor", [P, 2, D])
        loaded = st.sem("gu_loaded")
        chain = st.sem("gu_chain")
        pre_ready = st.sem("gu_pre_ready")
        spatial_ready = st.sem("gu_spatial_ready")
        factor_ready = st.sem("gu_factor_ready")
        step = st.sem("gu_step")
        with nc.Block() as block:
            @block.sync
            def _(sp):
                sp.dma_start(bias[:], gcn_b.rearrange("(a n) -> a n", a=1).to_broadcast([P, 1])).then_inc(loaded, 16)

            @block.scalar
            def _(act):
                act.wait_ge(loaded, 16)
                act.wait_ge(pre_ready, 1)
                nc.scalar.activation(spatial[:], pre[:], ACT.Sigmoid, bias=bias[:, 0:1]).then_inc(spatial_ready, 1)
                act.wait_ge(spatial_ready, 1)
                with act.Fori(0, NB // 2) as h:
                    for k in range(2):
                        b = h * 2 + k
                        act.wait_ge(step, h * 6)
                        nc.scalar.activation(factor[:, k, :], gate[:], ACT.Identity, bias=spatial[:, bass.ds(b, 1)]).then_inc(factor_ready, 1)

            @block.vector
            def _(dve):
                link = chained(dve, chain)
                link(nc.vector.tensor_tensor(pre[:], sums[:], g[:], ALU.add))
                nc.vector.tensor_tensor(pre[:], pre[:], dis[:], ALU.mult).then_inc(pre_ready, 1)
                with dve.Fori(0, NB // 2) as h:
                    for k in range(2):
                        b = h * 2 + k
                        of = x[:, bass.ds(b, 1), :].rearrange("p a d -> p (a d)")
                        nc.vector.tensor_scalar(rows[:, k, :], of, mean[:, bass.ds(b, 1)], rstd[:, bass.ds(b, 1)],
                                                ALU.subtract, ALU.mult).then_inc(step, 1)
                        dve.wait_ge(factor_ready, b + 1)
                        dve.wait_ge(step, b * 3 + 1)
                        nc.vector.tensor_tensor(rows[:, k, :], rows[:, k, :], factor[:, k, :], ALU.mult).then_inc(step, 1)
                        dve.wait_ge(step, b * 3 + 2)
                        nc.vector.tensor_tensor(of, of, rows[:, k, :], ALU.add).then_inc(step, 1)


def routed_ffn(nc, st, xt, w1, b1, wg, bg, wd, bd, x, order, ident, ones):
    H = w1.shape[1]
    HC = H // P
    PAIRS = EX // 2
    with ExitStack() as ctx:
        def sb(name, shape, dt=F32):
            return ctx.enter_context(nc.sbuf_tensor(f"rf_{name}", shape, dt))

        w1_sb = sb("w1", [P, DC, H])
        b1_sb = sb("b1", [P, HC])
        wg_sb = sb("wg", [P, HC, EX])
        bg_sb = sb("bg", [1, EX])
        wd_sb = sb("wd", [P, HC, EX, D])
        bd_sb = sb("bd", [EX, D])
        hidden = sb("hidden", [P, 2, HC, 2 * P])
        logits = sb("logits", [P, EX])
        shifted = sb("shifted", [P, EX])
        exps = sb("exps", [P, EX])
        small = sb("small", [P, 4])
        mask = sb("mask", [P, EX])
        share = sb("share", [P, 2, EX])
        share_t = sb("share_t", [EX, 2, P])
        ph = ctx.enter_context(nc.psum_tensor("rf_ph", [P, 2, 512], F32))
        ps = ctx.enter_context(nc.psum_tensor("rf_ps", [P, 512], F32))
        pb = ctx.enter_context(nc.psum_tensor("rf_pb", [P, 512], F32))
        py = ctx.enter_context(nc.psum_tensor("rf_py", [P, PAIRS, 512], F32))
        loaded = st.sem("rf_loaded")
        h_product = st.sem("rf_h_product")
        h_ready = st.sem("rf_h_ready")
        logit_product = st.sem("rf_logit_product")
        chain = st.sem("rf_chain")
        shift_ready = st.sem("rf_shift_ready")
        exps_ready = st.sem("rf_exps_ready")
        share_ready = st.sem("rf_share_ready")
        share_turned = st.sem("rf_share_turned")
        share_t_ready = st.sem("rf_share_t_ready")
        bias_ready = st.sem("rf_bias_ready")
        bias_added = st.sem("rf_bias_added")
        y_product = st.sem("rf_y_product")
        y_added = st.sem("rf_y_added")
        CHAIN = 9
        with nc.Block() as block:
            @block.sync
            def _(sp):
                sp.dma_start(w1_sb[:], w1.rearrange("(c p) h -> p c h", p=P)).then_inc(loaded, 16)
                sp.dma_start(b1_sb[:], b1.rearrange("(c p) -> p c", p=P), allow_slow_non_contiguous=True).then_inc(loaded, 16)
                sp.dma_start(wg_sb[:], wg.rearrange("(c p) e -> p c e", p=P)).then_inc(loaded, 16)
                sp.dma_start(bg_sb[:], bg.rearrange("(a e) -> a e", a=1)).then_inc(loaded, 16)
                sp.dma_start(bd_sb[:], bd).then_inc(loaded, 16)
                for e in range(EX):
                    sp.dma_start(wd_sb[:, :, e, :], wd[e].rearrange("(c p) d -> p c d", p=P)).then_inc(loaded, 16)

            @block.tensor
            def _(pe):
                pe.wait_ge(loaded, 16 * (5 + EX))
                with pe.Fori(0, NB // 2) as s:
                    for hc in range(HC):
                        pe.wait_ge(h_ready, s * HC + hc + 1)
                        for c in range(DC):
                            last = nc.tensor.matmul(ph[:, hc % 2, 0:2 * P], w1_sb[:, c, hc * P:(hc + 1) * P],
                                                    xt[:, c, bass.ds(s * 2 * P, 2 * P)], start=(c == 0), stop=(c == DC - 1))
                        last.then_inc(h_product, 1)
                    pe.wait_ge(h_ready, s * HC + HC + 2)
                    for k in range(2):
                        b = s * 2 + k
                        pe.wait_ge(shift_ready, b)
                        for hc in range(HC):
                            nc.tensor.matmul(ps[:, 0:EX], hidden[:, 0, hc, k * P:(k + 1) * P], wg_sb[:, hc, :], start=(hc == 0), stop=False)
                        nc.tensor.matmul(ps[:, 0:EX], ones[0:1, :], bg_sb[:], start=False, stop=True).then_inc(logit_product, 1)
                        for pair in range(PAIRS):
                            pe.wait_ge(y_added, b * EX + 2 * pair + 2)
                            for hc in range(HC):
                                last = nc.tensor.matmul(py[:, pair, :], hidden[:, 0, hc, k * P:(k + 1) * P],
                                                        wd_sb[:, hc, 2 * pair:2 * pair + 2, :].rearrange("p e d -> p (e d)"),
                                                        start=(hc == 0), stop=(hc == HC - 1))
                            last.then_inc(y_product, 1)
                        pe.wait_ge(bias_added, b)
                        pe.wait_ge(share_ready, b + 1)
                        nc.tensor.transpose(pb[0:EX, D:D + P], share[:, 0, :], ident[:]).then_inc(share_turned, 1)
                        pe.wait_ge(share_t_ready, b + 1)
                        nc.tensor.matmul(pb[:, 0:D], share_t[:, 0, :], bd_sb[:], start=True, stop=True).then_inc(bias_ready, 1)

            @block.scalar
            def _(act):
                act.sem_inc(h_ready, 2)
                act.wait_ge(loaded, 16 * (5 + EX))
                with act.Fori(0, NB // 2) as s:
                    act.wait_ge(bias_ready, s * 2)
                    for hc in range(HC):
                        act.wait_ge(h_product, s * HC + hc + 1)
                        nc.scalar.activation(hidden[:, 0, hc, :], ph[:, hc % 2, 0:2 * P], ACT.Gelu, bias=b1_sb[:, hc:hc + 1]).then_inc(h_ready, 1)
                    for k in range(2):
                        b = s * 2 + k
                        act.wait_ge(shift_ready, b + 1)
                        nc.scalar.activation(exps[:], shifted[:], ACT.Exp).then_inc(exps_ready, 1)
                        act.wait_ge(share_turned, b + 1)
                        nc.scalar.copy(share_t[:, 0, :], pb[0:EX, D:D + P]).then_inc(share_t_ready, 1)

            @block.vector
            def _(dve):
                dve.sem_inc(y_added, EX)
                with dve.Fori(0, NB // 2) as s:
                    for k in range(2):
                        b = s * 2 + k
                        at = [0]

                        def link(instruction, b=b, at=at):
                            at[0] += 1
                            instruction.then_inc(chain, 1)
                            dve.wait_ge(chain, b * CHAIN + at[0])

                        dve.wait_ge(logit_product, b + 1)
                        link(nc.vector.tensor_reduce(small[:, 0:1], ps[:, 0:EX], AX.X, ALU.max))
                        link(nc.vector.tensor_scalar(mask[:], ps[:, 0:EX], small[:, 0:1], None, ALU.is_equal))
                        nc.vector.tensor_scalar(shifted[:], ps[:, 0:EX], small[:, 0:1], None, ALU.subtract).then_inc(shift_ready, 1)
                        link(nc.vector.tensor_tensor(mask[:], mask[:], order[:], ALU.mult))
                        link(nc.vector.tensor_reduce(small[:, 1:2], mask[:], AX.X, ALU.max))
                        link(nc.vector.tensor_scalar(mask[:], order[:], small[:, 1:2], None, ALU.is_equal))
                        dve.wait_ge(exps_ready, b + 1)
                        link(nc.vector.tensor_reduce(small[:, 2:3], exps[:], AX.X, ALU.add))
                        link(nc.vector.reciprocal(small[:, 3:4], small[:, 2:3]))
                        link(nc.vector.tensor_scalar(share[:, 1, :], mask[:], small[:, 3:4], None, ALU.mult))
                        dve.wait_ge(share_turned, b)
                        link(nc.vector.tensor_copy(share[:, 0, :], share[:, 1, :]))
                        assert at[0] == CHAIN
                        dve.sem_inc(share_ready, 1)
                        to = x[:, bass.ds(b, 1), :].rearrange("p a d -> p (a d)")
                        for e in range(EX):
                            dve.wait_ge(y_product, b * PAIRS + e // 2 + 1)
                            dve.wait_ge(y_added, b * EX + e + EX)
                            nc.vector.scalar_tensor_tensor(out=to, in0=py[:, e // 2, (e % 2) * D:(e % 2 + 1) * D],
                                                           scalar=share[:, 0, e:e + 1], in1=to, op0=ALU.mult,
                                                           op1=ALU.add).then_inc(y_added, 1)
                        dve.wait_ge(bias_ready, b + 1)
                        dve.wait_ge(y_added, b * EX + 2 * EX)
                        nc.vector.tensor_tensor(to, to, pb[:, 0:D], ALU.add).then_inc(bias_added, 1)


def move(nc, st, name, pairs):
    moved = st.sem(f"{name}_moved")
    with nc.Block() as block:
        @block.sync
        def _(sp):
            for to, of in pairs:
                sp.dma_start(to, of).then_inc(moved, 16)
            sp.wait_ge(moved, 16 * len(pairs))


def load_columns(nc, st, name, pairs):
    moved = st.sem(f"{name}_moved")
    with nc.Block() as block:
        @block.sync
        def _(sp):
            for to, of in pairs:
                sp.dma_start(to, of.rearrange("(c p) -> p c", p=P), allow_slow_non_contiguous=True).then_inc(moved, 16)
            sp.wait_ge(moved, 16 * len(pairs))


def build(nc, a, out):
    st = Stage(nc)
    keep = st.keep

    def dram(name, shape, dt=F32):
        return nc.dram_tensor(name, shape, dt, kind="Internal").ap()

    k_dram, v_dram = dram("k_table", (NB * P, D)), dram("v_table", (NB * P, D))
    scratch = {"rows": dram("edge_rows", (ET, P), I32), "cols": dram("edge_cols", (ET, P), I32),
               "item_block": dram("item_block", (NI,), I32), "keys": dram("item_keys", (NI, P), I16)}
    rel_dram, col_dram = dram("item_rel", (P, NI)), dram("item_col", (P, NI), I32)
    bounce = [dram(f"bounce{n}", (P, 1)) for n in range(2)]
    h_dram, g_dram = dram("h_values", (NB * P, 1)), dram("g_values", (NB * P, 1))

    def sb(ctx, name, shape, dt=F32):
        return ctx.enter_context(nc.sbuf_tensor(name, shape, dt))

    ident, identb = sb(keep, "ident", [P, P]), sb(keep, "identb", [P, P], BF16)
    iota_free, iota_part = sb(keep, "iota_free", [P, P]), sb(keep, "iota_part", [P, 1])
    ones, order = sb(keep, "ones", [P, P]), sb(keep, "order", [P, EX])
    stats, tmp = sb(keep, "stats", [P, NB, 6]), sb(keep, "ln_tmp", [P, NB])
    mean, rstd = sb(keep, "mean", [P, NB]), sb(keep, "rstd", [P, NB])
    mean2, rstd2 = sb(keep, "mean2", [P, NB]), sb(keep, "rstd2", [P, NB])
    degree = sb(keep, "degree", [P, NB])
    constants(nc, st, ident, identb, iota_free, iota_part, ones, order)

    with ExitStack() as ctx:
        rel, col = sb(ctx, "rel", [P, NI + QUAD]), sb(ctx, "col", [P, NI + QUAD], I32)
        item_block = sb(ctx, "item_block_sb", [1, NI], I32)
        item_tables(nc, st, a["dst"], a["src"], scratch, ident, ones, rel, col)
        move(nc, st, "items", [(item_block[:], scratch["item_block"].rearrange("(a i) -> a i", a=1)),
                               (rel_dram, rel[:, 0:NI]), (col_dram, col[:, 0:NI])])
        scores = sb(ctx, "scores", [P, NI, HEADS])
        with ExitStack() as queries:
            q_all = sb(queries, "q_all", [P, NB, D])
            with ExitStack() as nodes:
                x = sb(nodes, "x_first", [P, NB, D])
                load_x(nc, st, "x_first", a["x"], x)
                layernorm_stats(nc, st, "ln_attention", x, stats, mean, rstd, tmp)
                project_qkv(nc, st, x, mean, rstd, ident, ones, [a[f"L0_gnn_W{n}"] for n in "qkv"],
                            [a[f"L0_gnn_b{n}"] for n in "qkv"], q_all, (k_dram, v_dram))
            edge_scores(nc, st, q_all, k_dram, rel, col, item_block, iota_free, ident, scores)
        softmax_over_rows(nc, st, scores, scratch["keys"], bounce, ident)
        acc = sb(ctx, "acc", [P, NB, AW])
        aggregate(nc, st, scores, v_dram, rel, col, item_block, iota_free, acc)
        copied = st.sem("degree_copied")
        with nc.Block() as block:
            @block.vector
            def _(dve):
                nc.vector.tensor_copy(degree[:], acc[:, :, AW - 1]).then_inc(copied, 1)
        x = sb(ctx, "x_second", [P, NB, D])
        load_x(nc, st, "x_second", a["x"], x)
        attention_output(nc, st, acc, x, a["L0_gnn_Wo"], a["L0_gnn_bo"], ident, ones)
        x_dram = dram("x_between", (P, NB, D))
        move(nc, st, "x_out", [(x_dram, x[:])])
    st.hand_back()

    with ExitStack() as ctx:
        x = sb(ctx, "x", [P, NB, D])
        move(nc, st, "x_in", [(x[:], x_dram)])

        with ExitStack() as ffn:
            xt = sb(ffn, "xt_first", [P, DC, NB * P])
            share = sb(ffn, "share", [P, NB, EX])
            line = sb(ffn, "ln_line", [P, D])
            gamma, beta = sb(ffn, "gamma", [P, DC]), sb(ffn, "beta", [P, DC])
            load_columns(nc, st, "affine", [(gamma[:], a["L0_ffn_gamma"]), (beta[:], a["L0_ffn_beta"])])
            layernorm_stats(nc, st, "ln_outer", x, stats, mean, rstd, tmp)
            layernorm_stats(nc, st, "ln_inner", x, stats, mean2, rstd2, tmp, inner=(mean, rstd, line))
            turn(nc, st, "turn_first", x, ((mean, rstd), (mean2, rstd2)), xt, ident, gamma, beta)
            route_two(nc, st, xt, a["L0_ffn_Wr"], a["L0_ffn_br"], x, a["L0_ffn_b2"], order, ident, share)
            mixture_ffn(nc, st, xt, a["L0_ffn_W1"], a["L0_ffn_b1"], a["L0_ffn_W2"], share, x)

        st.hand_back()

        with ExitStack() as gnn:
            gate = sb(gnn, "gate", [P, D])
            h, dis, g = sb(gnn, "h", [P, NB]), sb(gnn, "dis", [P, NB]), sb(gnn, "g", [P, NB])
            sums = sb(gnn, "neighbour_sums", [P, NB])
            layernorm_stats(nc, st, "ln_gates", x, stats, mean, rstd, tmp)
            with ExitStack() as turned:
                xt = sb(turned, "xt_second", [P, DC, NB * P])
                turn(nc, st, "turn_second", x, ((mean, rstd),), xt, ident)
                gate_and_values(nc, st, xt, a["L1_gnn_w1"], a["L1_gnn_b1"], a["L1_gnn_w2"], a["L1_gnn_b2"],
                                a["L1_gnn_gcn_w"], h_dram, ident, gate, h)
            graph_values(nc, st, h, degree, dis, g, g_dram, ident)
            with ExitStack() as edges:
                rel, col = sb(edges, "rel_again", [P, NI + QUAD]), sb(edges, "col_again", [P, NI + QUAD], I32)
                item_block = sb(edges, "item_block_again", [1, NI], I32)
                move(nc, st, "items_again", [(item_block[:], scratch["item_block"].rearrange("(a i) -> a i", a=1)),
                                             (rel[:, 0:NI], rel_dram), (col[:, 0:NI], col_dram)])
                aggregate_values(nc, st, g_dram, rel, col, item_block, iota_free, sums)
            gated_update(nc, st, x, mean, rstd, dis, g, sums, a["L1_gnn_gcn_b"], gate)

        st.hand_back()

        with ExitStack() as ffn:
            xt = sb(ffn, "xt_third", [P, DC, NB * P])
            layernorm_stats(nc, st, "ln_routed", x, stats, mean, rstd, tmp)
            turn(nc, st, "turn_third", x, ((mean, rstd),), xt, ident)
            routed_ffn(nc, st, xt, a["L1_ffn_W1"], a["L1_ffn_b1"], a["L1_ffn_Wg"], a["L1_ffn_bg"], a["L1_ffn_Wd"],
                       a["L1_ffn_bd"], x, order, ident, ones)
        move(nc, st, "result", [(out[0:FULL * P, :].rearrange("(b p) d -> p b d", p=P), x[:, 0:FULL, :]),
                                (out[FULL * P:N, :], x[0:TAIL, FULL, :])])
    keep.close()


def kernel(**inputs):
    import numpy as _np
    import concourse.bacc as _bacc
    from concourse.bass_utils import run_bass_kernel_spmd as _run

    nc = _bacc.Bacc("TRN2", target_bir_lowering=False, num_devices=1)
    arrays, aps = {}, {}
    for name, value in inputs.items():
        value = _np.ascontiguousarray(value)
        arrays[f"in_{name}"] = value
        aps[name] = nc.dram_tensor(f"in_{name}", value.shape, mybir.dt.from_np(value.dtype), kind="ExternalInput").ap()
    out = nc.dram_tensor("out", (N, D), F32, kind="ExternalOutput").ap()
    build(nc, aps, out)
    result = _run(nc, [arrays], core_ids=[0])
    return result.results[0]["out"]
```

```python
from contextlib import ExitStack

import concourse.bass as bass
from concourse import mybir

F32 = mybir.dt.float32
BF16 = mybir.dt.bfloat16
I32 = mybir.dt.int32
I16 = mybir.dt.int16
ALU = mybir.AluOpType
ACT = mybir.ActivationFunctionType
AX = mybir.AxisListType

P = 128
N = 6250
D = 256
DC = D // P
HEADS, HD = 8, 32
E = 206250
NB = 50
FULL = N // P
TAIL = N - FULL * P
ET = -(-E // P)
ETAIL = E - (ET - 1) * P
CH = 16
CI = 104
NI = CH * CI
IG = NI // P
assert NI >= ET + FULL + 1
PAD_ROW = 8192
BIG = 1.0e38
CL = CI * P
EPS = 1e-5
EX = 8
QUAD = 4
RING = 4
AW = D + HEADS + 1


class Stage:

    def __init__(self, nc):
        self.nc = nc
        self.keep = ExitStack()
        self.taken = []

    def sem(self, name):
        self.taken.append(self.nc.alloc_semaphore(name=name))
        return self.taken[-1]

    def hand_back(self):
        self.nc.all_engine_barrier()
        self.nc.clear_and_free_semaphores(self.taken)
        self.nc.all_engine_barrier()
        self.taken = []


def chained(engine, sem, start=0):
    count = [start]

    def link(instruction):
        count[0] += 1
        instruction.then_inc(sem, 1)
        engine.wait_ge(sem, count[0])

    return link


def constants(nc, st, ident, before, iota_free, iota_part, ones, order):
    made = st.sem("const_made")
    with nc.Block() as block:
        @block.gpsimd
        def _(pool):
            link = chained(pool, made)
            link(nc.gpsimd.memset(ones[:], 1.0))
            link(nc.gpsimd.iota(iota_free[:], pattern=[[1, P]], base=0, channel_multiplier=0,
                                allow_small_or_imprecise_dtypes=True))
            link(nc.gpsimd.iota(iota_part[:], pattern=[[0, 1]], base=0, channel_multiplier=1,
                                allow_small_or_imprecise_dtypes=True))
            link(nc.gpsimd.tensor_scalar(ident[:], iota_free[:], iota_part[:, 0:1], None, ALU.is_equal))
            link(nc.gpsimd.tensor_scalar(before[:], iota_free[:], iota_part[:, 0:1], None, ALU.is_gt))
            link(nc.gpsimd.iota(order[:], pattern=[[-1, EX]], base=EX, channel_multiplier=0,
                                allow_small_or_imprecise_dtypes=True))


def layernorm_stats(nc, st, name, x, stats, mean, rstd, tmp, inner=None):
    inner_done = st.sem(f"{name}_inner_done")
    stat_done = st.sem(f"{name}_stat_done")
    chain = st.sem(f"{name}_chain")
    var_ready = st.sem(f"{name}_var_ready")
    root_ready = st.sem(f"{name}_root_ready")
    with nc.Block() as block:
        @block.vector
        def _(dve):
            with dve.Fori(0, NB) as b:
                of = x[:, bass.ds(b, 1), :].rearrange("p a d -> p (a d)")
                if inner:
                    nc.vector.tensor_scalar(inner[2][:], of, inner[0][:, bass.ds(b, 1)], inner[1][:, bass.ds(b, 1)],
                                            ALU.subtract, ALU.mult).then_inc(inner_done, 1)
                    dve.wait_ge(inner_done, b + 1)
                    of = inner[2][:]
                nc.vector.bn_stats(stats[:, bass.ds(b, 1), :].rearrange("p a s -> p (a s)"), of).then_inc(stat_done, 1)
                if inner:
                    dve.wait_ge(stat_done, b + 1)
            dve.wait_ge(stat_done, NB)
            link = chained(dve, chain)
            link(nc.vector.tensor_tensor(mean[:], stats[:, :, 1], stats[:, :, 4], ALU.add))
            link(nc.vector.tensor_scalar(mean[:], mean[:], 0.5, None, ALU.mult))
            link(nc.vector.tensor_tensor(tmp[:], stats[:, :, 1], stats[:, :, 4], ALU.subtract))
            link(nc.vector.tensor_tensor(tmp[:], tmp[:], tmp[:], ALU.mult))
            link(nc.vector.tensor_tensor(rstd[:], stats[:, :, 2], stats[:, :, 5], ALU.add))
            link(nc.vector.tensor_scalar(rstd[:], rstd[:], 1.0 / D, EPS, ALU.mult, ALU.add))
            link(nc.vector.scalar_tensor_tensor(out=rstd[:], in0=tmp[:], scalar=0.25, in1=rstd[:],
                                                op0=ALU.mult, op1=ALU.add))
            nc.vector.memset(tmp[:, 0:1], 0.0).then_inc(var_ready, 1)
            dve.wait_ge(root_ready, 1)
            link(nc.vector.reciprocal(rstd[:], tmp[:]))

        @block.scalar
        def _(act):
            act.wait_ge(var_ready, 1)
            nc.scalar.activation(tmp[:], rstd[:], ACT.Sqrt).then_inc(root_ready, 1)


def load_x(nc, st, name, x_dram, x):
    zeroed = st.sem(f"{name}_zeroed")
    loaded = st.sem(f"{name}_loaded")
    with nc.Block() as block:
        @block.vector
        def _(dve):
            nc.vector.memset(x[:, FULL:NB, :], 0.0).then_inc(zeroed, 1)

        @block.sync
        def _(sp):
            sp.dma_start(x[:, 0:FULL, :], x_dram[0:FULL * P, :].rearrange("(b p) d -> p b d", p=P)).then_inc(loaded, 16)
            sp.wait_ge(zeroed, 1)
            sp.dma_start(x[0:TAIL, FULL, :], x_dram[FULL * P:N, :]).then_inc(loaded, 16)
            sp.wait_ge(loaded, 32)


def project_qkv(nc, st, x, mean, rstd, ident, ones, weights, biases, q_all, kv_dram):
    with ExitStack() as ctx:
        w = ctx.enter_context(nc.sbuf_tensor("wqkv", [P, DC, 3 * D], F32))
        bias = ctx.enter_context(nc.sbuf_tensor("bqkv", [1, 3 * D], F32))
        xn = ctx.enter_context(nc.sbuf_tensor("qkv_xn", [P, 2, D], F32))
        xt = ctx.enter_context(nc.sbuf_tensor("qkv_xt", [P, 2, D], F32))
        kv = ctx.enter_context(nc.sbuf_tensor("qkv_kv", [P, 2, 2 * D], F32))
        pt = ctx.enter_context(nc.psum_tensor("qkv_pt", [P, 2, 512], F32))
        pq = ctx.enter_context(nc.psum_tensor("qkv_pq", [P, 2, 512], F32))
        pkv = ctx.enter_context(nc.psum_tensor("qkv_pkv", [P, 2, 512], F32))
        w_loaded = st.sem("qkv_w_loaded")
        xn_ready = st.sem("qkv_xn_ready")
        xt_psum = st.sem("qkv_xt_psum")
        xt_ready = st.sem("qkv_xt_ready")
        products = st.sem("qkv_products")
        q_out = st.sem("qkv_q_out")
        kv_out = st.sem("qkv_kv_out")
        stored = [st.sem(f"qkv_stored{k}") for k in range(2)]
        with nc.Block() as block:
            @block.sync
            def _(sp):
                for j, (wm, bm) in enumerate(zip(weights, biases)):
                    sp.dma_start(w[:, :, j * D:(j + 1) * D], wm.rearrange("(c p) n -> p c n", p=P)).then_inc(w_loaded, 16)
                    sp.dma_start(bias[0:1, j * D:(j + 1) * D], bm.rearrange("(a n) -> a n", a=1)).then_inc(w_loaded, 16)
                with sp.Fori(0, NB // 2) as h:
                    b = h * 2
                    for k in range(2):
                        sp.wait_ge(kv_out, b + k + 1)
                        for j in range(2):
                            sp.dma_start(kv_dram[j][bass.ds((b + k) * P, P), :],
                                         kv[:, k, j * D:(j + 1) * D]).then_inc(stored[k], 16)
                for k in range(2):
                    sp.wait_ge(stored[k], 32 * (NB // 2))

            @block.vector
            def _(dve):
                with dve.Fori(0, NB // 2) as h:
                    b = h * 2
                    for k in range(2):
                        dve.wait_ge(xt_psum, b)
                        nc.vector.tensor_scalar(xn[:, k, :], x[:, bass.ds(b + k, 1), :].rearrange("p a d -> p (a d)"),
                                                mean[:, bass.ds(b + k, 1)], rstd[:, bass.ds(b + k, 1)],
                                                ALU.subtract, ALU.mult).then_inc(xn_ready, 1)
                    for k in range(2):
                        dve.wait_ge(products, b + k + 1)
                        dve.wait_ge(stored[k], b * 16)
                        nc.vector.tensor_copy(kv[:, k, :], pkv[:, k, :]).then_inc(kv_out, 1)

            @block.tensor
            def _(pe):
                pe.wait_ge(w_loaded, 96)
                with pe.Fori(0, NB // 2) as h:
                    b = h * 2
                    for k in range(2):
                        pe.wait_ge(xn_ready, b + k + 1)
                        pe.wait_ge(xt_ready, b)
                        for c in range(DC):
                            last = nc.tensor.transpose(pt[:, k, c * P:(c + 1) * P], xn[:, k, c * P:(c + 1) * P], ident[:])
                        last.then_inc(xt_psum, 1)
                    for k in range(2):
                        pe.wait_ge(xt_ready, b + k + 1)
                        pe.wait_ge(q_out, b)
                        pe.wait_ge(kv_out, b)
                        for out, lo, hi in ((pq[:, k, 0:D], 0, D), (pkv[:, k, :], D, 3 * D)):
                            for c in range(DC):
                                nc.tensor.matmul(out, xt[:, k, c * P:(c + 1) * P], w[:, c, lo:hi], start=(c == 0), stop=False)
                            last = nc.tensor.matmul(out, ones[0:1, :], bias[0:1, lo:hi], start=False, stop=True)
                        last.then_inc(products, 1)

            @block.scalar
            def _(act):
                with act.Fori(0, NB // 2) as h:
                    b = h * 2
                    for k in range(2):
                        act.wait_ge(xt_psum, b + k + 1)
                        act.wait_ge(products, b)
                        nc.scalar.copy(xt[:, k, :], pt[:, k, 0:D]).then_inc(xt_ready, 1)
                    for k in range(2):
                        act.wait_ge(products, b + k + 1)
                        nc.scalar.activation(q_all[:, bass.ds(b + k, 1), :].rearrange("p a d -> p (a d)"), pq[:, k, 0:D], ACT.Copy, scale=float(HD) ** -0.5).then_inc(q_out, 1)


def item_tables(nc, st, row_in, col_in, scratch, ident, ones, rel, col):
    RP = 125
    RE = E // RP
    assert RP * RE == E
    with ExitStack() as ctx:
        def sb(name, shape, dt=F32):
            return ctx.enter_context(nc.sbuf_tensor(f"it_{name}", shape, dt))

        raw = sb("raw", [RP, RE], I32)
        rows = sb("rows", [RP, RE])
        below = sb("below", [RP, RE])
        bound = sb("bound", [P, NB])
        count = sb("count", [P, NB])
        padding = sb("padding", [1, 2 * P], I32)
        ptr = sb("ptr", [P, NB], I32)
        up = sb("up", [P, NB], I32)
        first = sb("first", [P, NB])
        behind = sb("behind", [P, NB])
        many = sb("many", [P, FULL + 1])
        ends = sb("ends", [P, FULL + 1])
        shift = sb("shift", [P, FULL + 1])
        item = sb("item", [P, IG])
        block_of = sb("block_of", [P, IG])
        block_int = sb("block_int", [P, IG], I32)
        tile_of = sb("tile_of", [P, IG])
        tile_int = sb("tile_int", [P, IG], I32)
        table = sb("table", [P, IG, FULL + 1])
        got_row = sb("got_row", [P, IG, P], I32)
        got_col = sb("got_col", [P, IG, P], I32)
        rowf = sb("rowf", [P, IG, P])
        key = sb("key", [P, IG, P], I16)
        colf = sb("colf", [P, IG, P])
        total = ctx.enter_context(nc.psum_tensor("it_total", [P, 512], F32))
        turned = ctx.enter_context(nc.psum_tensor("it_turned", [P, 2, 512], F32))
        loaded = st.sem("it_loaded")
        pad_made = st.sem("it_pad_made")
        padded = st.sem("it_padded")
        made = st.sem("it_made")
        counted = st.sem("it_counted")
        chain = st.sem("it_chain")
        counts_done = st.sem("it_counts_done")
        summed = st.sem("it_summed")
        tiles_ready = st.sem("it_tiles_ready")
        gathered = st.sem("it_gathered")
        tables_ready = st.sem("it_tables_ready")
        turned_ready = st.sem("it_turned_ready")
        turned_out = st.sem("it_turned_out")
        stored = st.sem("it_stored")
        NBLK = FULL + 1
        with nc.Block() as block:
            @block.sync
            def _(sp):
                sp.dma_start(raw[:], row_in.rearrange("(p e) -> p e", p=RP)).then_inc(loaded, 16)
                for n, (src, dst) in enumerate(((row_in, scratch["rows"]), (col_in, scratch["cols"]))):
                    flat = dst.rearrange("t e -> (t e)")
                    sp.dma_start(flat[0:E].rearrange("(a e) -> a e", a=50), src.rearrange("(a e) -> a e", a=50)).then_inc(padded, 16)
                    if n == 0:
                        sp.wait_ge(pad_made, 2)
                    sp.dma_start(dst[ET - 1:ET, ETAIL:P], padding[0:1, n * P + ETAIL:(n + 1) * P]).then_inc(padded, 16)
                sp.wait_ge(tables_ready, 1)
                sp.dma_start(scratch["item_block"].rearrange("(g p) -> p g", p=P), block_int[:], allow_slow_non_contiguous=True).then_inc(stored, 16)
                sp.dma_start(scratch["keys"].rearrange("(g p) e -> p g e", p=P), key[:]).then_inc(stored, 16)
                sp.wait_ge(stored, 32)

            @block.gpsimd
            def _(pool):
                nc.gpsimd.memset(padding[0:1, 0:P], PAD_ROW - 1).then_inc(pad_made, 1)
                nc.gpsimd.memset(padding[0:1, P:2 * P], 0).then_inc(pad_made, 1)
                nc.gpsimd.iota(bound[:], pattern=[[P, NB]], base=0, channel_multiplier=0,
                               allow_small_or_imprecise_dtypes=True).then_inc(made, 1)
                nc.gpsimd.iota(item[:], pattern=[[P, IG]], base=0, channel_multiplier=1,
                               allow_small_or_imprecise_dtypes=True).then_inc(made, 1)
                pool.wait_ge(padded, 64)
                pool.wait_ge(tiles_ready, 1)
                for g in range(IG):
                    for got, name in ((got_row, "rows"), (got_col, "cols")):
                        nc.gpsimd.indirect_dma_start(got[:, g, :], None, scratch[name],
                                                     bass.IndirectOffsetOnAxis(ap=tile_int[:, g:g + 1], axis=0)).then_inc(gathered, 16)

            @block.tensor
            def _(pe):
                pe.wait_ge(counts_done, 1)
                nc.tensor.matmul(total[:, 0:NB], ones[0:RP, :], count[0:RP, :], start=True, stop=True).then_inc(summed, 1)
                pe.wait_ge(tables_ready, 1)
                for n in range(2 * IG):
                    if n >= 2:
                        pe.wait_ge(turned_out, n - 1)
                    of = rowf if n % 2 == 0 else colf
                    nc.tensor.transpose(turned[:, n % 2, 0:P], of[:, n // 2, :], ident[:]).then_inc(turned_ready, 1)

            @block.vector
            def _(dve):
                link = chained(dve, chain)
                dve.wait_ge(made, 2)
                dve.wait_ge(loaded, 16)
                link(nc.vector.tensor_copy(rows[:], raw[:]))
                with dve.Fori(0, NB) as b:
                    nc.vector.tensor_scalar(below[:], rows[:], bound[0:RP, bass.ds(b, 1)], None, ALU.is_lt).then_inc(counted, 1)
                    dve.wait_ge(counted, 2 * b + 1)
                    nc.vector.tensor_reduce(count[0:RP, bass.ds(b, 1)], below[:], AX.X, ALU.add).then_inc(counted, 1)
                    dve.wait_ge(counted, 2 * b + 2)
                nc.vector.memset(many[:], 0.0).then_inc(counts_done, 1)
                dve.wait_ge(summed, 1)
                link(nc.vector.tensor_copy(ptr[:], total[:, 0:NB]))
                link(nc.vector.tensor_scalar(behind[:], total[:, 0:NB], float(P - 1), None, ALU.add))
                link(nc.vector.tensor_copy(up[:], behind[:]))
                link(nc.vector.tensor_scalar(ptr[:], ptr[:], 7, None, ALU.arith_shift_right))
                link(nc.vector.tensor_scalar(up[:], up[:], 7, None, ALU.arith_shift_right))
                link(nc.vector.tensor_copy(first[:], ptr[:]))
                link(nc.vector.tensor_copy(behind[:], up[:]))
                link(nc.vector.tensor_copy(count[:], total[:, 0:NB]))
                link(nc.vector.tensor_tensor(many[:], behind[:, 1:NBLK + 1], first[:, 0:NBLK], ALU.subtract))
                link(nc.vector.tensor_tensor(shift[:], count[:, 1:NBLK + 1], count[:, 0:NBLK], ALU.is_gt))
                link(nc.vector.tensor_tensor(many[:], many[:], shift[:], ALU.mult))
                link(nc.vector.tensor_tensor_scan(ends[:], ones[:, 0:NBLK], many[:], 0.0, ALU.mult, ALU.add))
                link(nc.vector.tensor_tensor(shift[:], first[:, 0:NBLK], ends[:], ALU.subtract))
                link(nc.vector.tensor_tensor(shift[:], shift[:], many[:], ALU.add))
                wide = [P, IG, NBLK]
                ends_b = ends[:].unsqueeze(1).to_broadcast(wide)
                shift_b = shift[:].unsqueeze(1).to_broadcast(wide)
                link(nc.vector.tensor_tensor(table[:], ends_b, item[:].unsqueeze(2).to_broadcast(wide), ALU.is_le))
                link(nc.vector.tensor_reduce(block_of[:], table[:], AX.X, ALU.add))
                link(nc.vector.tensor_scalar(tile_of[:], block_of[:], float(P), None, ALU.mult))
                link(nc.vector.tensor_tensor(table[:], bound[:, 0:NBLK].unsqueeze(1).to_broadcast(wide),
                                             tile_of[:].unsqueeze(2).to_broadcast(wide), ALU.is_equal))
                link(nc.vector.tensor_tensor(table[:], table[:], shift_b, ALU.mult))
                link(nc.vector.tensor_reduce(tile_of[:], table[:], AX.X, ALU.add))
                link(nc.vector.tensor_tensor(tile_of[:], tile_of[:], item[:], ALU.add))
                link(nc.vector.tensor_scalar(tile_of[:], tile_of[:], float(ET - 1), None, ALU.min))
                link(nc.vector.tensor_copy(block_int[:], block_of[:]))
                nc.vector.tensor_copy(tile_int[:], tile_of[:]).then_inc(tiles_ready, 1)
                dve.wait_ge(gathered, 16 * 2 * IG)
                link(nc.vector.tensor_copy(rowf[:], got_row[:]))
                link(nc.vector.tensor_copy(colf[:], got_col[:]))
                link(nc.vector.tensor_scalar(tile_of[:], block_of[:], float(NBLK), float(PAD_ROW), ALU.is_equal, ALU.mult))
                link(nc.vector.tensor_tensor(key[:], rowf[:], tile_of[:].unsqueeze(2).to_broadcast([P, IG, P]), ALU.add))
                link(nc.vector.tensor_scalar(tile_of[:], block_of[:], float(P), None, ALU.mult))
                nc.vector.tensor_tensor(rowf[:], rowf[:], tile_of[:].unsqueeze(2).to_broadcast([P, IG, P]),
                                        ALU.subtract).then_inc(tables_ready, 1)
                for n in range(2 * IG):
                    dve.wait_ge(turned_ready, n + 1)
                    to = rel if n % 2 == 0 else col
                    nc.vector.tensor_copy(to[:, (n // 2) * P:(n // 2 + 1) * P], turned[:, n % 2, 0:P]).then_inc(turned_out, 1)




def load_blocks(nc, item_block, q, engine):
    _, values = nc.values_load_multi_w_load_instructions(
        item_block[0:1, bass.ds(q * QUAD, QUAD)], engines=[engine], min_val=0, max_val=NB - 1,
        skip_runtime_bounds_check_because="item_tables counts at most FULL + 1 block ends before an item")
    return values


def edge_scores(nc, st, q_all, k_dram, rel, col, item_block, iota_free, ident, scores):
    with ExitStack() as ctx:
        def sb(name, shape, dt=F32):
            return ctx.enter_context(nc.sbuf_tensor(f"sc_{name}", shape, dt))

        kg = sb("kg", [P, RING, QUAD, D])
        index = sb("index", [P, RING, QUAD], I32)
        hot = sb("hot", [P, 2, QUAD, P])
        hot_t = sb("hot_t", [P, 2, QUAD, P])
        product = sb("product", [P, QUAD, D])
        pt = ctx.enter_context(nc.psum_tensor("sc_pt", [P, 2, 512], F32))
        pq = ctx.enter_context(nc.psum_tensor("sc_pq", [P, 2, 2, 512], F32))
        gathered = [st.sem(f"sc_gathered{k}") for k in range(RING * QUAD)]
        index_ready = st.sem("sc_index_ready")
        hot_ready = st.sem("sc_hot_ready")
        hot_turned = st.sem("sc_hot_turned")
        hot_t_ready = st.sem("sc_hot_t_ready")
        q_expanded = st.sem("sc_q_expanded")
        product_ready = st.sem("sc_product_ready")
        reduced = st.sem("sc_reduced")
        QUADS = NI // QUAD
        with nc.Block() as block:
            @block.gpsimd
            def _(pool):
                nc.gpsimd.memset(col[:, NI:NI + QUAD], 0).then_inc(index_ready, 1)
                nc.gpsimd.tensor_copy(index[:, 0, :], col[:, 0:QUAD]).then_inc(index_ready, 1)
                with pool.Fori(0, QUADS // RING) as s:
                    for u in range(RING):
                        q = s * RING + u
                        pool.wait_ge(product_ready, q * 2)
                        pool.wait_ge(index_ready, q + 2)
                        nc.gpsimd.tensor_copy(index[:, (u + 1) % RING, :],
                                              col[:, bass.ds((q + 1) * QUAD, QUAD)]).then_inc(index_ready, 1)
                        for j in range(QUAD):
                            nc.gpsimd.indirect_dma_start(
                                kg[:, u, j, :], None, k_dram,
                                bass.IndirectOffsetOnAxis(ap=index[:, u, j:j + 1], axis=0)).then_inc(gathered[u * QUAD + j], 16)

            @block.tensor
            def _(pe):
                def turn(u):
                    for j in range(QUAD):
                        last = nc.tensor.transpose(pt[:, u, j * P:(j + 1) * P], hot[:, u, j, :], ident[:])
                    last.then_inc(hot_turned, 1)

                pe.wait_ge(hot_ready, 1)
                turn(0)
                with pe.Fori(0, QUADS // 2) as s:
                    for u in range(2):
                        q = s * 2 + u
                        blk = load_blocks(nc, item_block, q, mybir.EngineType.PE)
                        pe.wait_ge(hot_t_ready, q + 1)
                        for half in range(2):
                            pe.wait_ge(product_ready, q * 2 + half + 1)
                            for j in (2 * half, 2 * half + 1):
                                last = nc.tensor.matmul(pq[:, u, half, (j % 2) * D:(j % 2 + 1) * D], hot_t[:, u, j, :],
                                                        q_all[:, bass.ds(blk[j], 1), :].rearrange("p a d -> p (a d)"),
                                                        start=True, stop=True)
                            last.then_inc(q_expanded, 1)
                            if half == 0:
                                pe.wait_ge(hot_ready, q + 2)
                                turn(1 - u)

            @block.scalar
            def _(act):
                def copy_turned(u):
                    nc.scalar.copy(hot_t[:, u, :, :].rearrange("p j n -> p (j n)"), pt[:, u, 0:QUAD * P]).then_inc(hot_t_ready, 1)

                act.wait_ge(hot_turned, 1)
                copy_turned(0)
                with act.Fori(0, QUADS // 2) as s:
                    for u in range(2):
                        q = s * 2 + u
                        act.wait_ge(q_expanded, q * 2)
                        act.wait_ge(hot_turned, q + 2)
                        copy_turned(1 - u)

            @block.vector
            def _(dve):
                def one_hots(q, u):
                    for j in range(QUAD):
                        last = nc.vector.tensor_scalar(hot[:, u, j, :], iota_free[:], rel[:, bass.ds(q * QUAD + j, 1)], None, ALU.is_equal)
                    last.then_inc(hot_ready, 1)

                nc.vector.memset(rel[:, NI:NI + QUAD], float(P)).then_inc(product_ready, 4)
                nc.vector.memset(product[:], 0.0).then_inc(reduced, 2)
                one_hots(0, 0)
                with dve.Fori(0, QUADS // RING) as s:
                    for v in range(RING):
                        q, u = s * RING + v, v % 2
                        dve.wait_ge(hot_turned, q)
                        one_hots(q + 1, 1 - u)
                        for half in range(2):
                            pair = slice(2 * half, 2 * half + 2)
                            dve.wait_ge(q_expanded, q * 2 + half + 1)
                            for j in (2 * half, 2 * half + 1):
                                dve.wait_ge(gathered[v * QUAD + j], s * 16 + 16)
                            dve.wait_ge(reduced, q * 2 + half + 1)
                            nc.vector.tensor_tensor(product[:, pair, :].rearrange("p j d -> p (j d)"),
                                                    kg[:, v, pair, :].rearrange("p j d -> p (j d)"),
                                                    pq[:, u, half, :], ALU.mult).then_inc(product_ready, 1)
                            dve.wait_ge(product_ready, q * 2 + half + 5)
                            nc.vector.tensor_reduce(
                                scores[:, bass.ds(q * QUAD + 2 * half, 2), :].rearrange("p j h -> p (j h)"),
                                product[:, pair, :].rearrange("p j (h d) -> p (j h) d", h=HEADS),
                                AX.X, ALU.add).then_inc(reduced, 1)


def softmax_over_rows(nc, st, scores, keys, bounce, ident):
    view = scores[:].rearrange("p (c g) h -> p g c h", c=CH)
    largest = scores[:].rearrange("p i h -> p (i h)")
    keys_flat = keys.rearrange("i e -> (i e)")
    GROUPS = CI // QUAD
    with ExitStack() as ctx:
        def sb(name, shape, dt=F32):
            return ctx.enter_context(nc.sbuf_tensor(f"sm_{name}", shape, dt))

        line = sb("line", [P, CL])
        key = sb("key", [P, CL], I16)
        cut = sb("cut", [P, CL + 1], BF16)
        part = sb("part", [P, 2, QUAD * P])
        end_keys = sb("end_keys", [HEADS, 2, CH], I16)
        end_keyf = sb("end_keyf", [HEADS, 2, CH])
        same = sb("same", [HEADS, CH])
        forth = sb("forth", [HEADS, CH])
        back = sb("back", [HEADS, CH])
        ends = sb("ends", [HEADS, CH])
        reach = sb("reach", [HEADS, CH])
        carried = sb("carried", [HEADS, CH])
        carry = sb("carry", [P, 2])
        turned = ctx.enter_context(nc.psum_tensor("sm_turned", [P, 2, 512], F32))
        part_ready = st.sem("sm_part_ready")
        turned_ready = st.sem("sm_turned_ready")
        turned_out = st.sem("sm_turned_out")
        keys_loaded = st.sem("sm_keys_loaded")
        chain = st.sem("sm_chain")
        bounced = st.sem("sm_bounced")
        to_bounce = st.sem("sm_to_bounce")
        differences = st.sem("sm_differences")
        with nc.Block() as block:
            @block.sync
            def _(sp):
                for c in range(CH):
                    sp.dma_start(key[c * HEADS:(c + 1) * HEADS, :],
                                 keys_flat[c * CL:(c + 1) * CL].unsqueeze(0).to_broadcast([HEADS, CL])).then_inc(keys_loaded, 16)
                for n, at in enumerate((0, CL - 1)):
                    ends_of = keys_flat.rearrange("(c l) -> c l", c=CH)[:, at:at + 1].rearrange("c o -> o c")
                    sp.dma_start(end_keys[:, n, :], ends_of.to_broadcast([HEADS, CH]),
                                 allow_slow_non_contiguous=True).then_inc(keys_loaded, 16)
                for n, at in enumerate((CL - 1, 0)):
                    sp.wait_ge(to_bounce, 2 * n + 1)
                    sp.dma_start(bounce[0], largest[:, at:at + 1]).then_inc(bounced, 16)
                    sp.wait_ge(bounced, 16 * (4 * n + 1))
                    sp.dma_start(ends[:], bounce[0].rearrange("(c h) o -> h (c o)", h=HEADS),
                                 allow_slow_non_contiguous=True).then_inc(bounced, 16)
                    sp.wait_ge(to_bounce, 2 * n + 2)
                    sp.wait_ge(bounced, 16 * (4 * n + 2))
                    sp.dma_start(bounce[1].rearrange("(c h) o -> h (c o)", h=HEADS), carried[:],
                                 allow_slow_non_contiguous=True).then_inc(bounced, 16)
                    sp.wait_ge(bounced, 16 * (4 * n + 3))
                    sp.dma_start(carry[:, n:n + 1], bounce[1]).then_inc(bounced, 16)

            @block.scalar
            def _(act):
                with act.Fori(0, GROUPS // 2) as s:
                    for u in range(2):
                        g = s * 2 + u
                        act.wait_ge(turned_ready, s * 2)
                        nc.scalar.copy(part[:, u, :].rearrange("p (g c h) -> p g c h", g=QUAD, c=CH),
                                       view[:, bass.ds(g * QUAD, QUAD), :, :]).then_inc(part_ready, 1)
                act.wait_ge(differences, 1)
                with act.Fori(0, GROUPS // 2) as s:
                    for u in range(2):
                        g = s * 2 + u
                        act.wait_ge(turned_ready, s * 2 + GROUPS)
                        nc.scalar.activation(part[:, u, :], line[:, bass.ds(g * QUAD * P, QUAD * P)], ACT.Exp).then_inc(part_ready, 1)

            @block.tensor
            def _(pe):
                with pe.Fori(0, GROUPS) as s:
                    for u in range(2):
                        pe.wait_ge(part_ready, s * 2 + u + 1)
                        pe.wait_ge(turned_out, s * 2)
                        for j in range(QUAD):
                            last = nc.tensor.transpose(turned[:, u, j * P:(j + 1) * P], part[:, u, j * P:(j + 1) * P], ident[:])
                        last.then_inc(turned_ready, 1)

            @block.vector
            def _(dve):
                link = chained(dve, chain)
                dve.wait_ge(keys_loaded, 16 * (CH + 2))
                link(nc.vector.memset(cut[:, 0:1], 0.0))
                link(nc.vector.memset(cut[:, CL:CL + 1], 0.0))
                link(nc.vector.tensor_tensor(cut[:, 1:CL], key[:, 1:CL], key[:, 0:CL - 1], ALU.not_equal))
                link(nc.vector.tensor_scalar(cut[:, 1:CL], cut[:, 1:CL], -BIG, None, ALU.mult))
                link(nc.vector.tensor_copy(end_keyf[:], end_keys[:]))
                link(nc.vector.memset(same[:], 1.0))
                link(nc.vector.tensor_tensor(same[:, 0:CH - 1], end_keyf[:, 0, 1:CH], end_keyf[:, 1, 0:CH - 1], ALU.not_equal))
                link(nc.vector.tensor_tensor(reach[:], end_keyf[:, 0, :], end_keyf[:, 1, :], ALU.not_equal))
                link(nc.vector.tensor_tensor(back[:], same[:], reach[:], ALU.max))
                link(nc.vector.memset(forth[:], 1.0))
                link(nc.vector.tensor_tensor(forth[:, 1:CH], same[:, 0:CH - 1], reach[:, 1:CH], ALU.max))
                for flags in (same, forth, back):
                    link(nc.vector.tensor_scalar(flags[:], flags[:], -BIG, None, ALU.mult))
                with dve.Fori(0, GROUPS // 2) as s:
                    for u in range(2):
                        g = s * 2 + u
                        dve.wait_ge(turned_ready, g + 1)
                        nc.vector.tensor_copy(line[:, bass.ds(g * QUAD * P, QUAD * P)], turned[:, u, :]).then_inc(turned_out, 1)
                dve.wait_ge(turned_out, GROUPS)

                link(nc.vector.tensor_tensor_scan(largest, cut[:, 0:CL], line[:], -BIG, ALU.add, ALU.max))
                nc.vector.memset(carried[:], -BIG).then_inc(to_bounce, 1)
                dve.wait_ge(bounced, 32)
                link(nc.vector.tensor_tensor_scan(reach[:], forth[:], ends[:], -BIG, ALU.add, ALU.max))
                nc.vector.tensor_tensor(carried[:, 1:CH], reach[:, 0:CH - 1], same[:, 0:CH - 1], ALU.add).then_inc(to_bounce, 1)
                dve.wait_ge(bounced, 64)
                link(nc.vector.tensor_tensor_scan(largest, cut[:, 0:CL], line[:], carry[:, 0:1], ALU.add, ALU.max))
                link(nc.vector.tensor_tensor_scan(largest[:, ::-1], cut[:, :0:-1], largest[:, ::-1], -BIG, ALU.add, ALU.max))
                nc.vector.memset(carried[:], -BIG).then_inc(to_bounce, 1)
                dve.wait_ge(bounced, 96)
                link(nc.vector.tensor_tensor_scan(reach[:, ::-1], back[:, ::-1], ends[:, ::-1], -BIG, ALU.add, ALU.max))
                nc.vector.tensor_tensor(carried[:, 0:CH - 1], reach[:, 1:CH], same[:, 0:CH - 1], ALU.add).then_inc(to_bounce, 1)
                dve.wait_ge(bounced, 128)
                link(nc.vector.tensor_tensor_scan(largest[:, ::-1], cut[:, :0:-1], largest[:, ::-1], carry[:, 1:2], ALU.add, ALU.max))
                nc.vector.tensor_tensor(line[:], line[:], largest, ALU.subtract).then_inc(differences, 1)
                dve.wait_ge(differences, 1)
                with dve.Fori(0, GROUPS // 2) as s:
                    for u in range(2):
                        g = s * 2 + u
                        dve.wait_ge(turned_ready, g + GROUPS + 1)
                        nc.vector.tensor_copy(view[:, bass.ds(g * QUAD, QUAD), :, :],
                                              turned[:, u, :].rearrange("p (g c h) -> p g c h", g=QUAD, c=CH)).then_inc(turned_out, 1)
                dve.wait_ge(turned_out, 2 * GROUPS)


def aggregate(nc, st, probs, v_dram, rel, col, item_block, iota_free, acc):
    with ExitStack() as ctx:
        def sb(name, shape, dt=F32):
            return ctx.enter_context(nc.sbuf_tensor(f"ag_{name}", shape, dt))

        vg = sb("vg", [P, RING, QUAD, D])
        index = sb("index", [P, RING, QUAD], I32)
        hot = sb("hot", [P, 2, QUAD, P])
        weighted = sb("weighted", [P, 2, QUAD, AW])
        sums = ctx.enter_context(nc.psum_tensor("ag_sums", [P, 2, QUAD, 512], F32))
        gathered = [st.sem(f"ag_gathered{k}") for k in range(RING * QUAD)]
        index_ready = st.sem("ag_index_ready")
        hot_ready = st.sem("ag_hot_ready")
        p_ready = st.sem("ag_p_ready")
        weighted_ready = st.sem("ag_weighted_ready")
        summed = st.sem("ag_summed")
        added = st.sem("ag_added")
        QUADS = NI // QUAD
        with nc.Block() as block:
            @block.gpsimd
            def _(pool):
                nc.gpsimd.memset(col[:, NI:NI + QUAD], 0).then_inc(index_ready, 1)
                nc.gpsimd.tensor_copy(index[:, 0, :], col[:, 0:QUAD]).then_inc(index_ready, 1)
                with pool.Fori(0, QUADS // RING) as s:
                    for u in range(RING):
                        q = s * RING + u
                        pool.wait_ge(weighted_ready, q * 2)
                        pool.wait_ge(index_ready, q + 2)
                        nc.gpsimd.tensor_copy(index[:, (u + 1) % RING, :],
                                              col[:, bass.ds((q + 1) * QUAD, QUAD)]).then_inc(index_ready, 1)
                        for j in range(QUAD):
                            nc.gpsimd.indirect_dma_start(
                                vg[:, u, j, :], None, v_dram,
                                bass.IndirectOffsetOnAxis(ap=index[:, u, j:j + 1], axis=0)).then_inc(gathered[u * QUAD + j], 16)

            @block.scalar
            def _(act):
                with act.Fori(0, QUADS // 2) as s:
                    for u in range(2):
                        q = s * 2 + u
                        act.wait_ge(added, q * 4)
                        nc.scalar.copy(weighted[:, u, :, D:D + HEADS], probs[:, bass.ds(q * QUAD, QUAD), :]).then_inc(p_ready, 1)

            @block.tensor
            def _(pe):
                with pe.Fori(0, QUADS // 2) as s:
                    for u in range(2):
                        q = s * 2 + u
                        pe.wait_ge(added, q * 4)
                        pe.wait_ge(hot_ready, q + 1)
                        pe.wait_ge(p_ready, q + 1)
                        for half in range(2):
                            pe.wait_ge(weighted_ready, q * 2 + half + 5)
                            for j in (2 * half, 2 * half + 1):
                                last = nc.tensor.matmul(sums[:, u, j, 0:AW], hot[:, u, j, :], weighted[:, u, j, :], start=True, stop=True)
                            last.then_inc(summed, 1)

            @block.vector
            def _(dve):
                def weigh(q, v, s):
                    u = v % 2
                    for j in range(QUAD):
                        last = nc.vector.tensor_scalar(hot[:, u, j, :], iota_free[:], rel[:, bass.ds(q * QUAD + j, 1)], None, ALU.is_equal)
                    last.then_inc(hot_ready, 1)
                    for half in range(2):
                        pair = slice(2 * half, 2 * half + 2)
                        for j in (2 * half, 2 * half + 1):
                            dve.wait_ge(gathered[v * QUAD + j], s * 16 + 16)
                        nc.vector.tensor_tensor(
                            weighted[:, u, pair, 0:D].rearrange("p j (h d) -> p j h d", h=HEADS),
                            vg[:, v, pair, :].rearrange("p j (h d) -> p j h d", h=HEADS),
                            probs[:, bass.ds(q * QUAD + 2 * half, 2), :].unsqueeze(3).to_broadcast([P, 2, HEADS, HD]),
                            ALU.mult).then_inc(weighted_ready, 1)

                def add(q, v):
                    u = v % 2
                    blk = load_blocks(nc, item_block, q, mybir.EngineType.DVE)
                    for j in range(QUAD):
                        dve.wait_ge(summed, q * 2 + j // 2 + 1)
                        dve.wait_ge(added, q * 4 + j + 4)
                        to = acc[:, bass.ds(blk[j], 1), :].rearrange("p a d -> p (a d)")
                        nc.vector.tensor_tensor(to, to, sums[:, u, j, 0:AW], ALU.add).then_inc(added, 1)

                nc.vector.memset(acc[:], 0.0).then_inc(added, 4)
                nc.vector.memset(weighted[:, :, :, AW - 1], 1.0).then_inc(weighted_ready, 4)
                weigh(0, 0, 0)
                with dve.Fori(0, QUADS // RING - 1) as s:
                    for v in range(RING):
                        q = s * RING + v
                        weigh(q + 1, (v + 1) % RING, s + (v + 1) // RING)
                        add(q, v)
                for v in range(RING):
                    q = QUADS - RING + v
                    if v + 1 < RING:
                        weigh(q + 1, v + 1, QUADS // RING - 1)
                    add(q, v)


def attention_output(nc, st, acc, x, wo, bo, ident, ones):
    with ExitStack() as ctx:
        w = ctx.enter_context(nc.sbuf_tensor("ao_w", [P, DC, D], F32))
        bias = ctx.enter_context(nc.sbuf_tensor("ao_b", [1, D], F32))
        share = ctx.enter_context(nc.sbuf_tensor("ao_share", [P, NB, HEADS], F32))
        rows = ctx.enter_context(nc.sbuf_tensor("ao_rows", [P, 2, D], F32))
        turned = ctx.enter_context(nc.sbuf_tensor("ao_turned", [P, 2, D], F32))
        pt = ctx.enter_context(nc.psum_tensor("ao_pt", [P, 2, 512], F32))
        po = ctx.enter_context(nc.psum_tensor("ao_po", [P, 2, 512], F32))
        w_loaded = st.sem("ao_w_loaded")
        chain = st.sem("ao_chain")
        rows_ready = st.sem("ao_rows_ready")
        pt_ready = st.sem("ao_pt_ready")
        turned_ready = st.sem("ao_turned_ready")
        po_ready = st.sem("ao_po_ready")
        added = st.sem("ao_added")
        with nc.Block() as block:
            @block.sync
            def _(sp):
                sp.dma_start(w[:], wo.rearrange("(c p) n -> p c n", p=P)).then_inc(w_loaded, 16)
                sp.dma_start(bias[:], bo.rearrange("(a n) -> a n", a=1)).then_inc(w_loaded, 16)

            @block.vector
            def _(dve):
                link = chained(dve, chain)
                link(nc.vector.tensor_scalar(share[:], acc[:, :, D:D + HEADS], 1e-30, None, ALU.max))
                link(nc.vector.reciprocal(share[:], share[:]))
                with dve.Fori(0, NB // 2) as h:
                    b = h * 2
                    for k in range(2):
                        dve.wait_ge(pt_ready, b)
                        nc.vector.tensor_tensor(
                            rows[:, k, :].rearrange("p (h d) -> p h d", h=HEADS),
                            acc[:, bass.ds(b + k, 1), 0:D].rearrange("p a (h d) -> p (a h) d", h=HEADS),
                            share[:, bass.ds(b + k, 1), :].rearrange("p a h -> p (a h)").unsqueeze(2).to_broadcast([P, HEADS, HD]),
                            ALU.mult).then_inc(rows_ready, 1)
                    for k in range(2):
                        dve.wait_ge(po_ready, b + k + 1)
                        to = x[:, bass.ds(b + k, 1), :].rearrange("p a d -> p (a d)")
                        nc.vector.tensor_tensor(to, to, po[:, k, 0:D], ALU.add).then_inc(added, 1)

            @block.scalar
            def _(act):
                with act.Fori(0, NB // 2) as h:
                    b = h * 2
                    for k in range(2):
                        act.wait_ge(po_ready, b)
                        act.wait_ge(pt_ready, b + k + 1)
                        nc.scalar.copy(turned[:, k, :], pt[:, k, 0:D]).then_inc(turned_ready, 1)

            @block.tensor
            def _(pe):
                pe.wait_ge(w_loaded, 32)
                with pe.Fori(0, NB // 2) as h:
                    b = h * 2
                    for k in range(2):
                        pe.wait_ge(turned_ready, b)
                        pe.wait_ge(rows_ready, b + k + 1)
                        for c in range(DC):
                            last = nc.tensor.transpose(pt[:, k, c * P:(c + 1) * P], rows[:, k, c * P:(c + 1) * P], ident[:])
                        last.then_inc(pt_ready, 1)
                    for k in range(2):
                        pe.wait_ge(added, b)
                        pe.wait_ge(turned_ready, b + k + 1)
                        for c in range(DC):
                            nc.tensor.matmul(po[:, k, 0:D], turned[:, k, c * P:(c + 1) * P], w[:, c, :], start=(c == 0), stop=False)
                        nc.tensor.matmul(po[:, k, 0:D], ones[0:1, :], bias[:], start=False, stop=True).then_inc(po_ready, 1)


def turn(nc, st, name, x, affine, xt, ident, scale=None, shift=None):
    with ExitStack() as ctx:
        rows = ctx.enter_context(nc.sbuf_tensor(f"{name}_rows", [P, 2, D], F32))
        pt = ctx.enter_context(nc.psum_tensor(f"{name}_pt", [P, 2, 512], F32))
        rows_step = st.sem(f"{name}_rows_step")
        pt_ready = st.sem(f"{name}_pt_ready")
        out = st.sem(f"{name}_out")
        steps = len(affine)
        with nc.Block() as block:
            @block.vector
            def _(dve):
                with dve.Fori(0, NB // 2) as h:
                    b = h * 2
                    for k in range(2):
                        dve.wait_ge(pt_ready, b)
                        of = x[:, bass.ds(b + k, 1), :].rearrange("p a d -> p (a d)")
                        for n, (mean, rstd) in enumerate(affine):
                            if n:
                                dve.wait_ge(rows_step, (b + k) * steps + n)
                            nc.vector.tensor_scalar(rows[:, k, :], of, mean[:, bass.ds(b + k, 1)], rstd[:, bass.ds(b + k, 1)],
                                                    ALU.subtract, ALU.mult).then_inc(rows_step, 1)
                            of = rows[:, k, :]

            @block.tensor
            def _(pe):
                with pe.Fori(0, NB // 2) as h:
                    b = h * 2
                    for k in range(2):
                        pe.wait_ge(out, b)
                        pe.wait_ge(rows_step, (b + k + 1) * steps)
                        for c in range(DC):
                            last = nc.tensor.transpose(pt[:, k, c * P:(c + 1) * P], rows[:, k, c * P:(c + 1) * P], ident[:])
                        last.then_inc(pt_ready, 1)

            @block.scalar
            def _(act):
                with act.Fori(0, NB // 2) as h:
                    b = h * 2
                    for k in range(2):
                        act.wait_ge(pt_ready, b + k + 1)
                        if scale is None:
                            nc.scalar.copy(xt[:, :, bass.ds((b + k) * P, P)],
                                           pt[:, k, 0:D].rearrange("p (c n) -> p c n", c=DC)).then_inc(out, 1)
                        else:
                            for c in range(DC):
                                last = nc.scalar.activation(xt[:, c, bass.ds((b + k) * P, P)], pt[:, k, c * P:(c + 1) * P],
                                                            ACT.Identity, bias=shift[:, c:c + 1], scale=scale[:, c:c + 1])
                            last.then_inc(out, 1)


def first_largest(nc, link, values, mask, best, tmp, order, shape):
    link(nc.vector.tensor_reduce(best, values, AX.X, ALU.max))
    link(nc.vector.tensor_tensor(mask, values, best.unsqueeze(len(shape) - 1).to_broadcast(shape), ALU.is_equal))
    link(nc.vector.tensor_tensor(mask, mask, order, ALU.mult))
    link(nc.vector.tensor_reduce(tmp, mask, AX.X, ALU.max))
    link(nc.vector.tensor_tensor(mask, order, tmp.unsqueeze(len(shape) - 1).to_broadcast(shape), ALU.is_equal))


def route_two(nc, st, xt, wr, br, order, ident, picks, shares):
    with ExitStack() as ctx:
        def sb(name, shape, dt=F32):
            return ctx.enter_context(nc.sbuf_tensor(f"ro_{name}", shape, dt))

        w = sb("w", [P, DC, EX])
        bias = sb("bias", [EX, 1])
        lines = sb("lines", [EX, 2, 2 * P])
        logits = sb("logits", [P, NB, EX])
        best = sb("best", [P, NB])
        next_best = sb("next_best", [P, NB])
        tmp = sb("tmp", [P, NB])
        pl = ctx.enter_context(nc.psum_tensor("ro_pl", [EX, 2, 512], F32))
        pt = ctx.enter_context(nc.psum_tensor("ro_pt", [P, 2, 512], F32))
        loaded = st.sem("ro_loaded")
        product = st.sem("ro_product")
        line_ready = st.sem("ro_line_ready")
        line_turned = st.sem("ro_line_turned")
        logits_out = st.sem("ro_logits_out")
        chain = st.sem("ro_chain")
        gap_ready = st.sem("ro_gap_ready")
        ratio_ready = st.sem("ro_ratio_ready")
        WINDOWS = NB // 2
        with nc.Block() as block:
            @block.sync
            def _(sp):
                sp.dma_start(w[:], wr.rearrange("(c p) e -> p c e", p=P)).then_inc(loaded, 16)
                sp.dma_start(bias[:], br.rearrange("(e a) -> e a", a=1)).then_inc(loaded, 16)

            @block.tensor
            def _(pe):
                pe.sem_inc(line_turned, 2)
                pe.wait_ge(loaded, 32)

                def product_of(window, u):
                    for c in range(DC):
                        last = nc.tensor.matmul(pl[:, u, 0:2 * P], w[:, c, :], xt[:, c, bass.ds(window * 2 * P, 2 * P)],
                                                start=(c == 0), stop=(c == DC - 1))
                    last.then_inc(product, 1)

                def turn_lines(window, u):
                    pe.wait_ge(logits_out, window + 1)
                    pe.wait_ge(line_ready, window + 2)
                    for j in range(2):
                        last = nc.tensor.matmul(pt[:, u, j * EX:(j + 1) * EX], lines[:, u, j * P:(j + 1) * P], ident[0:EX, 0:EX],
                                                start=True, stop=True)
                    last.then_inc(line_turned, 1)

                product_of(0, 0)
                with pe.Fori(0, WINDOWS // 2) as s:
                    for u in range(2):
                        window = s * 2 + u
                        pe.wait_ge(line_ready, window + 1)
                        product_of(window + 1, 1 - u)
                        turn_lines(window, u)
                turn_lines(WINDOWS - 1, 0)

            @block.scalar
            def _(act):
                act.sem_inc(line_ready, 1)
                act.wait_ge(loaded, 32)

                def line(window, u):
                    act.wait_ge(product, window + 1)
                    act.wait_ge(line_turned, window + 1)
                    nc.scalar.activation(lines[:, u, :], pl[:, u, 0:2 * P], ACT.Identity, bias=bias[:, 0:1]).then_inc(line_ready, 1)

                with act.Fori(0, WINDOWS // 2) as s:
                    for u in range(2):
                        line(s * 2 + u, u)
                line(WINDOWS - 1, 0)
                act.wait_ge(gap_ready, 1)
                nc.scalar.activation(tmp[:], next_best[:], ACT.Exp).then_inc(ratio_ready, 1)

            @block.vector
            def _(dve):
                dve.sem_inc(logits_out, 2)

                def out(window, u):
                    dve.wait_ge(line_turned, window + 3)
                    nc.vector.tensor_copy(logits[:, bass.ds(window * 2, 2), :],
                                          pt[:, u, 0:2 * EX].rearrange("p (j e) -> p j e", e=EX)).then_inc(logits_out, 1)

                with dve.Fori(0, WINDOWS // 2) as s:
                    for u in range(2):
                        out(s * 2 + u, u)
                out(WINDOWS - 1, 0)
                dve.wait_ge(logits_out, WINDOWS + 2)
                link = chained(dve, chain)
                shape = [P, NB, EX]
                order_b = order[:].unsqueeze(1).to_broadcast(shape)
                first_largest(nc, link, logits[:], picks[0][:], best[:], tmp[:], order_b, shape)
                link(nc.vector.scalar_tensor_tensor(out=logits[:], in0=picks[0][:], scalar=-BIG, in1=logits[:], op0=ALU.mult, op1=ALU.add))
                first_largest(nc, link, logits[:], picks[1][:], next_best[:], tmp[:], order_b, shape)
                nc.vector.tensor_tensor(next_best[:], next_best[:], best[:], ALU.subtract).then_inc(gap_ready, 1)
                dve.wait_ge(ratio_ready, 1)
                link(nc.vector.tensor_scalar(best[:], tmp[:], 1.0, None, ALU.add))
                link(nc.vector.reciprocal(shares[0][:], best[:]))
                link(nc.vector.tensor_tensor(shares[1][:], tmp[:], shares[0][:], ALU.mult))


def slots(nc, st, name, picks, scatter, gather, expert_of, ones, iota_part, before, tiles):
    listed = expert_of.shape[1]
    with ExitStack() as ctx:
        def sb(what, shape, dt=F32):
            return ctx.enter_context(nc.sbuf_tensor(f"{name}_{what}", shape, dt))

        node = sb("node", [P, NB])
        valid = sb("valid", [P, NB])
        tile_no = sb("tile_no", [P, listed])
        both = sb("both", [P, NB, EX])
        totals = sb("totals", [P, NB, EX])
        place = sb("place", [P, NB, EX])
        upto = sb("upto", [P, NB, EX])
        count = sb("count", [P, EX])
        count_int = sb("count_int", [P, EX], I32)
        ends = sb("ends", [P, EX])
        slot = sb("slot", [P, NB])
        aside = sb("aside", [P, NB])
        behind = sb("behind", [P, NB])
        moved = sb("moved", [P, NB])
        table = sb("table", [1, listed, EX])
        expert = sb("expert", [1, listed])
        ps = ctx.enter_context(nc.psum_tensor(f"{name}_ps", [P, 2, 512], F32))
        made = st.sem(f"{name}_made")
        chain = st.sem(f"{name}_chain")
        masks_ready = st.sem(f"{name}_masks_ready")
        summed = st.sem(f"{name}_summed")
        with nc.Block() as block:
            @block.gpsimd
            def _(pool):
                nc.gpsimd.iota(node[:], pattern=[[P, NB]], base=0, channel_multiplier=1,
                               allow_small_or_imprecise_dtypes=True).then_inc(made, 1)
                nc.gpsimd.iota(tile_no[:], pattern=[[1, listed]], base=0, channel_multiplier=0,
                               allow_small_or_imprecise_dtypes=True).then_inc(made, 1)

            @block.tensor
            def _(pe):
                pe.wait_ge(masks_ready, 1)
                flat = both[:].rearrange("p b e -> p (b e)")
                nc.tensor.matmul(ps[:, 0, 0:NB * EX], ones[:], flat, start=True, stop=True)
                nc.tensor.matmul(ps[:, 1, 0:NB * EX], before[:], flat, start=True, stop=True).then_inc(summed, 1)

            @block.vector
            def _(dve):
                link = chained(dve, chain)
                dve.wait_ge(made, 2)
                wide = [P, NB, EX]
                link(nc.vector.tensor_scalar(valid[:], node[:], float(N), None, ALU.is_lt))
                for pick in picks:
                    link(nc.vector.tensor_tensor(pick[:], pick[:], valid[:].unsqueeze(2).to_broadcast(wide), ALU.mult))
                if len(picks) == 2:
                    nc.vector.tensor_tensor(both[:], picks[0][:], picks[1][:], ALU.add).then_inc(masks_ready, 1)
                else:
                    nc.vector.tensor_copy(both[:], picks[0][:]).then_inc(masks_ready, 1)
                dve.wait_ge(summed, 1)
                view = lambda n: ps[:, n, 0:NB * EX].rearrange("p (b e) -> p b e", e=EX)
                link(nc.vector.tensor_copy(totals[:], view(0)))
                for e in range(EX):
                    link(nc.vector.tensor_tensor_scan(upto[:, :, e], ones[:, 0:NB], totals[:, :, e], 0.0, ALU.mult, ALU.add))
                link(nc.vector.tensor_tensor(place[:], view(1), upto[:], ALU.add))
                link(nc.vector.tensor_tensor(place[:], place[:], totals[:], ALU.subtract))
                link(nc.vector.tensor_scalar(count[:], upto[:, NB - 1, :], float(P - 1), None, ALU.add))
                link(nc.vector.tensor_copy(count_int[:], count[:]))
                link(nc.vector.tensor_scalar(count_int[:], count_int[:], 7, None, ALU.arith_shift_right))
                link(nc.vector.tensor_copy(count[:], count_int[:]))
                link(nc.vector.tensor_tensor_scan(ends[:], ones[:, 0:EX], count[:], 0.0, ALU.mult, ALU.add))
                link(nc.vector.tensor_tensor(count[:], ends[:], count[:], ALU.subtract))
                link(nc.vector.tensor_scalar(count[:], count[:], float(P), None, ALU.mult))
                link(nc.vector.tensor_tensor(place[:], place[:], count[:].unsqueeze(1).to_broadcast(wide), ALU.add))
                link(nc.vector.tensor_scalar(aside[:], valid[:], -1.0, 1.0, ALU.mult, ALU.add))
                link(nc.vector.tensor_scalar(behind[:], iota_part[:].to_broadcast([P, NB]), float(tiles * P), None, ALU.add))
                for k, pick in enumerate(picks):
                    link(nc.vector.tensor_tensor(upto[:], pick[:], place[:], ALU.mult))
                    link(nc.vector.tensor_reduce(slot[:], upto[:], AX.X, ALU.add))
                    link(nc.vector.tensor_copy(gather[k][:], slot[:]))
                    link(nc.vector.scalar_tensor_tensor(out=moved[:], in0=behind[:], scalar=float(k * P), in1=aside[:],
                                                        op0=ALU.add, op1=ALU.mult))
                    link(nc.vector.tensor_tensor(slot[:], slot[:], moved[:], ALU.add))
                    link(nc.vector.tensor_copy(scatter[k][:], slot[:]))
                link(nc.vector.tensor_tensor(table[:], ends[0:1, :].unsqueeze(1).to_broadcast([1, listed, EX]),
                                             tile_no[0:1, :].unsqueeze(2).to_broadcast([1, listed, EX]), ALU.is_le))
                link(nc.vector.tensor_reduce(expert[:], table[:], AX.X, ALU.add))
                link(nc.vector.tensor_scalar(expert[:], expert[:], float(EX - 1), None, ALU.min))
                link(nc.vector.tensor_copy(expert_of[:], expert[:]))


def clear_rows(nc, st, name, rows_dram):
    blocks = rows_dram.shape[0] // P
    with ExitStack() as ctx:
        zero = ctx.enter_context(nc.sbuf_tensor(f"{name}_zero", [P, D], F32))
        made = st.sem(f"{name}_made")
        stored = st.sem(f"{name}_stored")
        with nc.Block() as block:
            @block.vector
            def _(dve):
                nc.vector.memset(zero[:], 0.0).then_inc(made, 1)

            @block.sync
            def _(sp):
                sp.wait_ge(made, 1)
                sp.dma_start(rows_dram.rearrange("(t p) d -> p t d", p=P),
                             zero[:].unsqueeze(1).to_broadcast([P, blocks, D])).then_inc(stored, 16)
                sp.wait_ge(stored, 16)


def scatter_rows(nc, st, name, x, affine, scatter, rows_dram):
    picks = len(scatter)
    steps = len(affine)
    RS = 7
    assert NX % RS == 0
    with ExitStack() as ctx:
        rows = ctx.enter_context(nc.sbuf_tensor(f"{name}_rows", [P, RS, D], F32))
        index = ctx.enter_context(nc.sbuf_tensor(f"{name}_index", [P, RS, picks], I32))
        step = st.sem(f"{name}_step")
        index_ready = st.sem(f"{name}_index_ready")
        left = [st.sem(f"{name}_left{k}") for k in range(RS)]
        with nc.Block() as block:
            @block.vector
            def _(dve):
                def norm(h, k, first=False):
                    b = h * RS + k
                    if not first:
                        dve.wait_ge(left[k], h * 16 * picks)
                    of = x[:, bass.ds(b, 1), :].rearrange("p a d -> p (a d)")
                    for n, (mean, rstd) in enumerate(affine):
                        if n:
                            dve.wait_ge(step, b * steps + n)
                        nc.vector.tensor_scalar(rows[:, k, :], of, mean[:, bass.ds(b, 1)], rstd[:, bass.ds(b, 1)],
                                                ALU.subtract, ALU.mult).then_inc(step, 1)
                        of = rows[:, k, :]

                for k in range(RS):
                    norm(0, k, first=True)
                with dve.Fori(1, NX // RS) as h:
                    for k in range(RS):
                        norm(h, k)

            @block.gpsimd
            def _(pool):
                def copy_index(b, k):
                    for j in range(picks):
                        nc.gpsimd.tensor_copy(index[:, k, j:j + 1], scatter[j][:, bass.ds(b, 1)]).then_inc(index_ready, 1)

                def send(h, k, first=False, last=False):
                    b = h * RS + k
                    pool.wait_ge(step, b * steps + steps)
                    pool.wait_ge(index_ready, b * picks + picks)
                    if k == RS - 1:
                        pool.wait_ge(left[0], h * 16 * picks + 16 * picks)
                    elif not first:
                        pool.wait_ge(left[k + 1], h * 16 * picks)
                    if not last:
                        copy_index(b + 1, (k + 1) % RS)
                    for j in range(picks):
                        nc.gpsimd.indirect_dma_start(
                            rows_dram, bass.IndirectOffsetOnAxis(ap=index[:, k, j:j + 1], axis=0),
                            rows[:, k, :], None).then_inc(left[k], 16)

                copy_index(0, 0)
                for k in range(RS):
                    send(0, k, first=True)
                with pool.Fori(1, NX // RS - 1) as h:
                    for k in range(RS):
                        send(h, k)
                for k in range(RS):
                    send(NX // RS - 1, k, last=(k == RS - 1))
                for k in range(RS):
                    pool.wait_ge(left[k], 16 * picks * (NX // RS))


def gather_rows(nc, st, name, y_dram, gather, shares, x):
    picks = len(gather)
    RD = 6
    LOOP = NX // RD
    assert NX == LOOP * RD + 1
    with ExitStack() as ctx:
        rows = ctx.enter_context(nc.sbuf_tensor(f"{name}_rows", [P, RD, picks, D], F32))
        index = ctx.enter_context(nc.sbuf_tensor(f"{name}_index", [P, RD, picks], I32))
        index_ready = st.sem(f"{name}_index_ready")
        came = [st.sem(f"{name}_came{k}") for k in range(RD)]
        added = st.sem(f"{name}_added")
        with nc.Block() as block:
            @block.gpsimd
            def _(pool):
                def copy_index(b, k):
                    for j in range(picks):
                        nc.gpsimd.tensor_copy(index[:, k, j:j + 1], gather[j][:, bass.ds(b, 1)]).then_inc(index_ready, 1)

                def fetch(s, k, first=False, last=False):
                    b = s * RD + k
                    pool.wait_ge(added, b * picks + picks)
                    pool.wait_ge(index_ready, b * picks + picks)
                    if k == RD - 1:
                        pool.wait_ge(came[0], s * 16 * picks + 16 * picks)
                    elif not first and not last:
                        pool.wait_ge(came[k + 1], s * 16 * picks)
                    if not last:
                        copy_index(b + 1, (k + 1) % RD)
                    for j in range(picks):
                        nc.gpsimd.indirect_dma_start(
                            rows[:, k, j, :], None, y_dram,
                            bass.IndirectOffsetOnAxis(ap=index[:, k, j:j + 1], axis=0)).then_inc(came[k], 16)

                copy_index(0, 0)
                for k in range(RD):
                    fetch(0, k, first=True)
                with pool.Fori(1, LOOP) as s:
                    for k in range(RD):
                        fetch(s, k)
                fetch(LOOP, 0, last=True)

            @block.vector
            def _(dve):
                dve.sem_inc(added, RD * picks)

                def add(s, k):
                    b = s * RD + k
                    dve.wait_ge(came[k], s * 16 * picks + 16 * picks)
                    to = x[:, bass.ds(b, 1), :].rearrange("p a d -> p (a d)")
                    for j in range(picks):
                        dve.wait_ge(added, b * picks + RD * picks + j)
                        nc.vector.scalar_tensor_tensor(out=to, in0=rows[:, k, j, :], scalar=shares[j][:, bass.ds(b, 1)],
                                                       in1=to, op0=ALU.mult, op1=ALU.add).then_inc(added, 1)

                with dve.Fori(0, LOOP) as s:
                    for k in range(RD):
                        add(s, k)
                add(LOOP, 0)


NX = FULL + 1
T1 = -(-2 * N // P) + EX - 1
T1 += T1 % 2
T2 = -(-N // P) + EX - 1
T2 += T2 % 2


def bias_rows(sp, to, of, sem):
    sp.dma_start(to, of.rearrange("e n -> (e n)").unsqueeze(0).to_broadcast([P, of.shape[0] * of.shape[1]])).then_inc(sem, 16)


def mixture_tiles(nc, st, rows_dram, y_dram, expert_of, w1, b1, w2, b2, gamma, beta, ident):
    H = w1.shape[2]
    HC = H // P
    with ExitStack() as ctx:
        def sb(name, shape, dt=F32):
            return ctx.enter_context(nc.sbuf_tensor(f"mx_{name}", shape, dt))

        w1_sb = sb("w1", [P, EX, DC, H])
        w2_sb = sb("w2", [P, EX, HC, D])
        b1_sb = sb("b1", [P, EX, H])
        b2_sb = sb("b2", [P, EX, D])
        rows = sb("rows", [P, 4, D])
        xt = sb("xt", [P, 2, D])
        raw = sb("raw", [P, 2, H])
        hidden = sb("hidden", [P, 2, H])
        hidden_t = sb("hidden_t", [P, 2, H])
        y = sb("y", [P, 2, D])
        px = ctx.enter_context(nc.psum_tensor("mx_px", [P, 512], F32))
        ph = ctx.enter_context(nc.psum_tensor("mx_ph", [P, 2, 512], F32))
        pt = ctx.enter_context(nc.psum_tensor("mx_pt", [P, 2, 512], F32))
        py = ctx.enter_context(nc.psum_tensor("mx_py", [P, 2, 512], F32))
        loaded = st.sem("mx_loaded")
        came = [st.sem(f"mx_came{k}") for k in range(4)]
        x_turned = st.sem("mx_x_turned")
        xt_ready = st.sem("mx_xt_ready")
        h_product = st.sem("mx_h_product")
        raw_ready = st.sem("mx_raw_ready")
        hidden_ready = st.sem("mx_hidden_ready")
        h_turned = st.sem("mx_h_turned")
        hidden_t_ready = st.sem("mx_hidden_t_ready")
        y_product = st.sem("mx_y_product")
        y_ready = st.sem("mx_y_ready")
        y_left = [st.sem(f"mx_y_left{k}") for k in range(2)]
        ROUNDS = (T1 - 2) // 4
        assert T1 == 4 * ROUNDS + 2
        with nc.Block() as block:
            @block.sync
            def _(sp):
                for e in range(EX):
                    sp.dma_start(w1_sb[:, e, :, :], w1[e].rearrange("(c p) h -> p c h", p=P)).then_inc(loaded, 16)
                    sp.dma_start(w2_sb[:, e, :, :], w2[e].rearrange("(c p) d -> p c d", p=P)).then_inc(loaded, 16)
                bias_rows(sp, b1_sb[:].rearrange("p e n -> p (e n)"), b1, loaded)
                bias_rows(sp, b2_sb[:].rearrange("p e n -> p (e n)"), b2, loaded)

                def fetch(i, k):
                    sp.dma_start(rows[:, k, :], rows_dram[bass.ds(i * P, P), :]).then_inc(came[k], 16)

                def store(i, k):
                    sp.wait_ge(y_ready, i + 1)
                    sp.dma_start(y_dram[bass.ds(i * P, P), :], y[:, k % 2, :]).then_inc(y_left[k % 2], 16)

                for k in range(4):
                    fetch(k, k)
                for i in range(4):
                    sp.wait_ge(x_turned, i + 1)
                    fetch(i + 4, i)
                    if i > 0:
                        store(i - 1, i - 1)
                with sp.Fori(1, ROUNDS) as s:
                    for k in range(4):
                        i = s * 4 + k
                        sp.wait_ge(x_turned, i + 1)
                        fetch(i + 4, k)
                        store(i - 1, (k + 3) % 4)
                for i in range(T1 - 2, T1 + 1):
                    store(i - 1, (i + 3) % 4)
                for k in range(4):
                    sp.wait_ge(came[k], 16 * (ROUNDS + 1))
                for k in range(2):
                    sp.wait_ge(y_left[k], 16 * (T1 // 2))

            @block.scalar
            def _(act):
                def spread_x(i, k, first=False):
                    if not first:
                        act.wait_ge(h_product, i - 1)
                    act.wait_ge(x_turned, i + 1)
                    for c in range(DC):
                        last = nc.scalar.activation(xt[:, k, c * P:(c + 1) * P], px[:, c * P:(c + 1) * P],
                                                    ACT.Identity, bias=beta[:, c:c + 1], scale=gamma[:, c:c + 1])
                    last.then_inc(xt_ready, 1)

                def gelu(i, k, first=False):
                    if not first:
                        act.wait_ge(h_turned, i - 1)
                    act.wait_ge(raw_ready, i + 1)
                    nc.scalar.activation(hidden[:, k, :], raw[:, k, :], ACT.Gelu).then_inc(hidden_ready, 1)

                def step(i, k, first=False, more=2):
                    if more > 0:
                        gelu(i + 1, 1 - k, first and i == 0)
                    if not first or i > 1:
                        act.wait_ge(y_product, i - 1)
                    act.wait_ge(h_turned, i + 1)
                    nc.scalar.copy(hidden_t[:, k, :], pt[:, k, :]).then_inc(hidden_t_ready, 1)
                    if more > 1:
                        spread_x(i + 2, k)

                spread_x(0, 0, True)
                spread_x(1, 1, True)
                gelu(0, 0, True)
                for i in range(4):
                    step(i, i % 2, first=True)
                with act.Fori(1, ROUNDS) as s:
                    for k in range(4):
                        step(s * 4 + k, k % 2)
                step(T1 - 2, 0, more=1)
                step(T1 - 1, 1, more=0)

            @block.vector
            def _(dve):
                dve.wait_ge(loaded, 16 * (2 * EX + 2))

                def add_b1(i, k, first=False):
                    e, = load_experts(nc, expert_of, i, mybir.EngineType.DVE)
                    if not first:
                        dve.wait_ge(hidden_ready, i - 1)
                    dve.wait_ge(h_product, i + 1)
                    nc.vector.tensor_tensor(raw[:, k, :], ph[:, k, :], b1_sb[:, bass.ds(e, 1), :].rearrange("p a n -> p (a n)"),
                                            ALU.add).then_inc(raw_ready, 1)

                def add_b2(i, k, left=None):
                    e, = load_experts(nc, expert_of, i, mybir.EngineType.DVE)
                    if left is not None:
                        dve.wait_ge(y_left[k], left * 16)
                    dve.wait_ge(y_product, i + 1)
                    nc.vector.tensor_tensor(y[:, k, :], py[:, k, 0:D], b2_sb[:, bass.ds(e, 1), :].rearrange("p a n -> p (a n)"),
                                            ALU.add).then_inc(y_ready, 1)

                add_b1(0, 0, True)
                for i in range(4):
                    add_b1(i + 1, (i + 1) % 2, i == 0)
                    if i > 0:
                        add_b2(i - 1, (i - 1) % 2, (i - 1) // 2 or None)
                with dve.Fori(1, ROUNDS) as s:
                    for k in range(4):
                        add_b1(s * 4 + k + 1, (k + 1) % 2)
                        add_b2(s * 4 + k - 1, (k + 1) % 2, s * 2 + (k - 1) // 2)
                add_b1(T1 - 1, 1)
                for i in range(T1 - 2, T1 + 1):
                    add_b2(i - 1, (i - 1) % 2, (i - 1) // 2)

            @block.tensor
            def _(pe):
                pe.wait_ge(loaded, 16 * (2 * EX + 2))

                def turn_rows(i, k, round_no):
                    if k or not isinstance(i, int) or i:
                        pe.wait_ge(xt_ready, i)
                    pe.wait_ge(came[k], round_no * 16 + 16)
                    for c in range(DC):
                        last = nc.tensor.transpose(px[:, c * P:(c + 1) * P], rows[:, k, c * P:(c + 1) * P], ident[:])
                    last.then_inc(x_turned, 1)

                def front(i, k, first=False):
                    e, = load_experts(nc, expert_of, i, mybir.EngineType.PE)
                    if not first:
                        pe.wait_ge(raw_ready, i - 1)
                    pe.wait_ge(xt_ready, i + 1)
                    for c in range(DC):
                        last = nc.tensor.matmul(ph[:, k, :], xt[:, k, c * P:(c + 1) * P],
                                                w1_sb[:, bass.ds(e, 1), c, :].rearrange("p a h -> p (a h)"),
                                                start=(c == 0), stop=(c == DC - 1))
                    last.then_inc(h_product, 1)

                def turn_hidden(i, k, first=False):
                    if not first:
                        pe.wait_ge(hidden_t_ready, i - 1)
                    pe.wait_ge(hidden_ready, i + 1)
                    for hc in range(HC):
                        last = nc.tensor.transpose(pt[:, k, hc * P:(hc + 1) * P], hidden[:, k, hc * P:(hc + 1) * P], ident[:])
                    last.then_inc(h_turned, 1)

                def back(i, k, first=False):
                    e, = load_experts(nc, expert_of, i, mybir.EngineType.PE)
                    if not first:
                        pe.wait_ge(y_ready, i - 1)
                    pe.wait_ge(hidden_t_ready, i + 1)
                    for hc in range(HC):
                        last = nc.tensor.matmul(py[:, k, 0:D], hidden_t[:, k, hc * P:(hc + 1) * P],
                                                w2_sb[:, bass.ds(e, 1), hc, :].rearrange("p a d -> p (a d)"),
                                                start=(hc == 0), stop=(hc == HC - 1))
                    last.then_inc(y_product, 1)

                turn_rows(0, 0, 0)
                front(0, 0, True)
                turn_rows(1, 1, 0)
                for i in range(4):
                    front(i + 1, (i + 1) % 2, i == 0)
                    turn_hidden(i, i % 2, i < 2)
                    turn_rows(i + 2, (i + 2) % 4, (i + 2) // 4)
                    if i > 0:
                        back(i - 1, (i - 1) % 2, i < 3)
                with pe.Fori(1, ROUNDS) as s:
                    for k in range(4):
                        i = s * 4 + k
                        front(i + 1, (k + 1) % 2)
                        turn_hidden(i, k % 2)
                        turn_rows(i + 2, (k + 2) % 4, s + (k + 2) // 4)
                        back(i - 1, (k + 1) % 2)
                front(T1 - 1, 1)
                turn_hidden(T1 - 2, 0)
                back(T1 - 3, 1)
                turn_hidden(T1 - 1, 1)
                back(T1 - 2, 0)
                back(T1 - 1, 1)


def load_experts(nc, expert_of, tile, engine, many=1):
    _, values = nc.values_load_multi_w_load_instructions(
        expert_of[0:1, bass.ds(tile, many)], engines=[engine], min_val=0, max_val=EX - 1,
        skip_runtime_bounds_check_because="slots caps the experts' numbers at EX - 1")
    return values


def gate_and_values(nc, st, xt, w1, b1, w2, b2, gcn_w, h_dram, ident, gate, h):
    R = w1.shape[1]
    assert R == P
    with ExitStack() as ctx:
        def sb(name, shape, dt=F32):
            return ctx.enter_context(nc.sbuf_tensor(f"ga_{name}", shape, dt))

        w1_sb, w2_sb, gw = sb("w1", [P, DC, R]), sb("w2", [R, D]), sb("gw", [P, DC])
        b1_sb, b2_sb = sb("b1", [P, 1]), sb("b2", [P, DC])
        total = sb("total", [P, DC])
        squeezed = sb("squeezed", [P, 1])
        gate_t = sb("gate_t", [P, DC])
        h_line = sb("h_line", [1, 2, 2 * P])
        h_rows = sb("h_rows", [NB, P])
        ph = ctx.enter_context(nc.psum_tensor("ga_ph", [1, 2, 512], F32))
        pg = ctx.enter_context(nc.psum_tensor("ga_pg", [P, 3, 512], F32))
        loaded = st.sem("ga_loaded")
        product = st.sem("ga_product")
        line_ready = st.sem("ga_line_ready")
        line_stored = [st.sem(f"ga_line_stored{k}") for k in range(2)]
        h_loaded = st.sem("ga_h_loaded")
        chain = st.sem("ga_chain")
        mean_ready = st.sem("ga_mean_ready")
        gate_psum = st.sem("ga_gate_psum")
        gate_step = st.sem("ga_gate_step")
        h_flat = h_dram.rearrange("n a -> (n a)")
        with nc.Block() as block:
            @block.sync
            def _(sp):
                sp.dma_start(w1_sb[:], w1.rearrange("(c p) r -> p c r", p=P)).then_inc(loaded, 16)
                sp.dma_start(w2_sb[:], w2).then_inc(loaded, 16)
                sp.dma_start(gw[:], gcn_w.rearrange("(c p) a -> p (c a)", p=P), allow_slow_non_contiguous=True).then_inc(loaded, 16)
                sp.dma_start(b1_sb[:], b1.rearrange("(p a) -> p a", a=1)).then_inc(loaded, 16)
                sp.dma_start(b2_sb[:], b2.rearrange("(c p) -> p c", p=P), allow_slow_non_contiguous=True).then_inc(loaded, 16)
                with sp.Fori(0, NB // 2) as s:
                    sp.wait_ge(line_ready, s + 1)
                    sp.dma_start(h_flat[bass.ds(s * 2 * P, 2 * P)].rearrange("(a n) -> a n", a=1), h_line[:, 0, :]).then_inc(line_stored[0], 16)
                sp.wait_ge(line_stored[0], 16 * (NB // 2))
                sp.dma_start(h_rows[:], h_flat.rearrange("(b n) -> b n", b=NB)).then_inc(h_loaded, 16)

            @block.tensor
            def _(pe):
                pe.wait_ge(loaded, 80)
                with pe.Fori(0, NB // 2) as s:
                    pe.wait_ge(line_ready, s)
                    for c in range(DC):
                        last = nc.tensor.matmul(ph[:, 0, 0:2 * P], gw[:, c:c + 1], xt[:, c, bass.ds(s * 2 * P, 2 * P)],
                                                start=(c == 0), stop=(c == DC - 1))
                    last.then_inc(product, 1)
                pe.wait_ge(mean_ready, 1)
                for c in range(DC):
                    last = nc.tensor.matmul(pg[:, 0, 0:1], w1_sb[:, c, :], total[:, c:c + 1], start=(c == 0), stop=(c == DC - 1))
                last.then_inc(gate_psum, 1)
                pe.wait_ge(gate_step, 1)
                for c in range(DC):
                    last = nc.tensor.matmul(pg[:, 1, c:c + 1], w2_sb[:, c * P:(c + 1) * P], squeezed[:], start=True, stop=True)
                last.then_inc(gate_psum, 1)
                pe.wait_ge(gate_step, 2)
                for c in range(DC):
                    last = nc.tensor.matmul(pg[:, 2, c * P:(c + 1) * P], gate_t[:, c:c + 1].to_broadcast([P, P]), ident[:], start=True, stop=True)
                last.then_inc(gate_psum, 1)
                pe.wait_ge(h_loaded, 16)
                pe.wait_ge(gate_step, 3)
                nc.tensor.transpose(pg[:, 0, 0:NB], h_rows[:], ident[0:NB, 0:NB]).then_inc(gate_psum, 1)

            @block.scalar
            def _(act):
                with act.Fori(0, NB // 2) as s:
                    act.wait_ge(line_stored[0], s * 16)
                    act.wait_ge(product, s + 1)
                    nc.scalar.copy(h_line[:, 0, :], ph[:, 0, 0:2 * P]).then_inc(line_ready, 1)
                act.wait_ge(loaded, 80)
                act.wait_ge(gate_psum, 1)
                nc.scalar.activation(squeezed[:], pg[:, 0, 0:1], ACT.Relu, bias=b1_sb[:, 0:1]).then_inc(gate_step, 1)
                act.wait_ge(gate_psum, 2)
                for c in range(DC):
                    last = nc.scalar.activation(gate_t[:, c:c + 1], pg[:, 1, c:c + 1], ACT.Sigmoid, bias=b2_sb[:, c:c + 1])
                last.then_inc(gate_step, 1)

            @block.vector
            def _(dve):
                link = chained(dve, chain)
                link(nc.vector.tensor_reduce(total[:], xt[:, :, 0:N], AX.X, ALU.add))
                nc.vector.tensor_scalar(total[:], total[:], 1.0 / N, None, ALU.mult).then_inc(mean_ready, 1)
                dve.wait_ge(gate_psum, 3)
                nc.vector.tensor_scalar(gate[:], pg[:, 2, 0:D], 1.0, None, ALU.add).then_inc(gate_step, 1)
                dve.wait_ge(gate_psum, 4)
                link(nc.vector.tensor_copy(h[:], pg[:, 0, 0:NB]))


def graph_values(nc, st, h, degree, dis, g, g_dram, ident):
    with ExitStack() as ctx:
        g_rows = ctx.enter_context(nc.sbuf_tensor("gv_rows", [NB, P], F32))
        root = ctx.enter_context(nc.sbuf_tensor("gv_root", [P, NB], F32))
        pt = ctx.enter_context(nc.psum_tensor("gv_pt", [P, 512], F32))
        chain = st.sem("gv_chain")
        more = st.sem("gv_more")
        rooted = st.sem("gv_rooted")
        g_ready = st.sem("gv_g_ready")
        turned = st.sem("gv_turned")
        rows_ready = st.sem("gv_rows_ready")
        stored = st.sem("gv_stored")
        with nc.Block() as block:
            @block.vector
            def _(dve):
                nc.vector.tensor_scalar(dis[:], degree[:], 1.0, None, ALU.add).then_inc(more, 1)
                dve.wait_ge(rooted, 1)
                link = chained(dve, chain)
                link(nc.vector.reciprocal(dis[:], root[:]))
                nc.vector.tensor_tensor(g[:], h[:], dis[:], ALU.mult).then_inc(g_ready, 1)
                dve.wait_ge(turned, 1)
                nc.vector.tensor_copy(g_rows[:], pt[0:NB, 0:P]).then_inc(rows_ready, 1)

            @block.scalar
            def _(act):
                act.wait_ge(more, 1)
                nc.scalar.activation(root[:], dis[:], ACT.Sqrt).then_inc(rooted, 1)

            @block.tensor
            def _(pe):
                pe.wait_ge(g_ready, 1)
                nc.tensor.transpose(pt[0:NB, 0:P], g[:], ident[:]).then_inc(turned, 1)

            @block.sync
            def _(sp):
                sp.wait_ge(rows_ready, 1)
                sp.dma_start(g_dram.rearrange("(b n) a -> b (n a)", b=NB), g_rows[:]).then_inc(stored, 16)
                sp.wait_ge(stored, 16)


def aggregate_values(nc, st, g_dram, rel, col, item_block, iota_free, acc):
    with ExitStack() as ctx:
        def sb(name, shape, dt=F32):
            return ctx.enter_context(nc.sbuf_tensor(f"av_{name}", shape, dt))

        got = sb("got", [P, RING, QUAD])
        index = sb("index", [P, RING, QUAD], I32)
        hot = sb("hot", [P, 2, QUAD, P])
        sums = ctx.enter_context(nc.psum_tensor("av_sums", [P, 2, 512], F32))
        gathered = [st.sem(f"av_gathered{k}") for k in range(RING * QUAD)]
        index_ready = st.sem("av_index_ready")
        hot_ready = st.sem("av_hot_ready")
        summed = st.sem("av_summed")
        added = st.sem("av_added")
        QUADS = NI // QUAD
        with nc.Block() as block:
            @block.gpsimd
            def _(pool):
                nc.gpsimd.memset(col[:, NI:NI + QUAD], 0).then_inc(index_ready, 1)
                nc.gpsimd.tensor_copy(index[:, 0, :], col[:, 0:QUAD]).then_inc(index_ready, 1)
                with pool.Fori(0, QUADS // RING) as s:
                    for u in range(RING):
                        q = s * RING + u
                        pool.wait_ge(summed, q + 1)
                        pool.wait_ge(index_ready, q + 2)
                        nc.gpsimd.tensor_copy(index[:, (u + 1) % RING, :],
                                              col[:, bass.ds((q + 1) * QUAD, QUAD)]).then_inc(index_ready, 1)
                        for j in range(QUAD):
                            nc.gpsimd.indirect_dma_start(
                                got[:, u, j:j + 1], None, g_dram,
                                bass.IndirectOffsetOnAxis(ap=index[:, u, j:j + 1], axis=0)).then_inc(gathered[u * QUAD + j], 16)

            @block.tensor
            def _(pe):
                pe.sem_inc(summed, 3)
                with pe.Fori(0, QUADS // RING) as s:
                    for v in range(RING):
                        q, u = s * RING + v, v % 2
                        pe.wait_ge(added, q * 4 + 4)
                        pe.wait_ge(hot_ready, q + 1)
                        for j in range(QUAD):
                            pe.wait_ge(gathered[v * QUAD + j], s * 16 + 16)
                        for j in range(QUAD):
                            last = nc.tensor.matmul(sums[:, u, j:j + 1], hot[:, u, j, :], got[:, v, j:j + 1], start=True, stop=True)
                        last.then_inc(summed, 1)

            @block.vector
            def _(dve):
                def one_hots(q, u):
                    for j in range(QUAD):
                        last = nc.vector.tensor_scalar(hot[:, u, j, :], iota_free[:], rel[:, bass.ds(q * QUAD + j, 1)], None, ALU.is_equal)
                    last.then_inc(hot_ready, 1)

                nc.vector.memset(rel[:, NI:NI + QUAD], float(P)).then_inc(added, 4)
                nc.vector.memset(acc[:], 0.0).then_inc(added, 4)
                dve.wait_ge(added, 8)
                one_hots(0, 0)
                with dve.Fori(0, QUADS // 2) as s:
                    for u in range(2):
                        q = s * 2 + u
                        dve.wait_ge(summed, q + 3)
                        one_hots(q + 1, 1 - u)
                        blk = load_blocks(nc, item_block, q, mybir.EngineType.DVE)
                        dve.wait_ge(summed, q + 4)
                        for j in range(QUAD):
                            dve.wait_ge(added, q * 4 + j + 8)
                            to = acc[:, bass.ds(blk[j], 1)]
                            nc.vector.tensor_tensor(to, to, sums[:, u, j:j + 1], ALU.add).then_inc(added, 1)


def gated_update(nc, st, x, mean, rstd, dis, g, sums, gcn_b, gate):
    with ExitStack() as ctx:
        def sb(name, shape, dt=F32):
            return ctx.enter_context(nc.sbuf_tensor(f"gu_{name}", shape, dt))

        bias = sb("bias", [P, 1])
        pre = sb("pre", [P, NB])
        spatial = sb("spatial", [P, NB])
        rows = sb("rows", [P, 2, D])
        factor = sb("factor", [P, 2, D])
        loaded = st.sem("gu_loaded")
        chain = st.sem("gu_chain")
        pre_ready = st.sem("gu_pre_ready")
        spatial_ready = st.sem("gu_spatial_ready")
        factor_ready = st.sem("gu_factor_ready")
        step = st.sem("gu_step")
        with nc.Block() as block:
            @block.sync
            def _(sp):
                sp.dma_start(bias[:], gcn_b.rearrange("(a n) -> a n", a=1).to_broadcast([P, 1])).then_inc(loaded, 16)

            @block.scalar
            def _(act):
                act.wait_ge(loaded, 16)
                act.wait_ge(pre_ready, 1)
                nc.scalar.activation(spatial[:], pre[:], ACT.Sigmoid, bias=bias[:, 0:1]).then_inc(spatial_ready, 1)
                act.wait_ge(spatial_ready, 1)
                with act.Fori(0, NB // 2) as h:
                    for k in range(2):
                        b = h * 2 + k
                        act.wait_ge(step, h * 6)
                        nc.scalar.activation(factor[:, k, :], gate[:], ACT.Identity, bias=spatial[:, bass.ds(b, 1)]).then_inc(factor_ready, 1)

            @block.vector
            def _(dve):
                link = chained(dve, chain)
                link(nc.vector.tensor_tensor(pre[:], sums[:], g[:], ALU.add))
                nc.vector.tensor_tensor(pre[:], pre[:], dis[:], ALU.mult).then_inc(pre_ready, 1)
                with dve.Fori(0, NB // 2) as h:
                    for k in range(2):
                        b = h * 2 + k
                        of = x[:, bass.ds(b, 1), :].rearrange("p a d -> p (a d)")
                        nc.vector.tensor_scalar(rows[:, k, :], of, mean[:, bass.ds(b, 1)], rstd[:, bass.ds(b, 1)],
                                                ALU.subtract, ALU.mult).then_inc(step, 1)
                        dve.wait_ge(factor_ready, b + 1)
                        dve.wait_ge(step, b * 3 + 1)
                        nc.vector.tensor_tensor(rows[:, k, :], rows[:, k, :], factor[:, k, :], ALU.mult).then_inc(step, 1)
                        dve.wait_ge(step, b * 3 + 2)
                        nc.vector.tensor_tensor(of, of, rows[:, k, :], ALU.add).then_inc(step, 1)


def route_one(nc, st, xt, w1_sb, b1_sb, wg, bg, order, ones, pick, share):
    HC = b1_sb.shape[1]
    with ExitStack() as ctx:
        def sb(name, shape, dt=F32):
            return ctx.enter_context(nc.sbuf_tensor(f"r1_{name}", shape, dt))

        wg_sb = sb("wg", [P, HC, EX])
        bg_sb = sb("bg", [1, EX])
        hidden = sb("hidden", [P, HC, 2 * P])
        logits = sb("logits", [P, NB, EX])
        best = sb("best", [P, NB])
        tmp = sb("tmp", [P, NB])
        ph = ctx.enter_context(nc.psum_tensor("r1_ph", [P, 2, 512], F32))
        ps = ctx.enter_context(nc.psum_tensor("r1_ps", [P, 2, 2, 512], F32))
        loaded = st.sem("r1_loaded")
        h_product = st.sem("r1_h_product")
        h_ready = st.sem("r1_h_ready")
        h_used = st.sem("r1_h_used")
        logit_product = st.sem("r1_logit_product")
        logits_out = st.sem("r1_logits_out")
        chain = st.sem("r1_chain")
        shift_ready = st.sem("r1_shift_ready")
        exps_ready = st.sem("r1_exps_ready")
        PAIRS = NB // 2
        with nc.Block() as block:
            @block.sync
            def _(sp):
                sp.dma_start(wg_sb[:], wg.rearrange("(c p) e -> p c e", p=P)).then_inc(loaded, 16)
                sp.dma_start(bg_sb[:], bg.rearrange("(a e) -> a e", a=1)).then_inc(loaded, 16)

            @block.tensor
            def _(pe):
                pe.sem_inc(h_used, HC)
                pe.wait_ge(loaded, 32)

                def step(s, u):
                    def logit_part(hc):
                        pe.wait_ge(h_ready, s * HC + hc + 3)
                        for k in range(2):
                            last = nc.tensor.matmul(ps[:, u, k, 0:EX], hidden[:, hc, k * P:(k + 1) * P], wg_sb[:, hc, :],
                                                    start=False, stop=(hc == HC - 1))
                        last.then_inc(h_used, 1)
                        return last

                    pe.wait_ge(logits_out, s + 1)
                    for k in range(2):
                        nc.tensor.matmul(ps[:, u, k, 0:EX], ones[0:1, :], bg_sb[:], start=True, stop=False)
                    for hc in range(HC):
                        pe.wait_ge(h_ready, s * HC + hc + 1)
                        for c in range(DC):
                            last = nc.tensor.matmul(ph[:, hc % 2, 0:2 * P], w1_sb[:, c, hc * P:(hc + 1) * P],
                                                    xt[:, c, bass.ds(s * 2 * P, 2 * P)], start=(c == 0), stop=(c == DC - 1))
                        last.then_inc(h_product, 1)
                        if hc:
                            logit_part(hc - 1)
                    logit_part(HC - 1)

                with pe.Fori(0, PAIRS // 2) as v:
                    for u in range(2):
                        step(v * 2 + u, u)
                step(PAIRS - 1, 0)

            @block.scalar
            def _(act):
                act.sem_inc(h_ready, 2)
                with act.Fori(0, PAIRS) as s:
                    for hc in range(HC):
                        act.wait_ge(h_used, s * HC + hc + 1)
                        act.wait_ge(h_product, s * HC + hc + 1)
                        nc.scalar.activation(hidden[:, hc, :], ph[:, hc % 2, 0:2 * P], ACT.Gelu, bias=b1_sb[:, hc:hc + 1]).then_inc(h_ready, 1)
                act.wait_ge(shift_ready, 1)
                nc.scalar.activation(logits[:], logits[:], ACT.Exp).then_inc(exps_ready, 1)

            @block.vector
            def _(dve):
                dve.sem_inc(logits_out, 2)

                def out(s, u):
                    dve.wait_ge(h_used, s * HC + 2 * HC)
                    nc.vector.tensor_copy(logits[:, bass.ds(s * 2, 2), :], ps[:, u, :, 0:EX]).then_inc(logits_out, 1)

                with dve.Fori(0, PAIRS // 2) as v:
                    for u in range(2):
                        out(v * 2 + u, u)
                out(PAIRS - 1, 0)
                dve.wait_ge(logits_out, PAIRS + 2)
                link = chained(dve, chain)
                shape = [P, NB, EX]
                order_b = order[:].unsqueeze(1).to_broadcast(shape)
                link(nc.vector.tensor_reduce(best[:], logits[:], AX.X, ALU.max))
                nc.vector.tensor_tensor(logits[:], logits[:], best[:].unsqueeze(2).to_broadcast(shape), ALU.subtract).then_inc(shift_ready, 1)
                dve.wait_ge(exps_ready, 1)
                first_largest(nc, link, logits[:], pick[:], best[:], tmp[:], order_b, shape)
                link(nc.vector.tensor_reduce(tmp[:], logits[:], AX.X, ALU.add))
                link(nc.vector.reciprocal(share[:], tmp[:]))
                link(nc.vector.tensor_tensor(share[:], share[:], best[:], ALU.mult))


def routed_tiles(nc, st, rows_dram, y_dram, expert_of, w1_sb, b1_sb, wd, bd, ident):
    HC = b1_sb.shape[1]
    STEPS = T2 // 2
    assert STEPS % 2 == 0
    with ExitStack() as ctx:
        def sb(name, shape, dt=F32):
            return ctx.enter_context(nc.sbuf_tensor(f"rt_{name}", shape, dt))

        wd_sb = sb("wd", [P, EX, HC, D])
        bd_sb = sb("bd", [P, EX, D])
        rows = sb("rows", [P, 2, 2, D])
        xt = sb("xt", [P, 2, DC, 2 * P])
        hidden = sb("hidden", [P, HC, 2 * P])
        y = sb("y", [P, 2, 2, D])
        px = ctx.enter_context(nc.psum_tensor("rt_px", [P, DC, 2 * P], F32))
        ph = ctx.enter_context(nc.psum_tensor("rt_ph", [P, 2, 512], F32))
        py = ctx.enter_context(nc.psum_tensor("rt_py", [P, 2, 2, 512], F32))
        loaded = st.sem("rt_loaded")
        came = [st.sem(f"rt_came{u}") for u in range(2)]
        turned = st.sem("rt_turned")
        xt_ready = st.sem("rt_xt_ready")
        h_product = st.sem("rt_h_product")
        h_ready = st.sem("rt_h_ready")
        h_used = st.sem("rt_h_used")
        y_ready = st.sem("rt_y_ready")
        y_left = [st.sem(f"rt_y_left{u}") for u in range(2)]
        tiles = rows_dram.rearrange("(t p) d -> p t d", p=P)
        y_tiles = y_dram.rearrange("(t p) d -> p t d", p=P)
        with nc.Block() as block:
            @block.sync
            def _(sp):
                for e in range(EX):
                    sp.dma_start(wd_sb[:, e, :, :], wd[e].rearrange("(c p) d -> p c d", p=P)).then_inc(loaded, 16)
                bias_rows(sp, bd_sb[:].rearrange("p e n -> p (e n)"), bd, loaded)

                def fetch(s, u):
                    sp.dma_start(rows[:, u, :, :], tiles[:, bass.ds(s * 2, 2), :]).then_inc(came[u], 16)

                def step(s, u, more=True):
                    if more:
                        sp.wait_ge(turned, s + 1)
                        fetch(s + 2, u)
                    sp.wait_ge(y_ready, s * 2 + 6)
                    sp.dma_start(y_tiles[:, bass.ds(s * 2, 2), :], y[:, u, :, :]).then_inc(y_left[u], 16)

                for u in range(2):
                    fetch(u, u)
                with sp.Fori(0, STEPS // 2 - 1) as v:
                    for u in range(2):
                        step(v * 2 + u, u)
                for u in range(2):
                    step(STEPS - 2 + u, u, more=False)
                for u in range(2):
                    sp.wait_ge(y_left[u], 16 * (STEPS // 2))

            @block.tensor
            def _(pe):
                pe.sem_inc(h_used, HC)
                pe.wait_ge(loaded, 16 * (EX + 1))

                def turn_rows(s, u, v, first=False):
                    if not first:
                        pe.wait_ge(xt_ready, s)
                    pe.wait_ge(came[u], v * 16 + 16)
                    for c in range(DC):
                        for k in range(2):
                            last = nc.tensor.transpose(px[:, c, k * P:(k + 1) * P], rows[:, u, k, c * P:(c + 1) * P], ident[:])
                    last.then_inc(turned, 1)

                def step(s, u, v, more=True):
                    experts = load_experts(nc, expert_of, s * 2, mybir.EngineType.PE, many=2)

                    def y_part(hc):
                        pe.wait_ge(h_ready, s * HC + hc + 3)
                        for k in range(2):
                            last = nc.tensor.matmul(py[:, u, k, 0:D], hidden[:, hc, k * P:(k + 1) * P],
                                                    wd_sb[:, bass.ds(experts[k], 1), hc, :].rearrange("p a d -> p (a d)"),
                                                    start=(hc == 0), stop=(hc == HC - 1))
                        last.then_inc(h_used, 1)

                    pe.wait_ge(xt_ready, s + 1)
                    pe.wait_ge(y_ready, s * 2 + 2)
                    for hc in range(HC):
                        pe.wait_ge(h_ready, s * HC + hc + 1)
                        for c in range(DC):
                            last = nc.tensor.matmul(ph[:, hc % 2, 0:2 * P], w1_sb[:, c, hc * P:(hc + 1) * P],
                                                    xt[:, u, c, :], start=(c == 0), stop=(c == DC - 1))
                        last.then_inc(h_product, 1)
                        if hc:
                            y_part(hc - 1)
                        if more and hc == HC // 2:
                            turn_rows(s + 1, 1 - u, v + u)
                    y_part(HC - 1)

                turn_rows(0, 0, 0, first=True)
                with pe.Fori(0, STEPS // 2 - 1) as v:
                    for u in range(2):
                        step(v * 2 + u, u, v)
                step(STEPS - 2, 0, STEPS // 2 - 1)
                step(STEPS - 1, 1, STEPS // 2 - 1, more=False)

            @block.scalar
            def _(act):
                act.sem_inc(h_ready, 2)
                with act.Fori(0, STEPS) as s:
                    for hc in range(HC):
                        act.wait_ge(h_used, s * HC + hc + 1)
                        act.wait_ge(h_product, s * HC + hc + 1)
                        nc.scalar.activation(hidden[:, hc, :], ph[:, hc % 2, 0:2 * P], ACT.Gelu, bias=b1_sb[:, hc:hc + 1]).then_inc(h_ready, 1)

            @block.vector
            def _(dve):
                dve.sem_inc(y_ready, 4)
                dve.wait_ge(loaded, 16 * (EX + 1))

                def copy_xt(s, u, first=False):
                    if not first:
                        dve.wait_ge(h_product, s * HC - HC)
                    dve.wait_ge(turned, s + 1)
                    nc.vector.tensor_copy(xt[:, u, :, :], px[:]).then_inc(xt_ready, 1)

                def step(s, u, v=None, first=False, more=True):
                    if more:
                        copy_xt(s + 1, 1 - u, first and s == 0)
                    experts = load_experts(nc, expert_of, s * 2, mybir.EngineType.DVE, many=2)
                    if not first:
                        dve.wait_ge(y_left[u], v * 16)
                    dve.wait_ge(h_used, s * HC + 2 * HC)
                    for k in range(2):
                        nc.vector.tensor_tensor(y[:, u, k, :], py[:, u, k, 0:D],
                                                bd_sb[:, bass.ds(experts[k], 1), :].rearrange("p a d -> p (a d)"),
                                                ALU.add).then_inc(y_ready, 1)

                copy_xt(0, 0, first=True)
                for u in range(2):
                    step(u, u, first=True)
                with dve.Fori(1, STEPS // 2 - 1) as v:
                    for u in range(2):
                        step(v * 2 + u, u, v)
                step(STEPS - 2, 0, STEPS // 2 - 1)
                step(STEPS - 1, 1, STEPS // 2 - 1, more=False)


def move(nc, st, name, pairs):
    moved = st.sem(f"{name}_moved")
    with nc.Block() as block:
        @block.sync
        def _(sp):
            for to, of in pairs:
                sp.dma_start(to, of).then_inc(moved, 16)
            sp.wait_ge(moved, 16 * len(pairs))


def load_columns(nc, st, name, pairs):
    moved = st.sem(f"{name}_moved")
    with nc.Block() as block:
        @block.sync
        def _(sp):
            for to, of in pairs:
                sp.dma_start(to, of.rearrange("(c p) -> p c", p=P), allow_slow_non_contiguous=True).then_inc(moved, 16)
            sp.wait_ge(moved, 16 * len(pairs))


def build(nc, a, out):
    st = Stage(nc)
    keep = st.keep

    def dram(name, shape, dt=F32):
        return nc.dram_tensor(name, shape, dt, kind="Internal").ap()

    k_dram, v_dram = dram("k_table", (NB * P, D)), dram("v_table", (NB * P, D))
    scratch = {"rows": dram("edge_rows", (ET, P), I32), "cols": dram("edge_cols", (ET, P), I32),
               "item_block": dram("item_block", (NI,), I32), "keys": dram("item_keys", (NI, P), I16)}
    rel_dram, col_dram = dram("item_rel", (P, NI)), dram("item_col", (P, NI), I32)
    bounce = [dram(f"bounce{n}", (P, 1)) for n in range(2)]
    h_dram, g_dram = dram("h_values", (NB * P, 1)), dram("g_values", (NB * P, 1))

    def sb(ctx, name, shape, dt=F32):
        return ctx.enter_context(nc.sbuf_tensor(name, shape, dt))

    ident, before = sb(keep, "ident", [P, P]), sb(keep, "before", [P, P])
    iota_free, iota_part = sb(keep, "iota_free", [P, P]), sb(keep, "iota_part", [P, 1])
    ones, order = sb(keep, "ones", [P, P]), sb(keep, "order", [P, EX])
    stats, tmp = sb(keep, "stats", [P, NB, 6]), sb(keep, "ln_tmp", [P, NB])
    mean, rstd = sb(keep, "mean", [P, NB]), sb(keep, "rstd", [P, NB])
    mean2, rstd2 = sb(keep, "mean2", [P, NB]), sb(keep, "rstd2", [P, NB])
    degree = sb(keep, "degree", [P, NB])
    constants(nc, st, ident, before, iota_free, iota_part, ones, order)

    with ExitStack() as ctx:
        rel, col = sb(ctx, "rel", [P, NI + QUAD]), sb(ctx, "col", [P, NI + QUAD], I32)
        item_block = sb(ctx, "item_block_sb", [1, NI], I32)
        item_tables(nc, st, a["dst"], a["src"], scratch, ident, ones, rel, col)
        move(nc, st, "items", [(item_block[:], scratch["item_block"].rearrange("(a i) -> a i", a=1)),
                               (rel_dram, rel[:, 0:NI]), (col_dram, col[:, 0:NI])])
        scores = sb(ctx, "scores", [P, NI, HEADS])
        with ExitStack() as queries:
            q_all = sb(queries, "q_all", [P, NB, D])
            with ExitStack() as nodes:
                x = sb(nodes, "x_first", [P, NB, D])
                load_x(nc, st, "x_first", a["x"], x)
                layernorm_stats(nc, st, "ln_attention", x, stats, mean, rstd, tmp)
                project_qkv(nc, st, x, mean, rstd, ident, ones, [a[f"L0_gnn_W{n}"] for n in "qkv"],
                            [a[f"L0_gnn_b{n}"] for n in "qkv"], q_all, (k_dram, v_dram))
            edge_scores(nc, st, q_all, k_dram, rel, col, item_block, iota_free, ident, scores)
        softmax_over_rows(nc, st, scores, scratch["keys"], bounce, ident)
        acc = sb(ctx, "acc", [P, NB, AW])
        aggregate(nc, st, scores, v_dram, rel, col, item_block, iota_free, acc)
        copied = st.sem("degree_copied")
        with nc.Block() as block:
            @block.vector
            def _(dve):
                nc.vector.tensor_copy(degree[:], acc[:, :, AW - 1]).then_inc(copied, 1)
        x = sb(ctx, "x_second", [P, NB, D])
        load_x(nc, st, "x_second", a["x"], x)
        attention_output(nc, st, acc, x, a["L0_gnn_Wo"], a["L0_gnn_bo"], ident, ones)
        x_dram = dram("x_between", (P, NB, D))
        move(nc, st, "x_out", [(x_dram, x[:])])
    st.hand_back()

    with ExitStack() as ctx:
        x = sb(ctx, "x", [P, NB, D])
        move(nc, st, "x_in", [(x[:], x_dram)])

        rows_dram, y_dram = dram("mixture_rows", ((T1 + 2) * P, D)), dram("mixture_y", (T1 * P, D))
        with ExitStack() as ffn:
            share = [sb(ffn, f"share{k}", [P, NB]) for k in range(2)]
            scatter = [sb(ffn, f"scatter{k}", [P, NB], I32) for k in range(2)]
            gather = [sb(ffn, f"gather{k}", [P, NB], I32) for k in range(2)]
            expert_of = sb(ffn, "expert_of", [1, T1], I32)
            gamma, beta = sb(ffn, "gamma", [P, DC]), sb(ffn, "beta", [P, DC])
            load_columns(nc, st, "affine", [(gamma[:], a["L0_ffn_gamma"]), (beta[:], a["L0_ffn_beta"])])
            clear_rows(nc, st, "mixture_clear", rows_dram)
            with ExitStack() as router:
                xt = sb(router, "xt_first", [P, DC, NB * P])
                line = sb(router, "ln_line", [P, D])
                pick = [sb(router, f"pick{k}", [P, NB, EX]) for k in range(2)]
                layernorm_stats(nc, st, "ln_outer", x, stats, mean, rstd, tmp)
                layernorm_stats(nc, st, "ln_inner", x, stats, mean2, rstd2, tmp, inner=(mean, rstd, line))
                affine = ((mean, rstd), (mean2, rstd2))
                turn(nc, st, "turn_first", x, affine, xt, ident, gamma, beta)
                route_two(nc, st, xt, a["L0_ffn_Wr"], a["L0_ffn_br"], order, ident, pick, share)
                slots(nc, st, "mixture_slots", pick, scatter, gather, expert_of, ones, iota_part, before, T1)
            scatter_rows(nc, st, "mixture_scatter", x, affine, scatter, rows_dram)
            mixture_tiles(nc, st, rows_dram, y_dram, expert_of, a["L0_ffn_W1"], a["L0_ffn_b1"], a["L0_ffn_W2"],
                          a["L0_ffn_b2"], gamma, beta, ident)
            gather_rows(nc, st, "mixture_gather", y_dram, gather, share, x)
        st.hand_back()

        with ExitStack() as gnn:
            gate = sb(gnn, "gate", [P, D])
            h, dis, g = sb(gnn, "h", [P, NB]), sb(gnn, "dis", [P, NB]), sb(gnn, "g", [P, NB])
            sums = sb(gnn, "neighbour_sums", [P, NB])
            layernorm_stats(nc, st, "ln_gates", x, stats, mean, rstd, tmp)
            with ExitStack() as turned:
                xt = sb(turned, "xt_second", [P, DC, NB * P])
                turn(nc, st, "turn_second", x, ((mean, rstd),), xt, ident)
                gate_and_values(nc, st, xt, a["L1_gnn_w1"], a["L1_gnn_b1"], a["L1_gnn_w2"], a["L1_gnn_b2"],
                                a["L1_gnn_gcn_w"], h_dram, ident, gate, h)
            graph_values(nc, st, h, degree, dis, g, g_dram, ident)
            with ExitStack() as edges:
                rel, col = sb(edges, "rel_again", [P, NI + QUAD]), sb(edges, "col_again", [P, NI + QUAD], I32)
                item_block = sb(edges, "item_block_again", [1, NI], I32)
                move(nc, st, "items_again", [(item_block[:], scratch["item_block"].rearrange("(a i) -> a i", a=1)),
                                             (rel[:, 0:NI], rel_dram), (col[:, 0:NI], col_dram)])
                aggregate_values(nc, st, g_dram, rel, col, item_block, iota_free, sums)
            gated_update(nc, st, x, mean, rstd, dis, g, sums, a["L1_gnn_gcn_b"], gate)

        st.hand_back()

        with ExitStack() as ffn:
            hidden_channels = a["L1_ffn_W1"].shape[1]
            rows_dram, y_dram = dram("routed_rows", ((T2 + 1) * P, D)), dram("routed_y", (T2 * P, D))
            share = sb(ffn, "routed_share", [P, NB])
            scatter, gather = sb(ffn, "routed_scatter", [P, NB], I32), sb(ffn, "routed_gather", [P, NB], I32)
            expert_of = sb(ffn, "routed_expert_of", [1, T2], I32)
            w1_sb, b1_sb = sb(ffn, "routed_w1", [P, DC, hidden_channels]), sb(ffn, "routed_b1", [P, hidden_channels // P])
            move(nc, st, "routed_w1", [(w1_sb[:], a["L1_ffn_W1"].rearrange("(c p) n -> p c n", p=P))])
            load_columns(nc, st, "routed_b1", [(b1_sb[:], a["L1_ffn_b1"])])
            clear_rows(nc, st, "routed_clear", rows_dram)
            layernorm_stats(nc, st, "ln_routed", x, stats, mean, rstd, tmp)
            affine = ((mean, rstd),)
            with ExitStack() as router:
                xt = sb(router, "xt_third", [P, DC, NB * P])
                pick = sb(router, "routed_pick", [P, NB, EX])
                turn(nc, st, "turn_third", x, affine, xt, ident)
                route_one(nc, st, xt, w1_sb, b1_sb, a["L1_ffn_Wg"], a["L1_ffn_bg"], order, ones, pick, share)
                slots(nc, st, "routed_slots", [pick], [scatter], [gather], expert_of, ones, iota_part, before, T2)
            scatter_rows(nc, st, "routed_scatter", x, affine, [scatter], rows_dram)
            routed_tiles(nc, st, rows_dram, y_dram, expert_of, w1_sb, b1_sb, a["L1_ffn_Wd"], a["L1_ffn_bd"], ident)
            gather_rows(nc, st, "routed_gather", y_dram, [gather], [share], x)
        move(nc, st, "result", [(out[0:FULL * P, :].rearrange("(b p) d -> p b d", p=P), x[:, 0:FULL, :]),
                                (out[FULL * P:N, :], x[0:TAIL, FULL, :])])
    keep.close()


def kernel(**inputs):
    import numpy as _np
    import concourse.bacc as _bacc
    from concourse.bass_utils import run_bass_kernel_spmd as _run

    nc = _bacc.Bacc("TRN2", target_bir_lowering=False, num_devices=1)
    arrays, aps = {}, {}
    for name, value in inputs.items():
        value = _np.ascontiguousarray(value)
        arrays[f"in_{name}"] = value
        aps[name] = nc.dram_tensor(f"in_{name}", value.shape, mybir.dt.from_np(value.dtype), kind="ExternalInput").ap()
    out = nc.dram_tensor("out", (N, D), F32, kind="ExternalOutput").ap()
    build(nc, aps, out)
    result = _run(nc, [arrays], core_ids=[0])
    return result.results[0]["out"]
```

```python
from contextlib import ExitStack

import concourse.bass as bass
from concourse import mybir

F32 = mybir.dt.float32
BF16 = mybir.dt.bfloat16
I32 = mybir.dt.int32
I16 = mybir.dt.int16
ALU = mybir.AluOpType
ACT = mybir.ActivationFunctionType
AX = mybir.AxisListType

P = 128
N = 6250
D = 256
DC = D // P
HEADS, HD = 8, 32
E = 206250
NB = 50
FULL = N // P
TAIL = N - FULL * P
ET = -(-E // P)
ETAIL = E - (ET - 1) * P
CH = 16
CI = 104
NI = CH * CI
IG = NI // P
assert NI >= ET + FULL + 1
PAD_ROW = 8192
RP = 125
RE = E // RP
assert RP * RE == E and RE <= NI
SL = 2048
KEY_EXPONENT = 0x30000000
assert P * SL >= ET * P
BIG = 1.0e38
CL = CI * P
EPS = 1e-5
EX = 8
UNROLL = 5
QUAD = 4
GROUP = 16
RING = 4
AW = D + HEADS + 1


class Stage:

    def __init__(self, nc):
        self.nc = nc
        self.keep = ExitStack()
        self.taken = []

    def sem(self, name):
        self.taken.append(self.nc.alloc_semaphore(name=name))
        return self.taken[-1]

    def hand_back(self):
        self.nc.all_engine_barrier()
        self.nc.clear_and_free_semaphores(self.taken)
        self.nc.all_engine_barrier()
        self.taken = []


def chained(engine, sem, start=0):
    count = [start]

    def link(instruction):
        count[0] += 1
        instruction.then_inc(sem, 1)
        engine.wait_ge(sem, count[0])

    return link


def constants(nc, st, ident, before, iota_free, iota_part, ones, zero, order):
    made = st.sem("const_made")
    with nc.Block() as block:
        @block.gpsimd
        def _(pool):
            link = chained(pool, made)
            link(nc.gpsimd.memset(ones[:], 1.0))
            link(nc.gpsimd.memset(zero[:], 0.0))
            link(nc.gpsimd.iota(iota_free[:], pattern=[[1, P]], base=0, channel_multiplier=0,
                                allow_small_or_imprecise_dtypes=True))
            link(nc.gpsimd.iota(iota_part[:], pattern=[[0, 1]], base=0, channel_multiplier=1,
                                allow_small_or_imprecise_dtypes=True))
            link(nc.gpsimd.tensor_scalar(ident[:], iota_free[:], iota_part[:, 0:1], None, ALU.is_equal))
            link(nc.gpsimd.tensor_scalar(before[:], iota_free[:], iota_part[:, 0:1], None, ALU.is_gt))
            link(nc.gpsimd.iota(order[:], pattern=[[-1, EX]], base=EX, channel_multiplier=0,
                                allow_small_or_imprecise_dtypes=True))


def layernorm_stats(nc, st, name, x, stats, mean, rstd, tmp, inner=None):
    inner_done = st.sem(f"{name}_inner_done")
    stat_done = st.sem(f"{name}_stat_done")
    chain = st.sem(f"{name}_chain")
    var_ready = st.sem(f"{name}_var_ready")
    root_ready = st.sem(f"{name}_root_ready")
    with nc.Block() as block:
        @block.vector
        def _(dve):
            dve.sem_inc(stat_done, UNROLL)
            def stats_of(b, of):
                nc.vector.bn_stats(stats[:, bass.ds(b, 1), :].rearrange("p a s -> p (a s)"), of).then_inc(stat_done, 1)

            with dve.Fori(0, NB // UNROLL) as h:
                rows = [x[:, bass.ds(h * UNROLL + k, 1), :].rearrange("p a d -> p (a d)") for k in range(UNROLL)]
                if inner:
                    for k in range(UNROLL):
                        b = h * UNROLL + k
                        dve.wait_ge(stat_done, b + 1)
                        nc.vector.tensor_scalar(inner[2][:, k, :], rows[k], inner[0][:, bass.ds(b, 1)],
                                                inner[1][:, bass.ds(b, 1)], ALU.subtract, ALU.mult).then_inc(inner_done, 1)
                        rows[k] = inner[2][:, k, :]
                for k in range(UNROLL):
                    b = h * UNROLL + k
                    if inner:
                        dve.wait_ge(inner_done, b + 1)
                    stats_of(b, rows[k])
            dve.wait_ge(stat_done, NB + UNROLL)
            link = chained(dve, chain)
            link(nc.vector.tensor_tensor(mean[:], stats[:, :, 1], stats[:, :, 4], ALU.add))
            link(nc.vector.tensor_scalar(mean[:], mean[:], 0.5, None, ALU.mult))
            link(nc.vector.tensor_tensor(tmp[:], stats[:, :, 1], stats[:, :, 4], ALU.subtract))
            link(nc.vector.tensor_tensor(tmp[:], tmp[:], tmp[:], ALU.mult))
            link(nc.vector.tensor_tensor(rstd[:], stats[:, :, 2], stats[:, :, 5], ALU.add))
            link(nc.vector.tensor_scalar(rstd[:], rstd[:], 1.0 / D, EPS, ALU.mult, ALU.add))
            link(nc.vector.scalar_tensor_tensor(out=rstd[:], in0=tmp[:], scalar=0.25, in1=rstd[:],
                                                op0=ALU.mult, op1=ALU.add))
            nc.vector.memset(tmp[:, 0:1], 0.0).then_inc(var_ready, 1)
            dve.wait_ge(root_ready, 1)
            link(nc.vector.reciprocal(rstd[:], tmp[:]))

        @block.scalar
        def _(act):
            act.wait_ge(var_ready, 1)
            nc.scalar.activation(tmp[:], rstd[:], ACT.Sqrt).then_inc(root_ready, 1)


def load_x(nc, st, name, x_dram, x):
    zeroed = st.sem(f"{name}_zeroed")
    loaded = st.sem(f"{name}_loaded")
    with nc.Block() as block:
        @block.vector
        def _(dve):
            nc.vector.memset(x[:, FULL:NB, :], 0.0).then_inc(zeroed, 1)

        @block.sync
        def _(sp):
            sp.dma_start(x[:, 0:FULL, :], x_dram[0:FULL * P, :].rearrange("(b p) d -> p b d", p=P)).then_inc(loaded, 16)
            sp.wait_ge(zeroed, 1)
            sp.dma_start(x[0:TAIL, FULL, :], x_dram[FULL * P:N, :]).then_inc(loaded, 16)
            sp.wait_ge(loaded, 32)


class Projection:

    STEPS = NB // 2

    def __init__(self, nc, st, ctx, x, nshift, rstd, ident, ones, weights, biases, tables, clears, cleared):
        def sb(name, shape, dt=F32):
            return ctx.enter_context(nc.sbuf_tensor(f"qkv_{name}", shape, dt))

        self.nc, self.x, self.nshift, self.rstd = nc, x, nshift, rstd
        self.clears, self.cleared = clears, cleared
        self.ident, self.ones, self.weights, self.biases, self.tables = ident, ones, weights, biases, tables
        self.w, self.bias = sb("w", [P, DC, 3 * D]), sb("bias", [1, 3 * D])
        self.xn, self.xt = sb("xn", [P, 2, D]), sb("xt", [P, 2, 2 * D])
        self.out = sb("out", [P, 2, 3 * D])
        self.pt = ctx.enter_context(nc.psum_tensor("qkv_pt", [P, 2 * D], F32))
        self.pq = ctx.enter_context(nc.psum_tensor("qkv_pq", [P, 2 * D], F32))
        self.pkv = ctx.enter_context(nc.psum_tensor("qkv_pkv", [P, 2, 2 * D], F32))
        self.w_loaded = st.sem("qkv_w_loaded")
        self.xn_ready = st.sem("qkv_xn_ready")
        self.turned = st.sem("qkv_turned")
        self.xt_ready = st.sem("qkv_xt_ready")
        self.q_product = st.sem("qkv_q_product")
        self.kv_product = st.sem("qkv_kv_product")
        self.q_out = st.sem("qkv_q_out")
        self.kv_out = st.sem("qkv_kv_out")
        self.stored = st.sem("qkv_stored")

    def store(self, sp):
        for j, (wm, bm) in enumerate(zip(self.weights, self.biases)):
            sp.dma_start(self.w[:, :, j * D:(j + 1) * D], wm.rearrange("(c p) n -> p c n", p=P)).then_inc(self.w_loaded, 16)
            sp.dma_start(self.bias[0:1, j * D:(j + 1) * D], bm.rearrange("(a n) -> a n", a=1)).then_inc(self.w_loaded, 16)
        for to, of in self.clears:
            sp.dma_start(to, of).then_inc(self.cleared, 16)
        sp.sem_inc(self.stored, 96)
        with sp.Fori(0, self.STEPS) as s:
            sp.wait_ge(self.kv_out, s + 2)
            for k in range(2):
                for j in range(3):
                    sp.dma_start(self.tables[j][bass.ds((s * 2 + k) * P, P), :],
                                 self.out[:, k, j * D:(j + 1) * D]).then_inc(self.stored, 16)
        sp.wait_ge(self.stored, 96 * self.STEPS + 96)

    def pe_turn(self, pe, s):
        nc = self.nc
        pe.wait_ge(self.xn_ready, s + 1)
        for k in range(2):
            for c in range(DC):
                last = nc.tensor.transpose(self.pt[:, (2 * k + c) * P:(2 * k + c + 1) * P],
                                           self.xn[:, k, c * P:(c + 1) * P], self.ident[:])
        last.then_inc(self.turned, 1)

    def pe_step(self, pe, s, u, more=True):
        nc = self.nc

        def product(out, k, lo, hi):
            for c in range(DC):
                nc.tensor.matmul(out, self.xt[:, u, (2 * k + c) * P:(2 * k + c + 1) * P], self.w[:, c, lo:hi],
                                 start=(c == 0), stop=False)
            return nc.tensor.matmul(out, self.ones[0:1, :], self.bias[0:1, lo:hi], start=False, stop=True)

        pe.wait_ge(self.xt_ready, s + 1)
        pe.wait_ge(self.q_out, s + 1)
        for k in range(2):
            last = product(self.pq[:, k * D:(k + 1) * D], k, 0, D)
        last.then_inc(self.q_product, 1)
        if more:
            self.pe_turn(pe, s + 1)
        pe.wait_ge(self.kv_out, s + 1)
        for k in range(2):
            last = product(self.pkv[:, k, :], k, D, 3 * D)
        last.then_inc(self.kv_product, 1)

    def act_norm(self, s):
        nc = self.nc
        for k in range(2):
            b = s * 2 + k
            last = nc.scalar.activation(self.xn[:, k, :], self.x[:, bass.ds(b, 1), :].rearrange("p a d -> p (a d)"),
                                        ACT.Identity, bias=self.nshift[:, bass.ds(b, 1)], scale=self.rstd[:, bass.ds(b, 1)])
        last.then_inc(self.xn_ready, 1)

    def act_xt(self, act, s, u):
        act.wait_ge(self.kv_product, s)
        act.wait_ge(self.turned, s + 1)
        self.nc.scalar.copy(self.xt[:, u, :], self.pt[:]).then_inc(self.xt_ready, 1)

    def act_step(self, act, s, u, more=2):
        nc = self.nc
        if more > 0:
            self.act_xt(act, s + 1, 1 - u)
        if more > 1:
            self.act_norm(s + 2)
        act.wait_ge(self.stored, s * 96 + 96)
        act.wait_ge(self.q_product, s + 1)
        nc.scalar.activation(self.out[:, :, 0:D], self.pq[:].rearrange("p (k d) -> p k d", k=2), ACT.Copy,
                             scale=float(HD) ** -0.5).then_inc(self.q_out, 1)
        act.wait_ge(self.kv_product, s + 2)
        nc.scalar.copy(self.out[:, :, D:3 * D], self.pkv[:]).then_inc(self.kv_out, 1)

    def before(self, engine, pe=False):
        if pe:
            engine.sem_inc(self.kv_product, 1)
            engine.wait_ge(self.w_loaded, 96)
            self.pe_turn(engine, 0)
        else:
            engine.sem_inc(self.q_out, 1)
            engine.sem_inc(self.kv_out, 1)
            self.act_norm(0)
            engine.wait_ge(self.turned, 1)
            self.nc.scalar.copy(self.xt[:, 0, :], self.pt[:]).then_inc(self.xt_ready, 1)
            self.act_norm(1)

    def two_steps(self, engine, s, pe=False, more=2):
        for u in range(2):
            if pe:
                self.pe_step(engine, s + u, u)
            else:
                self.act_step(engine, s + u, u, more=min(2, more + 1 - u))

    def after(self, engine, pe=False):
        if pe:
            self.pe_step(engine, self.STEPS - 1, 0, more=False)
        else:
            self.act_step(engine, self.STEPS - 1, 0, more=0)


def sort_edges(nc, st, src, dst, scratch, row_blocks, ident, iota_part, projection):
    assert N <= 1 << 13
    CHUNKS = SL // P
    with ExitStack() as ctx:
        def sb(name, shape, dt=F32):
            return ctx.enter_context(nc.sbuf_tensor(f"so_{name}", shape, dt))

        raw = [sb("raw_src", [P, SL], I32), sb("raw_dst", [P, SL], I32)]
        keys = [sb("keys0", [P, SL]), sb("keys1", [P, SL])]
        part_int = sb("part_int", [P, 1], I32)
        bits = sb("bits", [P, 8], I32)
        sign = sb("sign", [P, 8])
        change = sb("change", [P, 8])
        turned = ctx.enter_context(nc.psum_tensor("so_turned", [P, SL], F32))
        padded = st.sem("so_padded")
        loaded = st.sem("so_loaded")
        chain = st.sem("so_chain")
        exchanged = st.sem("so_exchanged")
        to_turn = st.sem("so_to_turn")
        half_turned = st.sem("so_half_turned")
        half_out = st.sem("so_half_out")
        decoded = st.sem("so_decoded")
        stored = st.sem("so_stored")
        MERGES = 7
        buffers = []

        with nc.Block() as block:
            @block.sync
            def _(sp):
                sp.wait_ge(padded, 2)
                sp.dma_start(raw[0][0:RP, 0:RE], src.rearrange("(p e) -> p e", p=RP)).then_inc(loaded, 16)
                sp.dma_start(raw[1][0:RP, 0:RE], dst.rearrange("(p e) -> p e", p=RP)).then_inc(loaded, 16)
                projection.store(sp)
                sp.wait_ge(decoded, 1)
                for of, name in zip(raw, ("rows", "cols")):
                    sp.dma_start(scratch[name].rearrange("t e -> (t e)").rearrange("(p f) -> p f", p=P), of[:]).then_inc(stored, 16)
                sp.wait_ge(stored, 32)

            @block.vector
            def _(dve):
                link = chained(dve, chain)
                nc.vector.memset(raw[0][:], PAD_ROW - 1).then_inc(padded, 1)
                nc.vector.memset(raw[1][:], 0).then_inc(padded, 1)
                link(nc.vector.tensor_copy(part_int[:], iota_part[:]))
                link(nc.vector.memset(bits[:], 0))
                for n in range(MERGES):
                    link(nc.vector.tensor_scalar(bits[:, n:n + 1], part_int[:], n, 1, ALU.arith_shift_right, ALU.bitwise_and))
                link(nc.vector.tensor_copy(sign[:], bits[:]))
                link(nc.vector.tensor_scalar(sign[:], sign[:], -2.0, 1.0, ALU.mult, ALU.add))
                link(nc.vector.tensor_tensor(change[:, 1:8], sign[:, 1:8], sign[:, 0:7], ALU.mult))
                dve.wait_ge(loaded, 32)
                link(nc.vector.tensor_scalar(raw[0][:], raw[0][:], 13, KEY_EXPONENT, ALU.logical_shift_left, ALU.bitwise_or))
                link(nc.vector.tensor_tensor(raw[0][:], raw[0][:], raw[1][:], ALU.bitwise_or))
                link(nc.vector.tensor_scalar(keys[0][:], raw[0][:].bitcast(F32), sign[:, 0:1], None, ALU.mult))
                state = {"at": 0, "done": 0, "turns": 0}

                def exchange(half, mirrored=False):
                    if state["done"]:
                        dve.wait_ge(exchanged, state["done"])
                    of, to = (k[:].rearrange("p (n two h) -> p n two h", two=2, h=half)
                              for k in (keys[state["at"]], keys[1 - state["at"]]))
                    high = slice(None, None, -1) if mirrored else slice(None)
                    pair = of[:, :, 0, :], of[:, :, 1, high]
                    nc.vector.tensor_tensor(to[:, :, 0, :], *pair, ALU.min).then_inc(exchanged, 1)
                    nc.vector.tensor_tensor(to[:, :, 1, high], *pair, ALU.max).then_inc(exchanged, 1)
                    state["done"] += 2
                    state["at"] = 1 - state["at"]

                def turn_keys():
                    dve.sem_inc(to_turn, 1)
                    state["turns"] += 1
                    dve.wait_ge(half_turned, 2 * state["turns"] - 1)
                    to = keys[1 - state["at"]]
                    nc.vector.tensor_copy(to[:, 0:SL // 2], turned[:, 0:SL // 2]).then_inc(half_out, 1)
                    dve.wait_ge(half_out, 2 * state["turns"])
                    buffers.append(state["at"])
                    state["at"] = 1 - state["at"]

                half = 1
                while half < SL:
                    exchange(half, mirrored=True)
                    finer = half // 2
                    while finer:
                        exchange(finer)
                        finer //= 2
                    half *= 2
                for n in range(1, MERGES + 1):
                    dve.wait_ge(exchanged, state["done"])
                    link(nc.vector.tensor_scalar(keys[1 - state["at"]][:], keys[state["at"]][:], change[:, n:n + 1], None, ALU.mult))
                    state["at"] = 1 - state["at"]
                    turn_keys()
                    for m in range(n - 1, -1, -1):
                        exchange(1 << m)
                    dve.wait_ge(exchanged, state["done"])
                    turn_keys()
                    half = SL // 2
                    while half:
                        exchange(half)
                        half //= 2
                dve.wait_ge(exchanged, state["done"])
                final = keys[state["at"]][:].bitcast(I32)
                link(nc.vector.tensor_scalar(raw[0][:], final, 13, (1 << 13) - 1, ALU.arith_shift_right, ALU.bitwise_and))
                spare = keys[1 - state["at"]][:].bitcast(I32)
                link(nc.vector.tensor_scalar(spare, final, 20, 63, ALU.arith_shift_right, ALU.bitwise_and))
                link(nc.vector.tensor_copy(row_blocks[:], spare))
                nc.vector.tensor_scalar(raw[1][:], final, (1 << 13) - 1, None, ALU.bitwise_and).then_inc(decoded, 1)

            ahead = projection.STEPS - 1 - 2 * MERGES
            assert ahead % 2 == 0 and len(buffers) == 2 * MERGES

            @block.tensor
            def _(pe):
                projection.before(pe, pe=True)
                with pe.Fori(0, ahead // 2) as s:
                    projection.two_steps(pe, s * 2, pe=True)
                for n, at in enumerate(buffers):
                    pe.wait_ge(to_turn, n + 1)
                    for c in range(CHUNKS):
                        last = nc.tensor.transpose(turned[:, c * P:(c + 1) * P], keys[at][:, c * P:(c + 1) * P], ident[:])
                        if c % (CHUNKS // 2) == CHUNKS // 2 - 1:
                            last.then_inc(half_turned, 1)
                    if n % 2:
                        projection.two_steps(pe, ahead + n - 1, pe=True)
                projection.after(pe, pe=True)

            @block.scalar
            def _(act):
                act.wait_ge(loaded, 32)
                projection.before(act)
                with act.Fori(0, ahead // 2) as s:
                    projection.two_steps(act, s * 2)
                for n, at in enumerate(buffers):
                    act.wait_ge(half_turned, 2 * n + 2)
                    nc.scalar.copy(keys[1 - at][:, SL // 2:SL], turned[:, SL // 2:SL]).then_inc(half_out, 1)
                    if n % 2:
                        projection.two_steps(act, ahead + n - 1, more=1 if n == len(buffers) - 1 else 2)
                projection.after(act)


def item_tables(nc, st, row_blocks, scratch, ident, ones, rel, col, q_all, q_dram, cleared):
    with ExitStack() as ctx:
        def sb(name, shape, dt=F32):
            return ctx.enter_context(nc.sbuf_tensor(f"it_{name}", shape, dt))

        below = sb("below", [P, 2, SL], BF16)
        number = sb("number", [P, NB])
        bound = sb("bound", [P, NB])
        count = sb("count", [P, NB])
        ptr = sb("ptr", [P, NB], I32)
        up = sb("up", [P, NB], I32)
        first = sb("first", [P, NB])
        behind = sb("behind", [P, NB])
        many = sb("many", [P, FULL + 1])
        ends = sb("ends", [P, FULL + 1])
        shift = sb("shift", [P, FULL + 1])
        item = sb("item", [P, IG])
        block_of = sb("block_of", [P, IG])
        block_int = sb("block_int", [P, IG], I32)
        tile_of = sb("tile_of", [P, IG])
        tile_int = sb("tile_int", [P, IG], I32)
        table = sb("table", [P, IG, FULL + 1])
        got_row = sb("got_row", [P, IG, P], I32)
        got_col = sb("got_col", [P, IG, P], I32)
        rowf = sb("rowf", [P, IG, P])
        key = sb("key", [P, IG, P], I16)
        colf = sb("colf", [P, IG, P])
        total = ctx.enter_context(nc.psum_tensor("it_total", [P, 512], F32))
        turned = ctx.enter_context(nc.psum_tensor("it_turned", [P, 2, 512], F32))
        made = st.sem("it_made")
        counted = st.sem("it_counted")
        chain = st.sem("it_chain")
        counts_done = st.sem("it_counts_done")
        summed = st.sem("it_summed")
        tiles_ready = st.sem("it_tiles_ready")
        gathered = st.sem("it_gathered")
        tables_ready = st.sem("it_tables_ready")
        turned_ready = st.sem("it_turned_ready")
        turned_out = st.sem("it_turned_out")
        stored = st.sem("it_stored")
        NBLK = FULL + 1
        with nc.Block() as block:
            @block.sync
            def _(sp):
                sp.dma_start(q_all[:], q_dram.rearrange("(b p) d -> p b d", p=P)).then_inc(stored, 16)
                sp.wait_ge(cleared, 48)
                sp.wait_ge(tables_ready, 1)
                sp.dma_start(scratch["item_block"].rearrange("(g p) -> p g", p=P), block_int[:], allow_slow_non_contiguous=True).then_inc(stored, 16)
                sp.dma_start(scratch["keys"].rearrange("(g p) e -> p g e", p=P), key[:]).then_inc(stored, 16)
                sp.wait_ge(stored, 48)

            @block.gpsimd
            def _(pool):
                nc.gpsimd.iota(bound[:], pattern=[[P, NB]], base=0, channel_multiplier=0,
                               allow_small_or_imprecise_dtypes=True).then_inc(made, 1)
                nc.gpsimd.iota(number[:], pattern=[[1, NB]], base=0, channel_multiplier=0,
                               allow_small_or_imprecise_dtypes=True).then_inc(made, 1)
                nc.gpsimd.iota(item[:], pattern=[[P, IG]], base=0, channel_multiplier=1,
                               allow_small_or_imprecise_dtypes=True).then_inc(made, 1)
                pool.wait_ge(tiles_ready, 1)
                for g in range(IG):
                    for got, name in ((got_row, "rows"), (got_col, "cols")):
                        nc.gpsimd.indirect_dma_start(got[:, g, :], None, scratch[name],
                                                     bass.IndirectOffsetOnAxis(ap=tile_int[:, g:g + 1], axis=0)).then_inc(gathered, 16)

            @block.tensor
            def _(pe):
                pe.wait_ge(counts_done, 1)
                nc.tensor.matmul(total[:, 0:NB], ones[:], count[:], start=True, stop=True).then_inc(summed, 1)
                pe.wait_ge(tables_ready, 1)
                for n in range(2 * IG):
                    if n >= 2:
                        pe.wait_ge(turned_out, n - 1)
                    of = rowf if n % 2 == 0 else colf
                    nc.tensor.transpose(turned[:, n % 2, 0:P], of[:, n // 2, :], ident[:]).then_inc(turned_ready, 1)

            @block.vector
            def _(dve):
                link = chained(dve, chain)
                dve.wait_ge(made, 3)
                for k in range(2):
                    nc.vector.tensor_scalar(below[:, k, :], row_blocks[:], number[:, k:k + 1], None, ALU.is_lt,
                                            ALU.add, accum_out=count[:, k:k + 1]).then_inc(counted, 1)
                with dve.Fori(1, NB // 2) as h:
                    for k in range(2):
                        b = h * 2 + k
                        dve.wait_ge(counted, b - 1)
                        nc.vector.tensor_scalar(below[:, k, :], row_blocks[:], number[:, bass.ds(b, 1)], None, ALU.is_lt,
                                                ALU.add, accum_out=count[:, bass.ds(b, 1)]).then_inc(counted, 1)
                dve.wait_ge(counted, NB)
                nc.vector.memset(many[:], 0.0).then_inc(counts_done, 1)
                dve.wait_ge(summed, 1)
                link(nc.vector.tensor_copy(ptr[:], total[:, 0:NB]))
                link(nc.vector.tensor_scalar(behind[:], total[:, 0:NB], float(P - 1), None, ALU.add))
                link(nc.vector.tensor_copy(up[:], behind[:]))
                link(nc.vector.tensor_scalar(ptr[:], ptr[:], 7, None, ALU.arith_shift_right))
                link(nc.vector.tensor_scalar(up[:], up[:], 7, None, ALU.arith_shift_right))
                link(nc.vector.tensor_copy(first[:], ptr[:]))
                link(nc.vector.tensor_copy(behind[:], up[:]))
                link(nc.vector.tensor_copy(count[:], total[:, 0:NB]))
                link(nc.vector.tensor_tensor(many[:], behind[:, 1:NBLK + 1], first[:, 0:NBLK], ALU.subtract))
                link(nc.vector.tensor_tensor(shift[:], count[:, 1:NBLK + 1], count[:, 0:NBLK], ALU.is_gt))
                link(nc.vector.tensor_tensor(many[:], many[:], shift[:], ALU.mult))
                link(nc.vector.tensor_tensor_scan(ends[:], ones[:, 0:NBLK], many[:], 0.0, ALU.mult, ALU.add))
                link(nc.vector.tensor_tensor(shift[:], first[:, 0:NBLK], ends[:], ALU.subtract))
                link(nc.vector.tensor_tensor(shift[:], shift[:], many[:], ALU.add))
                wide = [P, IG, NBLK]
                ends_b = ends[:].unsqueeze(1).to_broadcast(wide)
                shift_b = shift[:].unsqueeze(1).to_broadcast(wide)
                link(nc.vector.tensor_tensor(table[:], ends_b, item[:].unsqueeze(2).to_broadcast(wide), ALU.is_le))
                link(nc.vector.tensor_reduce(block_of[:], table[:], AX.X, ALU.add))
                link(nc.vector.tensor_scalar(tile_of[:], block_of[:], float(P), None, ALU.mult))
                link(nc.vector.tensor_tensor(table[:], bound[:, 0:NBLK].unsqueeze(1).to_broadcast(wide),
                                             tile_of[:].unsqueeze(2).to_broadcast(wide), ALU.is_equal))
                link(nc.vector.tensor_tensor(table[:], table[:], shift_b, ALU.mult))
                link(nc.vector.tensor_reduce(tile_of[:], table[:], AX.X, ALU.add))
                link(nc.vector.tensor_tensor(tile_of[:], tile_of[:], item[:], ALU.add))
                link(nc.vector.tensor_scalar(tile_of[:], tile_of[:], float(ET - 1), None, ALU.min))
                link(nc.vector.tensor_copy(block_int[:], block_of[:]))
                nc.vector.tensor_copy(tile_int[:], tile_of[:]).then_inc(tiles_ready, 1)
                dve.wait_ge(gathered, 16 * 2 * IG)
                link(nc.vector.tensor_copy(rowf[:], got_row[:]))
                link(nc.vector.tensor_copy(colf[:], got_col[:]))
                link(nc.vector.tensor_scalar(tile_of[:], block_of[:], float(NBLK), float(PAD_ROW), ALU.is_equal, ALU.mult))
                link(nc.vector.tensor_tensor(key[:], rowf[:], tile_of[:].unsqueeze(2).to_broadcast([P, IG, P]), ALU.add))
                link(nc.vector.tensor_scalar(tile_of[:], block_of[:], float(P), None, ALU.mult))
                nc.vector.tensor_tensor(rowf[:], rowf[:], tile_of[:].unsqueeze(2).to_broadcast([P, IG, P]),
                                        ALU.subtract).then_inc(tables_ready, 1)
                for n in range(2 * IG):
                    dve.wait_ge(turned_ready, n + 1)
                    to = rel if n % 2 == 0 else col
                    nc.vector.tensor_copy(to[:, (n // 2) * P:(n // 2 + 1) * P], turned[:, n % 2, 0:P]).then_inc(turned_out, 1)




def load_blocks(nc, item_block, q, engine, many=QUAD):
    _, values = nc.values_load_multi_w_load_instructions(
        item_block[0:1, bass.ds(q * many, many)], engines=[engine], min_val=0, max_val=NB - 1,
        skip_runtime_bounds_check_because="item_tables counts at most FULL + 1 block ends before an item")
    return values


def edge_scores(nc, st, q_all, k_dram, rel, col, col_lo, col_hi, item_block, iota_free, ident, scores, degree):
    with ExitStack() as ctx:
        def sb(name, shape, dt=F32):
            return ctx.enter_context(nc.sbuf_tensor(f"sc_{name}", shape, dt))

        kg = sb("kg", [P, RING, QUAD, D])
        index = sb("index", [P, RING, QUAD], I32)
        hot = sb("hot", [P, 2, QUAD, P], BF16)
        ident_half = sb("ident_half", [P, P], BF16)
        hot_t = sb("hot_t", [P, 2, QUAD, P])
        product = sb("product", [P, QUAD, D])
        low = sb("low", [P, 2, QUAD, P], BF16)
        high = sb("high", [P, 2, QUAD, NB], BF16)
        zero = sb("zero", [P, P], BF16)
        degree_rows = sb("degree_rows", [NB, P])
        table = ctx.enter_context(nc.psum_tensor("sc_table", [P, 512], F32))
        pt = ctx.enter_context(nc.psum_tensor("sc_pt", [P, 2, 1024], BF16))
        pq = ctx.enter_context(nc.psum_tensor("sc_pq", [P, 2, 2, 512], F32))
        gathered = [st.sem(f"sc_gathered{k}") for k in range(RING * QUAD)]
        index_ready = st.sem("sc_index_ready")
        hot_ready = st.sem("sc_hot_ready")
        hot_turned = st.sem("sc_hot_turned")
        hot_t_ready = st.sem("sc_hot_t_ready")
        q_expanded = st.sem("sc_q_expanded")
        product_ready = st.sem("sc_product_ready")
        reduced = st.sem("sc_reduced")
        zeroed = st.sem("sc_zeroed")
        column_hot = st.sem("sc_column_hot")
        column_counted = st.sem("sc_column_counted")
        degree_out = st.sem("sc_degree_out")
        QUADS = NI // QUAD
        with nc.Block() as block:
            @block.gpsimd
            def _(pool):
                nc.gpsimd.memset(col[:, NI:NI + QUAD], 0).then_inc(index_ready, 1)
                nc.gpsimd.tensor_copy(index[:, 0, :], col[:, 0:QUAD]).then_inc(index_ready, 1)
                with pool.Fori(0, QUADS // RING) as s:
                    for u in range(RING):
                        q = s * RING + u
                        pool.wait_ge(product_ready, q * 2 + 1)
                        pool.wait_ge(index_ready, q + 2)
                        nc.gpsimd.tensor_copy(index[:, (u + 1) % RING, :],
                                              col[:, bass.ds((q + 1) * QUAD, QUAD)]).then_inc(index_ready, 1)
                        for j in range(QUAD):
                            nc.gpsimd.indirect_dma_start(
                                kg[:, u, j, :], None, k_dram,
                                bass.IndirectOffsetOnAxis(ap=index[:, u, j:j + 1], axis=0)).then_inc(gathered[u * QUAD + j], 16)

            @block.tensor
            def _(pe):
                pe.sem_inc(hot_turned, 1)
                pe.sem_inc(q_expanded, 1)
                def turn(u):
                    for j in range(QUAD):
                        last = nc.tensor.transpose(pt[:, u, j * P:(j + 1) * P], hot[:, u, j, :], ident_half[:])
                    last.then_inc(hot_turned, 1)

                pe.sem_inc(column_counted, 2)
                pe.wait_ge(zeroed, 2)
                nc.tensor.matmul(table[0:NB, 0:P], zero[:, 0:NB], zero[:], start=True, stop=False)
                for u in range(2):
                    pe.wait_ge(hot_ready, u + 1)
                    turn(u)
                with pe.Fori(0, QUADS // 2) as s:
                    for u in range(2):
                        q = s * 2 + u
                        blk = load_blocks(nc, item_block, q, mybir.EngineType.PE)
                        pe.wait_ge(hot_t_ready, q + 1)
                        for half in range(2):
                            pe.wait_ge(product_ready, q * 2 + half + 2)
                            for j in (2 * half, 2 * half + 1):
                                last = nc.tensor.matmul(pq[:, u, half, (j % 2) * D:(j % 2 + 1) * D], hot_t[:, u, j, :],
                                                        q_all[:, bass.ds(blk[j], 1), :].rearrange("p a d -> p (a d)"),
                                                        start=True, stop=True)
                            last.then_inc(q_expanded, 1)
                            if half == 0:
                                pe.wait_ge(hot_ready, q + 3)
                                turn(u)
                        pe.wait_ge(column_hot, q * 2 + 2)
                        for j in range(QUAD):
                            last = nc.tensor.matmul(table[0:NB, 0:P], high[:, u, j, :], low[:, u, j, :], start=False, stop=False)
                        last.then_inc(column_counted, 1)
                nc.tensor.matmul(table[0:NB, 0:P], zero[:, 0:NB], zero[:], start=False, stop=True).then_inc(column_counted, 1)
                pe.wait_ge(degree_out, 1)
                nc.tensor.transpose(pq[:, 0, 0, 0:NB], degree_rows[:], ident[0:NB, 0:NB]).then_inc(column_counted, 1)

            @block.scalar
            def _(act):
                def copy_turned(u):
                    nc.scalar.copy(hot_t[:, u, :, :].rearrange("p j n -> p (j n)"), pt[:, u, 0:QUAD * P]).then_inc(hot_t_ready, 1)

                for u in range(2):
                    act.wait_ge(hot_turned, u + 2)
                    copy_turned(u)
                with act.Fori(0, QUADS // 2) as s:
                    for u in range(2):
                        q = s * 2 + u
                        act.wait_ge(q_expanded, q * 2 + 3)
                        act.wait_ge(hot_turned, q + 4)
                        copy_turned(u)

            @block.vector
            def _(dve):
                dve.sem_inc(product_ready, 1)
                def one_hots(q, u):
                    wide = [P, QUAD, P]
                    nc.vector.tensor_tensor(hot[:, u, :, :], iota_free[:].unsqueeze(1).to_broadcast(wide),
                                            rel[:, bass.ds(q * QUAD, QUAD)].unsqueeze(2).to_broadcast(wide),
                                            ALU.is_equal).then_inc(hot_ready, 1)

                nc.vector.memset(rel[:, NI:NI + 2 * QUAD], float(P)).then_inc(product_ready, 4)
                nc.vector.memset(product[:], 0.0).then_inc(reduced, 2)
                nc.vector.tensor_copy(ident_half[:], ident[:]).then_inc(zeroed, 1)
                nc.vector.memset(zero[:], 0.0).then_inc(zeroed, 1)
                for u in range(2):
                    one_hots(u, u)
                with dve.Fori(0, QUADS // RING) as s:
                    for v in range(RING):
                        q, u = s * RING + v, v % 2
                        dve.wait_ge(hot_turned, q + 2)
                        one_hots(q + 2, u)
                        at = bass.ds(q * QUAD, QUAD)
                        dve.wait_ge(column_counted, q + 1)
                        for to, of in ((high, col_hi), (low, col_lo)):
                            shape = [P, QUAD, to.shape[3]]
                            nc.vector.tensor_tensor(to[:, u, :, :], iota_free[:, 0:shape[2]].unsqueeze(1).to_broadcast(shape),
                                                    of[:, at].unsqueeze(2).to_broadcast(shape), ALU.is_equal).then_inc(column_hot, 1)
                        for half in range(2):
                            pair = slice(2 * half, 2 * half + 2)
                            dve.wait_ge(q_expanded, q * 2 + half + 2)
                            for j in (2 * half, 2 * half + 1):
                                dve.wait_ge(gathered[v * QUAD + j], s * 16 + 16)
                            dve.wait_ge(reduced, q * 2 + half + 1)
                            nc.vector.tensor_tensor(product[:, pair, :].rearrange("p j d -> p (j d)"),
                                                    kg[:, v, pair, :].rearrange("p j d -> p (j d)"),
                                                    pq[:, u, half, :], ALU.mult).then_inc(product_ready, 1)
                        for half in range(2):
                            pair = slice(2 * half, 2 * half + 2)
                            dve.wait_ge(product_ready, q * 2 + half + 6)
                            nc.vector.tensor_reduce(
                                scores[:, bass.ds(q * QUAD + 2 * half, 2), :].rearrange("p j h -> p (j h)"),
                                product[:, pair, :].rearrange("p j (h d) -> p (j h) d", h=HEADS),
                                AX.X, ALU.add).then_inc(reduced, 1)
                dve.wait_ge(column_counted, QUADS + 3)
                nc.vector.tensor_copy(degree_rows[:], table[0:NB, 0:P]).then_inc(degree_out, 1)
                dve.wait_ge(column_counted, QUADS + 4)
                nc.vector.tensor_copy(degree[:], pq[:, 0, 0, 0:NB]).then_inc(degree_out, 1)


def softmax_over_rows(nc, st, scores, keys, bounce, ident):
    view = scores[:].rearrange("p (c g) h -> p g c h", c=CH)
    largest = scores[:].rearrange("p i h -> p (i h)")
    keys_flat = keys.rearrange("i e -> (i e)")
    GROUPS = CI // QUAD
    with ExitStack() as ctx:
        def sb(name, shape, dt=F32):
            return ctx.enter_context(nc.sbuf_tensor(f"sm_{name}", shape, dt))

        line = sb("line", [P, CL])
        key = sb("key", [P, CL], I16)
        cut = sb("cut", [P, CL + 1], BF16)
        part = sb("part", [P, 2, QUAD * P])
        end_keys = sb("end_keys", [HEADS, 2, CH], I16)
        end_keyf = sb("end_keyf", [HEADS, 2, CH])
        same = sb("same", [HEADS, CH])
        forth = sb("forth", [HEADS, CH])
        back = sb("back", [HEADS, CH])
        ends = sb("ends", [HEADS, CH])
        reach = sb("reach", [HEADS, CH])
        carried = sb("carried", [HEADS, CH])
        carry = sb("carry", [P, 2])
        turned = ctx.enter_context(nc.psum_tensor("sm_turned", [P, 2, 512], F32))
        part_ready = st.sem("sm_part_ready")
        turned_ready = st.sem("sm_turned_ready")
        turned_out = st.sem("sm_turned_out")
        keys_loaded = st.sem("sm_keys_loaded")
        chain = st.sem("sm_chain")
        bounced = st.sem("sm_bounced")
        to_bounce = st.sem("sm_to_bounce")
        differences = st.sem("sm_differences")
        with nc.Block() as block:
            @block.sync
            def _(sp):
                for c in range(CH):
                    sp.dma_start(key[c * HEADS:(c + 1) * HEADS, :],
                                 keys_flat[c * CL:(c + 1) * CL].unsqueeze(0).to_broadcast([HEADS, CL])).then_inc(keys_loaded, 16)
                for n, at in enumerate((0, CL - 1)):
                    ends_of = keys_flat.rearrange("(c l) -> c l", c=CH)[:, at:at + 1].rearrange("c o -> o c")
                    sp.dma_start(end_keys[:, n, :], ends_of.to_broadcast([HEADS, CH]),
                                 allow_slow_non_contiguous=True).then_inc(keys_loaded, 16)
                for n, at in enumerate((CL - 1, 0)):
                    sp.wait_ge(to_bounce, 2 * n + 1)
                    sp.dma_start(bounce[0], largest[:, at:at + 1]).then_inc(bounced, 16)
                    sp.wait_ge(bounced, 16 * (4 * n + 1))
                    sp.dma_start(ends[:], bounce[0].rearrange("(c h) o -> h (c o)", h=HEADS),
                                 allow_slow_non_contiguous=True).then_inc(bounced, 16)
                    sp.wait_ge(to_bounce, 2 * n + 2)
                    sp.wait_ge(bounced, 16 * (4 * n + 2))
                    sp.dma_start(bounce[1].rearrange("(c h) o -> h (c o)", h=HEADS), carried[:],
                                 allow_slow_non_contiguous=True).then_inc(bounced, 16)
                    sp.wait_ge(bounced, 16 * (4 * n + 3))
                    sp.dma_start(carry[:, n:n + 1], bounce[1]).then_inc(bounced, 16)

            @block.scalar
            def _(act):
                with act.Fori(0, GROUPS // 2) as s:
                    for u in range(2):
                        g = s * 2 + u
                        act.wait_ge(turned_ready, s * 2 + 1)
                        nc.scalar.copy(part[:, u, :].rearrange("p (g c h) -> p g c h", g=QUAD, c=CH),
                                       view[:, bass.ds(g * QUAD, QUAD), :, :]).then_inc(part_ready, 1)
                act.wait_ge(differences, 1)
                with act.Fori(0, GROUPS // 2) as s:
                    for u in range(2):
                        g = s * 2 + u
                        act.wait_ge(turned_ready, s * 2 + GROUPS + 1)
                        nc.scalar.activation(part[:, u, :], line[:, bass.ds(g * QUAD * P, QUAD * P)], ACT.Exp).then_inc(part_ready, 1)

            @block.tensor
            def _(pe):
                pe.sem_inc(turned_ready, 1)
                with pe.Fori(0, GROUPS) as s:
                    for u in range(2):
                        pe.wait_ge(part_ready, s * 2 + u + 1)
                        pe.wait_ge(turned_out, s * 2 + 1)
                        for j in range(QUAD):
                            last = nc.tensor.transpose(turned[:, u, j * P:(j + 1) * P], part[:, u, j * P:(j + 1) * P], ident[:])
                        last.then_inc(turned_ready, 1)

            @block.vector
            def _(dve):
                dve.sem_inc(turned_out, 1)
                link = chained(dve, chain)
                dve.wait_ge(keys_loaded, 16 * (CH + 2))
                link(nc.vector.memset(cut[:, 0:1], 0.0))
                link(nc.vector.memset(cut[:, CL:CL + 1], 0.0))
                link(nc.vector.tensor_tensor(cut[:, 1:CL], key[:, 1:CL], key[:, 0:CL - 1], ALU.not_equal))
                link(nc.vector.tensor_scalar(cut[:, 1:CL], cut[:, 1:CL], -BIG, None, ALU.mult))
                link(nc.vector.tensor_copy(end_keyf[:], end_keys[:]))
                link(nc.vector.memset(same[:], 1.0))
                link(nc.vector.tensor_tensor(same[:, 0:CH - 1], end_keyf[:, 0, 1:CH], end_keyf[:, 1, 0:CH - 1], ALU.not_equal))
                link(nc.vector.tensor_tensor(reach[:], end_keyf[:, 0, :], end_keyf[:, 1, :], ALU.not_equal))
                link(nc.vector.tensor_tensor(back[:], same[:], reach[:], ALU.max))
                link(nc.vector.memset(forth[:], 1.0))
                link(nc.vector.tensor_tensor(forth[:, 1:CH], same[:, 0:CH - 1], reach[:, 1:CH], ALU.max))
                for flags in (same, forth, back):
                    link(nc.vector.tensor_scalar(flags[:], flags[:], -BIG, None, ALU.mult))
                with dve.Fori(0, GROUPS // 2) as s:
                    for u in range(2):
                        g = s * 2 + u
                        dve.wait_ge(turned_ready, g + 2)
                        nc.vector.tensor_copy(line[:, bass.ds(g * QUAD * P, QUAD * P)], turned[:, u, :]).then_inc(turned_out, 1)
                dve.wait_ge(turned_out, GROUPS + 1)

                link(nc.vector.tensor_tensor_scan(largest, cut[:, 0:CL], line[:], -BIG, ALU.add, ALU.max))
                nc.vector.memset(carried[:], -BIG).then_inc(to_bounce, 1)
                dve.wait_ge(bounced, 32)
                link(nc.vector.tensor_tensor_scan(reach[:], forth[:], ends[:], -BIG, ALU.add, ALU.max))
                nc.vector.tensor_tensor(carried[:, 1:CH], reach[:, 0:CH - 1], same[:, 0:CH - 1], ALU.add).then_inc(to_bounce, 1)
                dve.wait_ge(bounced, 64)
                link(nc.vector.tensor_tensor_scan(largest, cut[:, 0:CL], line[:], carry[:, 0:1], ALU.add, ALU.max))
                link(nc.vector.tensor_tensor_scan(largest[:, ::-1], cut[:, :0:-1], largest[:, ::-1], -BIG, ALU.add, ALU.max))
                nc.vector.memset(carried[:], -BIG).then_inc(to_bounce, 1)
                dve.wait_ge(bounced, 96)
                link(nc.vector.tensor_tensor_scan(reach[:, ::-1], back[:, ::-1], ends[:, ::-1], -BIG, ALU.add, ALU.max))
                nc.vector.tensor_tensor(carried[:, 0:CH - 1], reach[:, 1:CH], same[:, 0:CH - 1], ALU.add).then_inc(to_bounce, 1)
                dve.wait_ge(bounced, 128)
                link(nc.vector.tensor_tensor_scan(largest[:, ::-1], cut[:, :0:-1], largest[:, ::-1], carry[:, 1:2], ALU.add, ALU.max))
                nc.vector.tensor_tensor(line[:], line[:], largest, ALU.subtract).then_inc(differences, 1)
                dve.wait_ge(differences, 1)
                with dve.Fori(0, GROUPS // 2) as s:
                    for u in range(2):
                        g = s * 2 + u
                        dve.wait_ge(turned_ready, g + GROUPS + 2)
                        nc.vector.tensor_copy(view[:, bass.ds(g * QUAD, QUAD), :, :],
                                              turned[:, u, :].rearrange("p (g c h) -> p g c h", g=QUAD, c=CH)).then_inc(turned_out, 1)
                dve.wait_ge(turned_out, 2 * GROUPS + 1)


def aggregate(nc, st, probs, v_dram, rel, col, item_block, iota_free, acc):
    with ExitStack() as ctx:
        def sb(name, shape, dt=F32):
            return ctx.enter_context(nc.sbuf_tensor(f"ag_{name}", shape, dt))

        vg = sb("vg", [P, RING, QUAD, D])
        index = sb("index", [P, RING, QUAD], I32)
        hot = sb("hot", [P, 2, QUAD, P])
        weighted = sb("weighted", [P, 2, QUAD, AW])
        sums = ctx.enter_context(nc.psum_tensor("ag_sums", [P, 2, QUAD, 512], F32))
        gathered = [st.sem(f"ag_gathered{k}") for k in range(RING * QUAD)]
        index_ready = st.sem("ag_index_ready")
        hot_ready = st.sem("ag_hot_ready")
        p_ready = st.sem("ag_p_ready")
        weighted_ready = st.sem("ag_weighted_ready")
        summed = st.sem("ag_summed")
        added = st.sem("ag_added")
        QUADS = NI // QUAD
        with nc.Block() as block:
            @block.gpsimd
            def _(pool):
                nc.gpsimd.memset(col[:, NI:NI + QUAD], 0).then_inc(index_ready, 1)
                nc.gpsimd.tensor_copy(index[:, 0, :], col[:, 0:QUAD]).then_inc(index_ready, 1)
                with pool.Fori(0, QUADS // RING) as s:
                    for u in range(RING):
                        q = s * RING + u
                        pool.wait_ge(weighted_ready, q * 2 + 1)
                        pool.wait_ge(index_ready, q + 2)
                        nc.gpsimd.tensor_copy(index[:, (u + 1) % RING, :],
                                              col[:, bass.ds((q + 1) * QUAD, QUAD)]).then_inc(index_ready, 1)
                        for j in range(QUAD):
                            nc.gpsimd.indirect_dma_start(
                                vg[:, u, j, :], None, v_dram,
                                bass.IndirectOffsetOnAxis(ap=index[:, u, j:j + 1], axis=0)).then_inc(gathered[u * QUAD + j], 16)

            @block.scalar
            def _(act):
                with act.Fori(0, QUADS // 2) as s:
                    for u in range(2):
                        q = s * 2 + u
                        act.wait_ge(added, q * 4 + 1)
                        nc.scalar.copy(weighted[:, u, :, D:D + HEADS], probs[:, bass.ds(q * QUAD, QUAD), :]).then_inc(p_ready, 1)

            @block.tensor
            def _(pe):
                with pe.Fori(0, QUADS // 2) as s:
                    for u in range(2):
                        q = s * 2 + u
                        pe.wait_ge(added, q * 4 + 1)
                        pe.wait_ge(hot_ready, q + 1)
                        pe.wait_ge(p_ready, q + 1)
                        for half in range(2):
                            pe.wait_ge(weighted_ready, q * 2 + half + 6)
                            for j in (2 * half, 2 * half + 1):
                                last = nc.tensor.matmul(sums[:, u, j, 0:AW], hot[:, u, j, :], weighted[:, u, j, :], start=True, stop=True)
                            last.then_inc(summed, 1)

            @block.vector
            def _(dve):
                dve.sem_inc(added, 1)
                dve.sem_inc(weighted_ready, 1)
                def weigh(q, v, s):
                    u = v % 2
                    wide = [P, QUAD, P]
                    nc.vector.tensor_tensor(hot[:, u, :, :], iota_free[:].unsqueeze(1).to_broadcast(wide),
                                            rel[:, bass.ds(q * QUAD, QUAD)].unsqueeze(2).to_broadcast(wide),
                                            ALU.is_equal).then_inc(hot_ready, 1)
                    for half in range(2):
                        pair = slice(2 * half, 2 * half + 2)
                        for j in (2 * half, 2 * half + 1):
                            dve.wait_ge(gathered[v * QUAD + j], s * 16 + 16)
                        nc.vector.tensor_tensor(
                            weighted[:, u, pair, 0:D].rearrange("p j (h d) -> p j h d", h=HEADS),
                            vg[:, v, pair, :].rearrange("p j (h d) -> p j h d", h=HEADS),
                            probs[:, bass.ds(q * QUAD + 2 * half, 2), :].unsqueeze(3).to_broadcast([P, 2, HEADS, HD]),
                            ALU.mult).then_inc(weighted_ready, 1)

                def add(q, v):
                    u = v % 2
                    blk = load_blocks(nc, item_block, q, mybir.EngineType.DVE)
                    for j in range(QUAD):
                        dve.wait_ge(summed, q * 2 + j // 2 + 1)
                        dve.wait_ge(added, q * 4 + j + 5)
                        to = acc[:, bass.ds(blk[j], 1), :].rearrange("p a d -> p (a d)")
                        nc.vector.tensor_tensor(to, to, sums[:, u, j, 0:AW], ALU.add).then_inc(added, 1)

                nc.vector.memset(acc[:], 0.0).then_inc(added, 4)
                nc.vector.memset(weighted[:, :, :, AW - 1], 1.0).then_inc(weighted_ready, 4)
                weigh(0, 0, 0)
                with dve.Fori(0, QUADS // RING - 1) as s:
                    for v in range(RING):
                        q = s * RING + v
                        weigh(q + 1, (v + 1) % RING, s + (v + 1) // RING)
                        add(q, v)
                for v in range(RING):
                    q = QUADS - RING + v
                    if v + 1 < RING:
                        weigh(q + 1, v + 1, QUADS // RING - 1)
                    add(q, v)


def attention_output(nc, st, acc, x, wo, bo, ident, ones, x_dram):
    with ExitStack() as ctx:
        w = ctx.enter_context(nc.sbuf_tensor("ao_w", [P, DC, D], F32))
        bias = ctx.enter_context(nc.sbuf_tensor("ao_b", [1, D], F32))
        share = ctx.enter_context(nc.sbuf_tensor("ao_share", [P, NB, HEADS], F32))
        rows = ctx.enter_context(nc.sbuf_tensor("ao_rows", [P, 2, D], F32))
        turned = ctx.enter_context(nc.sbuf_tensor("ao_turned", [P, 2, D], F32))
        pt = ctx.enter_context(nc.psum_tensor("ao_pt", [P, 2, 512], F32))
        po = ctx.enter_context(nc.psum_tensor("ao_po", [P, 2, 512], F32))
        w_loaded = st.sem("ao_w_loaded")
        chain = st.sem("ao_chain")
        rows_ready = st.sem("ao_rows_ready")
        pt_ready = st.sem("ao_pt_ready")
        turned_ready = st.sem("ao_turned_ready")
        po_ready = st.sem("ao_po_ready")
        x_stored = st.sem("ao_x_stored")
        added = st.sem("ao_added")
        with nc.Block() as block:
            @block.sync
            def _(sp):
                sp.dma_start(w[:], wo.rearrange("(c p) n -> p c n", p=P)).then_inc(w_loaded, 16)
                sp.dma_start(bias[:], bo.rearrange("(a n) -> a n", a=1)).then_inc(w_loaded, 16)
                with sp.Fori(0, NB // UNROLL) as s:
                    sp.wait_ge(added, s * UNROLL + UNROLL + 1)
                    at = bass.ds(s * UNROLL, UNROLL)
                    sp.dma_start(x_dram[:, at, :], x[:, at, :]).then_inc(x_stored, 16)
                sp.wait_ge(x_stored, 16 * (NB // UNROLL))

            @block.vector
            def _(dve):
                dve.sem_inc(added, 1)
                link = chained(dve, chain)
                link(nc.vector.tensor_scalar(share[:], acc[:, :, D:D + HEADS], 1e-30, None, ALU.max))
                link(nc.vector.reciprocal(share[:], share[:]))
                with dve.Fori(0, NB // 2) as h:
                    b = h * 2
                    for k in range(2):
                        dve.wait_ge(pt_ready, b + 1)
                        nc.vector.tensor_tensor(
                            rows[:, k, :].rearrange("p (h d) -> p h d", h=HEADS),
                            acc[:, bass.ds(b + k, 1), 0:D].rearrange("p a (h d) -> p (a h) d", h=HEADS),
                            share[:, bass.ds(b + k, 1), :].rearrange("p a h -> p (a h)").unsqueeze(2).to_broadcast([P, HEADS, HD]),
                            ALU.mult).then_inc(rows_ready, 1)
                    for k in range(2):
                        dve.wait_ge(po_ready, b + k + 2)
                        to = x[:, bass.ds(b + k, 1), :].rearrange("p a d -> p (a d)")
                        nc.vector.tensor_tensor(to, to, po[:, k, 0:D], ALU.add).then_inc(added, 1)

            @block.scalar
            def _(act):
                act.sem_inc(turned_ready, 1)
                with act.Fori(0, NB // 2) as h:
                    b = h * 2
                    for k in range(2):
                        act.wait_ge(po_ready, b + 1)
                        act.wait_ge(pt_ready, b + k + 2)
                        nc.scalar.copy(turned[:, k, :], pt[:, k, 0:D]).then_inc(turned_ready, 1)

            @block.tensor
            def _(pe):
                pe.sem_inc(po_ready, 1)
                pe.sem_inc(pt_ready, 1)
                pe.wait_ge(w_loaded, 32)
                with pe.Fori(0, NB // 2) as h:
                    b = h * 2
                    for k in range(2):
                        pe.wait_ge(turned_ready, b + 1)
                        pe.wait_ge(rows_ready, b + k + 1)
                        for c in range(DC):
                            last = nc.tensor.transpose(pt[:, k, c * P:(c + 1) * P], rows[:, k, c * P:(c + 1) * P], ident[:])
                        last.then_inc(pt_ready, 1)
                    for k in range(2):
                        pe.wait_ge(added, b + 1)
                        pe.wait_ge(turned_ready, b + k + 2)
                        for c in range(DC):
                            nc.tensor.matmul(po[:, k, 0:D], turned[:, k, c * P:(c + 1) * P], w[:, c, :], start=(c == 0), stop=False)
                        nc.tensor.matmul(po[:, k, 0:D], ones[0:1, :], bias[:], start=False, stop=True).then_inc(po_ready, 1)


def turn(nc, st, name, x, affine, xt, ident, scale=None, shift=None):
    with ExitStack() as ctx:
        rows = ctx.enter_context(nc.sbuf_tensor(f"{name}_rows", [P, 2, D], F32))
        pt = ctx.enter_context(nc.psum_tensor(f"{name}_pt", [P, 2, 512], F32))
        rows_step = st.sem(f"{name}_rows_step")
        pt_ready = st.sem(f"{name}_pt_ready")
        out = st.sem(f"{name}_out")
        steps = len(affine)
        with nc.Block() as block:
            @block.vector
            def _(dve):
                with dve.Fori(0, NB // 2) as h:
                    b = h * 2
                    for k in range(2):
                        dve.wait_ge(pt_ready, b + 1)
                        of = x[:, bass.ds(b + k, 1), :].rearrange("p a d -> p (a d)")
                        for n, (mean, rstd) in enumerate(affine):
                            if n:
                                dve.wait_ge(rows_step, (b + k) * steps + n)
                            nc.vector.tensor_scalar(rows[:, k, :], of, mean[:, bass.ds(b + k, 1)], rstd[:, bass.ds(b + k, 1)],
                                                    ALU.subtract, ALU.mult).then_inc(rows_step, 1)
                            of = rows[:, k, :]

            @block.tensor
            def _(pe):
                pe.sem_inc(pt_ready, 1)
                with pe.Fori(0, NB // 2) as h:
                    b = h * 2
                    for k in range(2):
                        pe.wait_ge(out, b + 1)
                        pe.wait_ge(rows_step, (b + k + 1) * steps)
                        for c in range(DC):
                            last = nc.tensor.transpose(pt[:, k, c * P:(c + 1) * P], rows[:, k, c * P:(c + 1) * P], ident[:])
                        last.then_inc(pt_ready, 1)

            @block.scalar
            def _(act):
                act.sem_inc(out, 1)
                with act.Fori(0, NB // 2) as h:
                    b = h * 2
                    for k in range(2):
                        act.wait_ge(pt_ready, b + k + 2)
                        if scale is None:
                            nc.scalar.copy(xt[:, :, bass.ds((b + k) * P, P)],
                                           pt[:, k, 0:D].rearrange("p (c n) -> p c n", c=DC)).then_inc(out, 1)
                        else:
                            for c in range(DC):
                                last = nc.scalar.activation(xt[:, c, bass.ds((b + k) * P, P)], pt[:, k, c * P:(c + 1) * P],
                                                            ACT.Identity, bias=shift[:, c:c + 1], scale=scale[:, c:c + 1])
                            last.then_inc(out, 1)


def first_largest(nc, link, values, mask, best, tmp, order, shape):
    link(nc.vector.tensor_reduce(best, values, AX.X, ALU.max))
    link(nc.vector.tensor_tensor(mask, values, best.unsqueeze(len(shape) - 1).to_broadcast(shape), ALU.is_equal))
    link(nc.vector.tensor_tensor(mask, mask, order, ALU.mult))
    link(nc.vector.tensor_reduce(tmp, mask, AX.X, ALU.max))
    link(nc.vector.tensor_tensor(mask, order, tmp.unsqueeze(len(shape) - 1).to_broadcast(shape), ALU.is_equal))


def route_two(nc, st, xt, wr, br, order, ident, picks, shares):
    with ExitStack() as ctx:
        def sb(name, shape, dt=F32):
            return ctx.enter_context(nc.sbuf_tensor(f"ro_{name}", shape, dt))

        w = sb("w", [P, DC, EX])
        bias = sb("bias", [EX, 1])
        lines = sb("lines", [EX, 2, 2 * P])
        logits = sb("logits", [P, NB, EX])
        best = sb("best", [P, NB])
        next_best = sb("next_best", [P, NB])
        tmp = sb("tmp", [P, NB])
        pl = ctx.enter_context(nc.psum_tensor("ro_pl", [EX, 2, 512], F32))
        pt = ctx.enter_context(nc.psum_tensor("ro_pt", [P, 2, 512], F32))
        loaded = st.sem("ro_loaded")
        product = st.sem("ro_product")
        line_ready = st.sem("ro_line_ready")
        line_turned = st.sem("ro_line_turned")
        logits_out = st.sem("ro_logits_out")
        chain = st.sem("ro_chain")
        gap_ready = st.sem("ro_gap_ready")
        ratio_ready = st.sem("ro_ratio_ready")
        WINDOWS = NB // 2
        with nc.Block() as block:
            @block.sync
            def _(sp):
                sp.dma_start(w[:], wr.rearrange("(c p) e -> p c e", p=P)).then_inc(loaded, 16)
                sp.dma_start(bias[:], br.rearrange("(e a) -> e a", a=1)).then_inc(loaded, 16)

            @block.tensor
            def _(pe):
                pe.sem_inc(line_turned, 2)
                pe.wait_ge(loaded, 32)

                def product_of(window, u):
                    for c in range(DC):
                        last = nc.tensor.matmul(pl[:, u, 0:2 * P], w[:, c, :], xt[:, c, bass.ds(window * 2 * P, 2 * P)],
                                                start=(c == 0), stop=(c == DC - 1))
                    last.then_inc(product, 1)

                def turn_lines(window, u):
                    pe.wait_ge(logits_out, window + 1)
                    pe.wait_ge(line_ready, window + 2)
                    for j in range(2):
                        last = nc.tensor.matmul(pt[:, u, j * EX:(j + 1) * EX], lines[:, u, j * P:(j + 1) * P], ident[0:EX, 0:EX],
                                                start=True, stop=True)
                    last.then_inc(line_turned, 1)

                product_of(0, 0)
                with pe.Fori(0, WINDOWS // 2) as s:
                    for u in range(2):
                        window = s * 2 + u
                        pe.wait_ge(line_ready, window + 1)
                        product_of(window + 1, 1 - u)
                        turn_lines(window, u)
                turn_lines(WINDOWS - 1, 0)

            @block.scalar
            def _(act):
                act.sem_inc(line_ready, 1)
                act.wait_ge(loaded, 32)

                def line(window, u):
                    act.wait_ge(product, window + 1)
                    act.wait_ge(line_turned, window + 1)
                    nc.scalar.activation(lines[:, u, :], pl[:, u, 0:2 * P], ACT.Identity, bias=bias[:, 0:1]).then_inc(line_ready, 1)

                with act.Fori(0, WINDOWS // 2) as s:
                    for u in range(2):
                        line(s * 2 + u, u)
                line(WINDOWS - 1, 0)
                act.wait_ge(gap_ready, 1)
                nc.scalar.activation(tmp[:], next_best[:], ACT.Exp).then_inc(ratio_ready, 1)

            @block.vector
            def _(dve):
                dve.sem_inc(logits_out, 2)

                def out(window, u):
                    dve.wait_ge(line_turned, window + 3)
                    nc.vector.tensor_copy(logits[:, bass.ds(window * 2, 2), :],
                                          pt[:, u, 0:2 * EX].rearrange("p (j e) -> p j e", e=EX)).then_inc(logits_out, 1)

                with dve.Fori(0, WINDOWS // 2) as s:
                    for u in range(2):
                        out(s * 2 + u, u)
                out(WINDOWS - 1, 0)
                dve.wait_ge(logits_out, WINDOWS + 2)
                link = chained(dve, chain)
                shape = [P, NB, EX]
                order_b = order[:].unsqueeze(1).to_broadcast(shape)
                first_largest(nc, link, logits[:], picks[0][:], best[:], tmp[:], order_b, shape)
                link(nc.vector.scalar_tensor_tensor(out=logits[:], in0=picks[0][:], scalar=-BIG, in1=logits[:], op0=ALU.mult, op1=ALU.add))
                first_largest(nc, link, logits[:], picks[1][:], next_best[:], tmp[:], order_b, shape)
                nc.vector.tensor_tensor(next_best[:], next_best[:], best[:], ALU.subtract).then_inc(gap_ready, 1)
                dve.wait_ge(ratio_ready, 1)
                link(nc.vector.tensor_scalar(best[:], tmp[:], 1.0, None, ALU.add))
                link(nc.vector.reciprocal(shares[0][:], best[:]))
                link(nc.vector.tensor_tensor(shares[1][:], tmp[:], shares[0][:], ALU.mult))


def slots(nc, st, name, picks, scatter, gather, expert_of, ones, iota_part, before, tiles):
    listed = expert_of.shape[1]
    with ExitStack() as ctx:
        def sb(what, shape, dt=F32):
            return ctx.enter_context(nc.sbuf_tensor(f"{name}_{what}", shape, dt))

        node = sb("node", [P, NB])
        valid = sb("valid", [P, NB])
        tile_no = sb("tile_no", [P, listed])
        both = sb("both", [P, NB, EX])
        totals = sb("totals", [P, NB, EX])
        place = sb("place", [P, NB, EX])
        upto = sb("upto", [P, NB, EX])
        count = sb("count", [P, EX])
        count_int = sb("count_int", [P, EX], I32)
        ends = sb("ends", [P, EX])
        slot = sb("slot", [P, NB])
        aside = sb("aside", [P, NB])
        behind = sb("behind", [P, NB])
        moved = sb("moved", [P, NB])
        table = sb("table", [1, listed, EX])
        expert = sb("expert", [1, listed])
        ps = ctx.enter_context(nc.psum_tensor(f"{name}_ps", [P, 2, 512], F32))
        made = st.sem(f"{name}_made")
        chain = st.sem(f"{name}_chain")
        masks_ready = st.sem(f"{name}_masks_ready")
        summed = st.sem(f"{name}_summed")
        with nc.Block() as block:
            @block.gpsimd
            def _(pool):
                nc.gpsimd.iota(node[:], pattern=[[P, NB]], base=0, channel_multiplier=1,
                               allow_small_or_imprecise_dtypes=True).then_inc(made, 1)
                nc.gpsimd.iota(tile_no[:], pattern=[[1, listed]], base=0, channel_multiplier=0,
                               allow_small_or_imprecise_dtypes=True).then_inc(made, 1)

            @block.tensor
            def _(pe):
                pe.wait_ge(masks_ready, 1)
                flat = both[:].rearrange("p b e -> p (b e)")
                nc.tensor.matmul(ps[:, 0, 0:NB * EX], ones[:], flat, start=True, stop=True)
                nc.tensor.matmul(ps[:, 1, 0:NB * EX], before[:], flat, start=True, stop=True).then_inc(summed, 1)

            @block.vector
            def _(dve):
                link = chained(dve, chain)
                dve.wait_ge(made, 2)
                wide = [P, NB, EX]
                link(nc.vector.tensor_scalar(valid[:], node[:], float(N), None, ALU.is_lt))
                for pick in picks:
                    link(nc.vector.tensor_tensor(pick[:], pick[:], valid[:].unsqueeze(2).to_broadcast(wide), ALU.mult))
                if len(picks) == 2:
                    nc.vector.tensor_tensor(both[:], picks[0][:], picks[1][:], ALU.add).then_inc(masks_ready, 1)
                else:
                    nc.vector.tensor_copy(both[:], picks[0][:]).then_inc(masks_ready, 1)
                dve.wait_ge(summed, 1)
                view = lambda n: ps[:, n, 0:NB * EX].rearrange("p (b e) -> p b e", e=EX)
                link(nc.vector.tensor_copy(totals[:], view(0)))
                for e in range(EX):
                    link(nc.vector.tensor_tensor_scan(upto[:, :, e], ones[:, 0:NB], totals[:, :, e], 0.0, ALU.mult, ALU.add))
                link(nc.vector.tensor_tensor(place[:], view(1), upto[:], ALU.add))
                link(nc.vector.tensor_tensor(place[:], place[:], totals[:], ALU.subtract))
                link(nc.vector.tensor_scalar(count[:], upto[:, NB - 1, :], float(P - 1), None, ALU.add))
                link(nc.vector.tensor_copy(count_int[:], count[:]))
                link(nc.vector.tensor_scalar(count_int[:], count_int[:], 7, None, ALU.arith_shift_right))
                link(nc.vector.tensor_copy(count[:], count_int[:]))
                link(nc.vector.tensor_tensor_scan(ends[:], ones[:, 0:EX], count[:], 0.0, ALU.mult, ALU.add))
                link(nc.vector.tensor_tensor(count[:], ends[:], count[:], ALU.subtract))
                link(nc.vector.tensor_scalar(count[:], count[:], float(P), None, ALU.mult))
                link(nc.vector.tensor_tensor(place[:], place[:], count[:].unsqueeze(1).to_broadcast(wide), ALU.add))
                link(nc.vector.tensor_scalar(aside[:], valid[:], -1.0, 1.0, ALU.mult, ALU.add))
                link(nc.vector.tensor_scalar(behind[:], iota_part[:].to_broadcast([P, NB]), float(tiles * P), None, ALU.add))
                for k, pick in enumerate(picks):
                    link(nc.vector.tensor_tensor(upto[:], pick[:], place[:], ALU.mult))
                    link(nc.vector.tensor_reduce(slot[:], upto[:], AX.X, ALU.add))
                    link(nc.vector.tensor_copy(gather[k][:], slot[:]))
                    link(nc.vector.scalar_tensor_tensor(out=moved[:], in0=behind[:], scalar=float(k * P), in1=aside[:],
                                                        op0=ALU.add, op1=ALU.mult))
                    link(nc.vector.tensor_tensor(slot[:], slot[:], moved[:], ALU.add))
                    link(nc.vector.tensor_copy(scatter[k][:], slot[:]))
                link(nc.vector.tensor_tensor(table[:], ends[0:1, :].unsqueeze(1).to_broadcast([1, listed, EX]),
                                             tile_no[0:1, :].unsqueeze(2).to_broadcast([1, listed, EX]), ALU.is_le))
                link(nc.vector.tensor_reduce(expert[:], table[:], AX.X, ALU.add))
                link(nc.vector.tensor_scalar(expert[:], expert[:], float(EX - 1), None, ALU.min))
                link(nc.vector.tensor_copy(expert_of[:], expert[:]))


def scatter_rows(nc, st, name, x, affine, scatter, rows_dram):
    picks = len(scatter)
    steps = len(affine)
    RS = 7
    assert NX % RS == 0
    with ExitStack() as ctx:
        rows = ctx.enter_context(nc.sbuf_tensor(f"{name}_rows", [P, RS, D], F32))
        index = ctx.enter_context(nc.sbuf_tensor(f"{name}_index", [P, RS, picks], I32))
        step = st.sem(f"{name}_step")
        index_ready = st.sem(f"{name}_index_ready")
        left = [st.sem(f"{name}_left{k}") for k in range(RS)]
        with nc.Block() as block:
            @block.vector
            def _(dve):
                def norm(h, k, first=False):
                    b = h * RS + k
                    if not first:
                        dve.wait_ge(left[k], h * 16 * picks)
                    of = x[:, bass.ds(b, 1), :].rearrange("p a d -> p (a d)")
                    for n, (mean, rstd) in enumerate(affine):
                        if n:
                            dve.wait_ge(step, b * steps + n)
                        nc.vector.tensor_scalar(rows[:, k, :], of, mean[:, bass.ds(b, 1)], rstd[:, bass.ds(b, 1)],
                                                ALU.subtract, ALU.mult).then_inc(step, 1)
                        of = rows[:, k, :]

                for k in range(RS):
                    norm(0, k, first=True)
                with dve.Fori(1, NX // RS) as h:
                    for k in range(RS):
                        norm(h, k)

            @block.gpsimd
            def _(pool):
                def copy_index(b, k):
                    for j in range(picks):
                        nc.gpsimd.tensor_copy(index[:, k, j:j + 1], scatter[j][:, bass.ds(b, 1)]).then_inc(index_ready, 1)

                def send(h, k, first=False, last=False):
                    b = h * RS + k
                    pool.wait_ge(step, b * steps + steps)
                    pool.wait_ge(index_ready, b * picks + picks)
                    if k == RS - 1:
                        pool.wait_ge(left[0], h * 16 * picks + 16 * picks)
                    elif not first:
                        pool.wait_ge(left[k + 1], h * 16 * picks)
                    if not last:
                        copy_index(b + 1, (k + 1) % RS)
                    for j in range(picks):
                        nc.gpsimd.indirect_dma_start(
                            rows_dram, bass.IndirectOffsetOnAxis(ap=index[:, k, j:j + 1], axis=0),
                            rows[:, k, :], None).then_inc(left[k], 16)

                copy_index(0, 0)
                for k in range(RS):
                    send(0, k, first=True)
                with pool.Fori(1, NX // RS - 1) as h:
                    for k in range(RS):
                        send(h, k)
                for k in range(RS):
                    send(NX // RS - 1, k, last=(k == RS - 1))
                for k in range(RS):
                    pool.wait_ge(left[k], 16 * picks * (NX // RS))


def gather_rows(nc, st, name, y_dram, gather, shares, x):
    picks = len(gather)
    RD = 6
    LOOP = NX // RD
    assert NX == LOOP * RD + 1
    with ExitStack() as ctx:
        rows = ctx.enter_context(nc.sbuf_tensor(f"{name}_rows", [P, RD, picks, D], F32))
        index = ctx.enter_context(nc.sbuf_tensor(f"{name}_index", [P, RD, picks], I32))
        index_ready = st.sem(f"{name}_index_ready")
        came = [st.sem(f"{name}_came{k}") for k in range(RD)]
        added = st.sem(f"{name}_added")
        with nc.Block() as block:
            @block.gpsimd
            def _(pool):
                def copy_index(b, k):
                    for j in range(picks):
                        nc.gpsimd.tensor_copy(index[:, k, j:j + 1], gather[j][:, bass.ds(b, 1)]).then_inc(index_ready, 1)

                def fetch(s, k, first=False, last=False):
                    b = s * RD + k
                    pool.wait_ge(added, b * picks + picks)
                    pool.wait_ge(index_ready, b * picks + picks)
                    if k == RD - 1:
                        pool.wait_ge(came[0], s * 16 * picks + 16 * picks)
                    elif not first and not last:
                        pool.wait_ge(came[k + 1], s * 16 * picks)
                    if not last:
                        copy_index(b + 1, (k + 1) % RD)
                    for j in range(picks):
                        nc.gpsimd.indirect_dma_start(
                            rows[:, k, j, :], None, y_dram,
                            bass.IndirectOffsetOnAxis(ap=index[:, k, j:j + 1], axis=0)).then_inc(came[k], 16)

                copy_index(0, 0)
                for k in range(RD):
                    fetch(0, k, first=True)
                with pool.Fori(1, LOOP) as s:
                    for k in range(RD):
                        fetch(s, k)
                fetch(LOOP, 0, last=True)

            @block.vector
            def _(dve):
                dve.sem_inc(added, RD * picks)

                def add(s, k):
                    b = s * RD + k
                    dve.wait_ge(came[k], s * 16 * picks + 16 * picks)
                    to = x[:, bass.ds(b, 1), :].rearrange("p a d -> p (a d)")
                    for j in range(picks):
                        dve.wait_ge(added, b * picks + RD * picks + j)
                        nc.vector.scalar_tensor_tensor(out=to, in0=rows[:, k, j, :], scalar=shares[j][:, bass.ds(b, 1)],
                                                       in1=to, op0=ALU.mult, op1=ALU.add).then_inc(added, 1)

                with dve.Fori(0, LOOP) as s:
                    for k in range(RD):
                        add(s, k)
                add(LOOP, 0)


NX = FULL + 1
T1 = -(-2 * N // P) + EX - 1
T1 += T1 % 2
WINDOW = 4
LAG = 2
T2 = -(-N // P) + EX - 1
T2 += T2 % 2


def bias_rows(sp, to, of, sem):
    sp.dma_start(to, of.rearrange("e n -> (e n)").unsqueeze(0).to_broadcast([P, of.shape[0] * of.shape[1]])).then_inc(sem, 16)


def mixture_tiles(nc, st, rows_dram, y_dram, expert_of, w1, b1, w2, b2, gamma, beta, ident):
    H = w1.shape[2]
    HC = H // P
    with ExitStack() as ctx:
        def sb(name, shape, dt=F32):
            return ctx.enter_context(nc.sbuf_tensor(f"mx_{name}", shape, dt))

        w1_sb = sb("w1", [P, EX, DC, H])
        w2_sb = sb("w2", [P, EX, HC, D])
        b1_sb = sb("b1", [P, EX, H])
        b2_sb = sb("b2", [P, EX, D])
        rows = sb("rows", [P, 4, D])
        xt = sb("xt", [P, 2, D])
        raw = sb("raw", [P, 2, H])
        hidden = sb("hidden", [P, 2, H])
        hidden_t = sb("hidden_t", [P, 2, H])
        y = sb("y", [P, 2, D])
        px = ctx.enter_context(nc.psum_tensor("mx_px", [P, 512], F32))
        ph = ctx.enter_context(nc.psum_tensor("mx_ph", [P, 2, 512], F32))
        pt = ctx.enter_context(nc.psum_tensor("mx_pt", [P, 2, 512], F32))
        py = ctx.enter_context(nc.psum_tensor("mx_py", [P, 2, 512], F32))
        loaded = st.sem("mx_loaded")
        came = [st.sem(f"mx_came{k}") for k in range(4)]
        x_turned = st.sem("mx_x_turned")
        xt_ready = st.sem("mx_xt_ready")
        h_product = st.sem("mx_h_product")
        raw_ready = st.sem("mx_raw_ready")
        hidden_ready = st.sem("mx_hidden_ready")
        h_turned = st.sem("mx_h_turned")
        hidden_t_ready = st.sem("mx_hidden_t_ready")
        y_product = st.sem("mx_y_product")
        y_ready = st.sem("mx_y_ready")
        y_left = [st.sem(f"mx_y_left{k}") for k in range(2)]
        ROUNDS = (T1 - 2) // 4
        assert T1 == 4 * ROUNDS + 2
        with nc.Block() as block:
            @block.sync
            def _(sp):
                for e in range(EX):
                    sp.dma_start(w1_sb[:, e, :, :], w1[e].rearrange("(c p) h -> p c h", p=P)).then_inc(loaded, 16)
                    sp.dma_start(w2_sb[:, e, :, :], w2[e].rearrange("(c p) d -> p c d", p=P)).then_inc(loaded, 16)
                bias_rows(sp, b1_sb[:].rearrange("p e n -> p (e n)"), b1, loaded)
                bias_rows(sp, b2_sb[:].rearrange("p e n -> p (e n)"), b2, loaded)

                def fetch(i, k):
                    sp.dma_start(rows[:, k, :], rows_dram[bass.ds(i * P, P), :]).then_inc(came[k], 16)

                def store(i, k):
                    sp.wait_ge(y_ready, i + 1)
                    sp.dma_start(y_dram[bass.ds(i * P, P), :], y[:, k % 2, :]).then_inc(y_left[k % 2], 16)

                for k in range(4):
                    fetch(k, k)
                for i in range(4):
                    sp.wait_ge(x_turned, i + 1)
                    fetch(i + 4, i)
                    if i > 0:
                        store(i - 1, i - 1)
                with sp.Fori(1, ROUNDS) as s:
                    for k in range(4):
                        i = s * 4 + k
                        sp.wait_ge(x_turned, i + 1)
                        fetch(i + 4, k)
                        store(i - 1, (k + 3) % 4)
                for i in range(T1 - 2, T1 + 1):
                    store(i - 1, (i + 3) % 4)
                for k in range(4):
                    sp.wait_ge(came[k], 16 * (ROUNDS + 1))
                for k in range(2):
                    sp.wait_ge(y_left[k], 16 * (T1 // 2))

            @block.scalar
            def _(act):
                def spread_x(i, k, first=False):
                    if not first:
                        act.wait_ge(h_product, i - 1)
                    act.wait_ge(x_turned, i + 1)
                    for c in range(DC):
                        last = nc.scalar.activation(xt[:, k, c * P:(c + 1) * P], px[:, c * P:(c + 1) * P],
                                                    ACT.Identity, bias=beta[:, c:c + 1], scale=gamma[:, c:c + 1])
                    last.then_inc(xt_ready, 1)

                def gelu(i, k, first=False):
                    if not first:
                        act.wait_ge(h_turned, i - 1)
                    act.wait_ge(raw_ready, i + 1)
                    nc.scalar.activation(hidden[:, k, :], raw[:, k, :], ACT.Gelu).then_inc(hidden_ready, 1)

                def step(i, k, first=False, more=2):
                    if more > 0:
                        gelu(i + 1, 1 - k, first and i == 0)
                    if not first or i > 1:
                        act.wait_ge(y_product, i - 1)
                    act.wait_ge(h_turned, i + 1)
                    nc.scalar.copy(hidden_t[:, k, :], pt[:, k, :]).then_inc(hidden_t_ready, 1)
                    if more > 1:
                        spread_x(i + 2, k)

                spread_x(0, 0, True)
                spread_x(1, 1, True)
                gelu(0, 0, True)
                for i in range(4):
                    step(i, i % 2, first=True)
                with act.Fori(1, ROUNDS) as s:
                    for k in range(4):
                        step(s * 4 + k, k % 2)
                step(T1 - 2, 0, more=1)
                step(T1 - 1, 1, more=0)

            @block.vector
            def _(dve):
                dve.wait_ge(loaded, 16 * (2 * EX + 2))

                def add_b1(i, k, first=False):
                    e, = load_experts(nc, expert_of, i, mybir.EngineType.DVE)
                    if not first:
                        dve.wait_ge(hidden_ready, i - 1)
                    dve.wait_ge(h_product, i + 1)
                    nc.vector.tensor_tensor(raw[:, k, :], ph[:, k, :], b1_sb[:, bass.ds(e, 1), :].rearrange("p a n -> p (a n)"),
                                            ALU.add).then_inc(raw_ready, 1)

                def add_b2(i, k, left=None):
                    e, = load_experts(nc, expert_of, i, mybir.EngineType.DVE)
                    if left is not None:
                        dve.wait_ge(y_left[k], left * 16)
                    dve.wait_ge(y_product, i + 1)
                    nc.vector.tensor_tensor(y[:, k, :], py[:, k, 0:D], b2_sb[:, bass.ds(e, 1), :].rearrange("p a n -> p (a n)"),
                                            ALU.add).then_inc(y_ready, 1)

                add_b1(0, 0, True)
                for i in range(4):
                    add_b1(i + 1, (i + 1) % 2, i == 0)
                    if i > 0:
                        add_b2(i - 1, (i - 1) % 2, (i - 1) // 2 or None)
                with dve.Fori(1, ROUNDS) as s:
                    for k in range(4):
                        add_b1(s * 4 + k + 1, (k + 1) % 2)
                        add_b2(s * 4 + k - 1, (k + 1) % 2, s * 2 + (k - 1) // 2)
                add_b1(T1 - 1, 1)
                for i in range(T1 - 2, T1 + 1):
                    add_b2(i - 1, (i - 1) % 2, (i - 1) // 2)

            @block.tensor
            def _(pe):
                pe.wait_ge(loaded, 16 * (2 * EX + 2))

                def turn_rows(i, k, round_no):
                    if k or not isinstance(i, int) or i:
                        pe.wait_ge(xt_ready, i)
                    pe.wait_ge(came[k], round_no * 16 + 16)
                    for c in range(DC):
                        last = nc.tensor.transpose(px[:, c * P:(c + 1) * P], rows[:, k, c * P:(c + 1) * P], ident[:])
                    last.then_inc(x_turned, 1)

                def front(i, k, first=False):
                    e, = load_experts(nc, expert_of, i, mybir.EngineType.PE)
                    if not first:
                        pe.wait_ge(raw_ready, i - 1)
                    pe.wait_ge(xt_ready, i + 1)
                    for c in range(DC):
                        last = nc.tensor.matmul(ph[:, k, :], xt[:, k, c * P:(c + 1) * P],
                                                w1_sb[:, bass.ds(e, 1), c, :].rearrange("p a h -> p (a h)"),
                                                start=(c == 0), stop=(c == DC - 1))
                    last.then_inc(h_product, 1)

                def turn_hidden(i, k, first=False):
                    if not first:
                        pe.wait_ge(hidden_t_ready, i - 1)
                    pe.wait_ge(hidden_ready, i + 1)
                    for hc in range(HC):
                        last = nc.tensor.transpose(pt[:, k, hc * P:(hc + 1) * P], hidden[:, k, hc * P:(hc + 1) * P], ident[:])
                    last.then_inc(h_turned, 1)

                def back(i, k, first=False):
                    e, = load_experts(nc, expert_of, i, mybir.EngineType.PE)
                    if not first:
                        pe.wait_ge(y_ready, i - 1)
                    pe.wait_ge(hidden_t_ready, i + 1)
                    for hc in range(HC):
                        last = nc.tensor.matmul(py[:, k, 0:D], hidden_t[:, k, hc * P:(hc + 1) * P],
                                                w2_sb[:, bass.ds(e, 1), hc, :].rearrange("p a d -> p (a d)"),
                                                start=(hc == 0), stop=(hc == HC - 1))
                    last.then_inc(y_product, 1)

                turn_rows(0, 0, 0)
                front(0, 0, True)
                turn_rows(1, 1, 0)
                for i in range(4):
                    front(i + 1, (i + 1) % 2, i == 0)
                    turn_hidden(i, i % 2, i < 2)
                    turn_rows(i + 2, (i + 2) % 4, (i + 2) // 4)
                    if i > 0:
                        back(i - 1, (i - 1) % 2, i < 3)
                with pe.Fori(1, ROUNDS) as s:
                    for k in range(4):
                        i = s * 4 + k
                        front(i + 1, (k + 1) % 2)
                        turn_hidden(i, k % 2)
                        turn_rows(i + 2, (k + 2) % 4, s + (k + 2) // 4)
                        back(i - 1, (k + 1) % 2)
                front(T1 - 1, 1)
                turn_hidden(T1 - 2, 0)
                back(T1 - 3, 1)
                turn_hidden(T1 - 1, 1)
                back(T1 - 2, 0)
                back(T1 - 1, 1)


def load_experts(nc, expert_of, tile, engine, many=1):
    _, values = nc.values_load_multi_w_load_instructions(
        expert_of[0:1, bass.ds(tile, many)], engines=[engine], min_val=0, max_val=EX - 1,
        skip_runtime_bounds_check_because="slots caps the experts' numbers at EX - 1")
    return values


def gate_and_values(nc, st, xt, w1, b1, w2, b2, gcn_w, h_dram, ident, gate, h):
    R = w1.shape[1]
    assert R == P
    with ExitStack() as ctx:
        def sb(name, shape, dt=F32):
            return ctx.enter_context(nc.sbuf_tensor(f"ga_{name}", shape, dt))

        w1_sb, w2_sb, gw = sb("w1", [P, DC, R]), sb("w2", [R, D]), sb("gw", [P, DC])
        b1_sb, b2_sb = sb("b1", [P, 1]), sb("b2", [P, DC])
        total = sb("total", [P, DC])
        squeezed = sb("squeezed", [P, 1])
        gate_t = sb("gate_t", [P, DC])
        h_line = sb("h_line", [1, NB * P])
        h_rows = sb("h_rows", [NB, P])
        ph = ctx.enter_context(nc.psum_tensor("ga_ph", [1, 2, 512], F32))
        pg = ctx.enter_context(nc.psum_tensor("ga_pg", [P, 3, 512], F32))
        loaded = st.sem("ga_loaded")
        product = st.sem("ga_product")
        line_ready = st.sem("ga_line_ready")
        line_stored = st.sem("ga_line_stored")
        h_loaded = st.sem("ga_h_loaded")
        chain = st.sem("ga_chain")
        mean_ready = st.sem("ga_mean_ready")
        gate_psum = st.sem("ga_gate_psum")
        gate_step = st.sem("ga_gate_step")
        h_flat = h_dram.rearrange("n a -> (n a)")
        with nc.Block() as block:
            @block.sync
            def _(sp):
                sp.dma_start(w1_sb[:], w1.rearrange("(c p) r -> p c r", p=P)).then_inc(loaded, 16)
                sp.dma_start(w2_sb[:], w2).then_inc(loaded, 16)
                sp.dma_start(gw[:], gcn_w.rearrange("(c p) a -> p (c a)", p=P), allow_slow_non_contiguous=True).then_inc(loaded, 16)
                sp.dma_start(b1_sb[:], b1.rearrange("(p a) -> p a", a=1)).then_inc(loaded, 16)
                sp.dma_start(b2_sb[:], b2.rearrange("(c p) -> p c", p=P), allow_slow_non_contiguous=True).then_inc(loaded, 16)
                sp.wait_ge(line_ready, NB // 2 + 1)
                sp.dma_start(h_flat.rearrange("(a n) -> a n", a=1), h_line[:]).then_inc(line_stored, 16)
                sp.wait_ge(line_stored, 16)
                sp.dma_start(h_rows[:], h_flat.rearrange("(b n) -> b n", b=NB)).then_inc(h_loaded, 16)

            @block.tensor
            def _(pe):
                pe.wait_ge(loaded, 80)
                with pe.Fori(0, NB // 2) as s:
                    pe.wait_ge(line_ready, s + 1)
                    for c in range(DC):
                        last = nc.tensor.matmul(ph[:, 0, 0:2 * P], gw[:, c:c + 1], xt[:, c, bass.ds(s * 2 * P, 2 * P)],
                                                start=(c == 0), stop=(c == DC - 1))
                    last.then_inc(product, 1)
                pe.wait_ge(mean_ready, 1)
                for c in range(DC):
                    last = nc.tensor.matmul(pg[:, 0, 0:1], w1_sb[:, c, :], total[:, c:c + 1], start=(c == 0), stop=(c == DC - 1))
                last.then_inc(gate_psum, 1)
                pe.wait_ge(gate_step, 1)
                for c in range(DC):
                    last = nc.tensor.matmul(pg[:, 1, c:c + 1], w2_sb[:, c * P:(c + 1) * P], squeezed[:], start=True, stop=True)
                last.then_inc(gate_psum, 1)
                pe.wait_ge(gate_step, 2)
                for c in range(DC):
                    last = nc.tensor.matmul(pg[:, 2, c * P:(c + 1) * P], gate_t[:, c:c + 1].to_broadcast([P, P]), ident[:], start=True, stop=True)
                last.then_inc(gate_psum, 1)
                pe.wait_ge(h_loaded, 16)
                pe.wait_ge(gate_step, 3)
                nc.tensor.transpose(pg[:, 0, 0:NB], h_rows[:], ident[0:NB, 0:NB]).then_inc(gate_psum, 1)

            @block.scalar
            def _(act):
                act.sem_inc(line_ready, 1)
                with act.Fori(0, NB // 2) as s:
                    act.wait_ge(product, s + 1)
                    nc.scalar.copy(h_line[:, bass.ds(s * 2 * P, 2 * P)], ph[:, 0, 0:2 * P]).then_inc(line_ready, 1)
                act.wait_ge(loaded, 80)
                act.wait_ge(gate_psum, 1)
                nc.scalar.activation(squeezed[:], pg[:, 0, 0:1], ACT.Relu, bias=b1_sb[:, 0:1]).then_inc(gate_step, 1)
                act.wait_ge(gate_psum, 2)
                for c in range(DC):
                    last = nc.scalar.activation(gate_t[:, c:c + 1], pg[:, 1, c:c + 1], ACT.Sigmoid, bias=b2_sb[:, c:c + 1])
                last.then_inc(gate_step, 1)

            @block.vector
            def _(dve):
                link = chained(dve, chain)
                link(nc.vector.tensor_reduce(total[:], xt[:, :, 0:N], AX.X, ALU.add))
                nc.vector.tensor_scalar(total[:], total[:], 1.0 / N, None, ALU.mult).then_inc(mean_ready, 1)
                dve.wait_ge(gate_psum, 3)
                nc.vector.tensor_scalar(gate[:], pg[:, 2, 0:D], 1.0, None, ALU.add).then_inc(gate_step, 1)
                dve.wait_ge(gate_psum, 4)
                link(nc.vector.tensor_copy(h[:], pg[:, 0, 0:NB]))


def graph_values(nc, st, h, degree, dis, g, g_dram, ident):
    with ExitStack() as ctx:
        g_rows = ctx.enter_context(nc.sbuf_tensor("gv_rows", [NB, P], F32))
        root = ctx.enter_context(nc.sbuf_tensor("gv_root", [P, NB], F32))
        pt = ctx.enter_context(nc.psum_tensor("gv_pt", [P, 512], F32))
        chain = st.sem("gv_chain")
        more = st.sem("gv_more")
        rooted = st.sem("gv_rooted")
        g_ready = st.sem("gv_g_ready")
        turned = st.sem("gv_turned")
        rows_ready = st.sem("gv_rows_ready")
        stored = st.sem("gv_stored")
        with nc.Block() as block:
            @block.vector
            def _(dve):
                nc.vector.tensor_scalar(dis[:], degree[:], 1.0, None, ALU.add).then_inc(more, 1)
                dve.wait_ge(rooted, 1)
                link = chained(dve, chain)
                link(nc.vector.reciprocal(dis[:], root[:]))
                nc.vector.tensor_tensor(g[:], h[:], dis[:], ALU.mult).then_inc(g_ready, 1)
                dve.wait_ge(turned, 1)
                nc.vector.tensor_copy(g_rows[:], pt[0:NB, 0:P]).then_inc(rows_ready, 1)

            @block.scalar
            def _(act):
                act.wait_ge(more, 1)
                nc.scalar.activation(root[:], dis[:], ACT.Sqrt).then_inc(rooted, 1)

            @block.tensor
            def _(pe):
                pe.wait_ge(g_ready, 1)
                nc.tensor.transpose(pt[0:NB, 0:P], g[:], ident[:]).then_inc(turned, 1)

            @block.sync
            def _(sp):
                sp.wait_ge(rows_ready, 1)
                sp.dma_start(g_dram.rearrange("(b n) a -> b (n a)", b=NB), g_rows[:]).then_inc(stored, 16)
                sp.wait_ge(stored, 16)


def value_of_rows(nc, st, count, g, g_dram, rows_dram, placed_dram, ones, before, weight):
    with ExitStack() as ctx:
        def sb(name, shape, dt=F32):
            return ctx.enter_context(nc.sbuf_tensor(f"vr_{name}", shape, dt))

        aside = sb("aside", [P, NB])
        upto = sb("upto", [P, NB])
        totals = sb("totals", [P, NB])
        has = sb("has", [P, NB])
        start = sb("start", [P, NB])
        index = sb("index", [P, NB], I32)
        rows_int = sb("rows_int", [RP, RE], I32)
        rows = sb("rows", [RP, RE])
        same = sb("same", [RP, RE])
        placed = sb("placed", [RP, RE])
        carried = sb("carried", [RP, 1])
        ps = ctx.enter_context(nc.psum_tensor("vr_ps", [P, 2, 512], F32))
        made = st.sem("vr_made")
        summed = st.sem("vr_summed")
        chain = st.sem("vr_chain")
        index_ready = st.sem("vr_index_ready")
        rows_loaded = st.sem("vr_rows_loaded")
        scattered = st.sem("vr_scattered")
        carried_came = st.sem("vr_carried_came")
        placed_loaded = st.sem("vr_placed_loaded")
        with nc.Block() as block:
            @block.tensor
            def _(pe):
                nc.tensor.matmul(ps[:, 0, 0:NB], ones[:], count[:], start=True, stop=True)
                nc.tensor.matmul(ps[:, 1, 0:NB], before[:], count[:], start=True, stop=True).then_inc(summed, 1)

            @block.sync
            def _(sp):
                sp.dma_start(rows_int[:], rows_dram.rearrange("t e -> (t e)")[0:E].rearrange("(p e) -> p e", p=RP)).then_inc(rows_loaded, 16)
                sp.wait_ge(scattered, 16 * NX)
                sp.dma_start(placed[:], placed_dram.rearrange("n a -> (n a)")[0:E].rearrange("(p e) -> p e", p=RP)).then_inc(placed_loaded, 16)

            @block.gpsimd
            def _(pool):
                nc.gpsimd.iota(aside[:], pattern=[[P, NB]], base=E, channel_multiplier=1,
                               allow_small_or_imprecise_dtypes=True).then_inc(made, 1)
                pool.wait_ge(rows_loaded, 16)
                nc.gpsimd.indirect_dma_start(carried[:], None, g_dram,
                                             bass.IndirectOffsetOnAxis(ap=rows_int[:, 0:1], axis=0)).then_inc(carried_came, 16)
                pool.wait_ge(index_ready, 1)
                for b in range(NX):
                    nc.gpsimd.indirect_dma_start(placed_dram, bass.IndirectOffsetOnAxis(ap=index[:, b:b + 1], axis=0),
                                                 g[:, b:b + 1], None).then_inc(scattered, 16)
                pool.wait_ge(scattered, 16 * NX)

            @block.vector
            def _(dve):
                link = chained(dve, chain)
                dve.wait_ge(made, 1)
                dve.wait_ge(summed, 1)
                link(nc.vector.tensor_copy(totals[:], ps[:, 0, 0:NB]))
                link(nc.vector.tensor_tensor_scan(upto[:], ones[:, 0:NB], totals[:], 0.0, ALU.mult, ALU.add))
                link(nc.vector.tensor_tensor(start[:], upto[:], totals[:], ALU.subtract))
                link(nc.vector.tensor_tensor(start[:], start[:], ps[:, 1, 0:NB], ALU.add))
                link(nc.vector.tensor_scalar(has[:], count[:], 0.0, None, ALU.is_gt))
                link(nc.vector.tensor_tensor(start[:], start[:], aside[:], ALU.subtract))
                link(nc.vector.tensor_tensor(start[:], start[:], has[:], ALU.mult))
                link(nc.vector.tensor_tensor(start[:], start[:], aside[:], ALU.add))
                nc.vector.tensor_copy(index[:], start[:]).then_inc(index_ready, 1)
                link(nc.vector.memset(weight[:], 0.0))
                dve.wait_ge(rows_loaded, 16)
                link(nc.vector.tensor_copy(rows[:], rows_int[:]))
                link(nc.vector.memset(same[:, 0:1], 0.0))
                link(nc.vector.tensor_tensor(same[:, 1:RE], rows[:, 1:RE], rows[:, 0:RE - 1], ALU.is_equal))
                dve.wait_ge(carried_came, 16)
                dve.wait_ge(placed_loaded, 16)
                link(nc.vector.tensor_copy(placed[:, 0:1], carried[:]))
                link(nc.vector.tensor_tensor_scan(weight[0:RP, 0:RE], same[:], placed[:], 0.0, ALU.mult, ALU.add))


def scatter_to_columns(nc, st, name, weight, col_lo, col_hi, iota_free, ident, sums):
    with ExitStack() as ctx:
        def sb(what, shape, dt=F32):
            return ctx.enter_context(nc.sbuf_tensor(f"{name}_{what}", shape, dt))

        low = sb("low", [P, 2, GROUP, P])
        high = sb("high", [P, 2, GROUP, NB])
        zero = sb("zero", [P, P])
        rows = sb("rows", [NB, P])
        table = ctx.enter_context(nc.psum_tensor(f"{name}_table", [P, 512], F32))
        turned = ctx.enter_context(nc.psum_tensor(f"{name}_turned", [P, 512], F32))
        zeroed = st.sem(f"{name}_zeroed")
        chosen = st.sem(f"{name}_chosen")
        ready = st.sem(f"{name}_ready")
        used = st.sem(f"{name}_used")
        out = st.sem(f"{name}_out")
        GROUPS = NI // GROUP
        with nc.Block() as block:
            @block.tensor
            def _(pe):
                pe.sem_inc(used, 2)
                pe.wait_ge(zeroed, 1)
                nc.tensor.matmul(table[0:NB, 0:P], zero[:, 0:NB], zero[:], start=True, stop=False)
                with pe.Fori(0, GROUPS // 2) as s:
                    for u in range(2):
                        pe.wait_ge(ready, s * 4 + 2 * u + 2)
                        for j in range(GROUP):
                            last = nc.tensor.matmul(table[0:NB, 0:P], high[:, u, j, :], low[:, u, j, :], start=False, stop=False)
                        last.then_inc(used, 1)
                nc.tensor.matmul(table[0:NB, 0:P], zero[:, 0:NB], zero[:], start=False, stop=True).then_inc(used, 1)
                pe.wait_ge(out, 1)
                nc.tensor.transpose(turned[:, 0:NB], rows[:], ident[0:NB, 0:NB]).then_inc(used, 1)

            @block.vector
            def _(dve):
                nc.vector.memset(zero[:], 0.0).then_inc(zeroed, 1)
                with dve.Fori(0, GROUPS // 2) as s:
                    for u in range(2):
                        q = s * 2 + u
                        at = bass.ds(q * GROUP, GROUP)
                        wide, narrow = [P, GROUP, P], [P, GROUP, NB]
                        dve.wait_ge(used, q + 1)
                        nc.vector.tensor_tensor(high[:, u, :, :], iota_free[:, 0:NB].unsqueeze(1).to_broadcast(narrow),
                                                col_hi[:, at].unsqueeze(2).to_broadcast(narrow), ALU.is_equal).then_inc(chosen, 1)
                        nc.vector.tensor_tensor(low[:, u, :, :], iota_free[:].unsqueeze(1).to_broadcast(wide),
                                                col_lo[:, at].unsqueeze(2).to_broadcast(wide), ALU.is_equal).then_inc(ready, 1)
                        dve.wait_ge(chosen, q + 1)
                        nc.vector.tensor_tensor(high[:, u, :, :], high[:, u, :, :],
                                                weight[:, at].unsqueeze(2).to_broadcast(narrow), ALU.mult).then_inc(ready, 1)
                dve.wait_ge(used, GROUPS + 3)
                nc.vector.tensor_copy(rows[:], table[0:NB, 0:P]).then_inc(out, 1)
                dve.wait_ge(used, GROUPS + 4)
                nc.vector.tensor_copy(sums[:], turned[:, 0:NB]).then_inc(out, 1)


def split_columns(nc, st, name, cols_dram, col_lo, col_hi):
    with ExitStack() as ctx:
        whole = ctx.enter_context(nc.sbuf_tensor(f"{name}_whole", [RP, RE], I32))
        high = ctx.enter_context(nc.sbuf_tensor(f"{name}_high", [RP, RE], I32))
        loaded = st.sem(f"{name}_loaded")
        chain = st.sem(f"{name}_chain")
        with nc.Block() as block:
            @block.sync
            def _(sp):
                sp.dma_start(whole[:], cols_dram.rearrange("t e -> (t e)")[0:E].rearrange("(p e) -> p e", p=RP)).then_inc(loaded, 16)

            @block.vector
            def _(dve):
                link = chained(dve, chain)
                link(nc.vector.memset(col_lo[:], 0.0))
                link(nc.vector.memset(col_hi[:], float(P)))
                dve.wait_ge(loaded, 16)
                link(nc.vector.tensor_scalar(high[:], whole[:], 7, None, ALU.arith_shift_right))
                link(nc.vector.tensor_copy(col_hi[0:RP, 0:RE], high[:]))
                link(nc.vector.tensor_scalar(high[:], whole[:], P - 1, None, ALU.bitwise_and))
                link(nc.vector.tensor_copy(col_lo[0:RP, 0:RE], high[:]))


def gated_update(nc, st, x, mean, rstd, dis, g, sums, gcn_b, gate):
    with ExitStack() as ctx:
        def sb(name, shape, dt=F32):
            return ctx.enter_context(nc.sbuf_tensor(f"gu_{name}", shape, dt))

        bias = sb("bias", [P, 1])
        pre = sb("pre", [P, NB])
        spatial = sb("spatial", [P, NB])
        rows = sb("rows", [P, 2, D])
        factor = sb("factor", [P, 2, D])
        loaded = st.sem("gu_loaded")
        chain = st.sem("gu_chain")
        pre_ready = st.sem("gu_pre_ready")
        spatial_ready = st.sem("gu_spatial_ready")
        factor_ready = st.sem("gu_factor_ready")
        step = st.sem("gu_step")
        with nc.Block() as block:
            @block.sync
            def _(sp):
                sp.dma_start(bias[:], gcn_b.rearrange("(a n) -> a n", a=1).to_broadcast([P, 1])).then_inc(loaded, 16)

            @block.scalar
            def _(act):
                act.wait_ge(loaded, 16)
                act.wait_ge(pre_ready, 1)
                nc.scalar.activation(spatial[:], pre[:], ACT.Sigmoid, bias=bias[:, 0:1]).then_inc(spatial_ready, 1)
                act.wait_ge(spatial_ready, 1)
                with act.Fori(0, NB // 2) as h:
                    for k in range(2):
                        b = h * 2 + k
                        act.wait_ge(step, h * 6 + 1)
                        nc.scalar.activation(factor[:, k, :], gate[:], ACT.Identity, bias=spatial[:, bass.ds(b, 1)]).then_inc(factor_ready, 1)

            @block.vector
            def _(dve):
                dve.sem_inc(step, 1)
                link = chained(dve, chain)
                link(nc.vector.tensor_tensor(pre[:], sums[:], g[:], ALU.add))
                nc.vector.tensor_tensor(pre[:], pre[:], dis[:], ALU.mult).then_inc(pre_ready, 1)
                with dve.Fori(0, NB // 2) as h:
                    for k in range(2):
                        b = h * 2 + k
                        of = x[:, bass.ds(b, 1), :].rearrange("p a d -> p (a d)")
                        nc.vector.tensor_scalar(rows[:, k, :], of, mean[:, bass.ds(b, 1)], rstd[:, bass.ds(b, 1)],
                                                ALU.subtract, ALU.mult).then_inc(step, 1)
                        dve.wait_ge(factor_ready, b + 1)
                        dve.wait_ge(step, b * 3 + 2)
                        nc.vector.tensor_tensor(rows[:, k, :], rows[:, k, :], factor[:, k, :], ALU.mult).then_inc(step, 1)
                        dve.wait_ge(step, b * 3 + 3)
                        nc.vector.tensor_tensor(of, of, rows[:, k, :], ALU.add).then_inc(step, 1)


def route_one(nc, st, xt, w1_sb, b1_sb, wg, bg, order, ident, pick, share, experts, fetched):
    HC = b1_sb.shape[1]
    with ExitStack() as ctx:
        def sb(name, shape, dt=F32):
            return ctx.enter_context(nc.sbuf_tensor(f"r1_{name}", shape, dt))

        wg_sb = sb("wg", [P, HC, EX])
        bg_sb = sb("bg", [EX, 1])
        hidden = sb("hidden", [P, 4, WINDOW * P])
        lines = sb("lines", [EX, WINDOW * P])
        logits = sb("logits", [P, NB, EX])
        best = sb("best", [P, NB])
        tmp = sb("tmp", [P, NB])
        ph = ctx.enter_context(nc.psum_tensor("r1_ph", [P, 4, 512], F32))
        pl = ctx.enter_context(nc.psum_tensor("r1_pl", [EX, 512], F32))
        pt = ctx.enter_context(nc.psum_tensor("r1_pt", [P, 512], F32))
        loaded = st.sem("r1_loaded")
        h_product = st.sem("r1_h_product")
        h_ready = st.sem("r1_h_ready")
        h_used = st.sem("r1_h_used")
        lines_ready = st.sem("r1_lines_ready")
        lines_turned = st.sem("r1_lines_turned")
        logits_out = st.sem("r1_logits_out")
        chain = st.sem("r1_chain")
        shift_ready = st.sem("r1_shift_ready")
        exps_ready = st.sem("r1_exps_ready")
        WINDOWS, REST = NB // WINDOW, NB % WINDOW
        with nc.Block() as block:
            @block.sync
            def _(sp):
                sp.dma_start(wg_sb[:], wg.rearrange("(c p) e -> p c e", p=P)).then_inc(loaded, 16)
                sp.dma_start(bg_sb[:], bg.rearrange("(e a) -> e a", a=1)).then_inc(loaded, 16)
                for to, of in experts:
                    sp.dma_start(to, of).then_inc(fetched, 16)

            @block.tensor
            def _(pe):
                pe.sem_inc(h_used, 4)
                pe.wait_ge(loaded, 32)

                def hidden_parts(s, many, turned=True):
                    def logit_part(hc):
                        pe.wait_ge(h_ready, s * HC + hc + 5)
                        nc.tensor.matmul(pl[:, 0:many * P], wg_sb[:, hc, :], hidden[:, hc % 4, 0:many * P],
                                         start=(hc == 0), stop=(hc == HC - 1)).then_inc(h_used, 1)

                    for hc in range(HC):
                        pe.wait_ge(h_ready, s * HC + hc + 1)
                        for c in range(DC):
                            last = nc.tensor.matmul(ph[:, hc % 4, 0:many * P], w1_sb[:, c, hc * P:(hc + 1) * P],
                                                    xt[:, c, bass.ds(s * WINDOW * P, many * P)],
                                                    start=(c == 0), stop=(c == DC - 1))
                        last.then_inc(h_product, 1)
                        if hc == LAG - 1 and turned:
                            turn_lines(s - 1, WINDOW)
                        if hc >= LAG:
                            logit_part(hc - LAG)
                    for hc in range(HC - LAG, HC):
                        logit_part(hc)

                def turn_lines(s, many):
                    pe.wait_ge(lines_ready, s + 1)
                    pe.wait_ge(logits_out, s + 1)
                    for j in range(many):
                        last = nc.tensor.matmul(pt[:, j * EX:(j + 1) * EX], lines[:, j * P:(j + 1) * P], ident[0:EX, 0:EX],
                                                start=True, stop=True)
                    last.then_inc(lines_turned, 1)

                hidden_parts(0, WINDOW, turned=False)
                with pe.Fori(1, WINDOWS) as s:
                    hidden_parts(s, WINDOW)
                hidden_parts(WINDOWS, REST)
                turn_lines(WINDOWS, REST)

            @block.scalar
            def _(act):
                act.sem_inc(h_ready, 4)
                act.wait_ge(loaded, 32)

                def window(s, many, first=False):
                    for hc in range(HC):
                        act.wait_ge(h_used, s * HC + hc + 1)
                        act.wait_ge(h_product, s * HC + hc + 1)
                        nc.scalar.activation(hidden[:, hc % 4, 0:many * P], ph[:, hc % 4, 0:many * P], ACT.Gelu,
                                             bias=b1_sb[:, hc:hc + 1]).then_inc(h_ready, 1)
                    if not first:
                        act.wait_ge(lines_turned, s)
                    act.wait_ge(h_used, s * HC + HC + 4)
                    nc.scalar.activation(lines[:, 0:many * P], pl[:, 0:many * P], ACT.Identity, bias=bg_sb[:, 0:1]).then_inc(lines_ready, 1)

                window(0, WINDOW, first=True)
                with act.Fori(1, WINDOWS) as s:
                    window(s, WINDOW)
                window(WINDOWS, REST)
                act.wait_ge(shift_ready, 1)
                nc.scalar.activation(logits[:], logits[:], ACT.Exp).then_inc(exps_ready, 1)

            @block.vector
            def _(dve):
                dve.sem_inc(logits_out, 1)

                def out(s, many):
                    dve.wait_ge(lines_turned, s + 1)
                    nc.vector.tensor_copy(logits[:, bass.ds(s * WINDOW, many), :],
                                          pt[:, 0:many * EX].rearrange("p (j e) -> p j e", e=EX)).then_inc(logits_out, 1)

                with dve.Fori(0, WINDOWS) as s:
                    out(s, WINDOW)
                out(WINDOWS, REST)
                dve.wait_ge(logits_out, WINDOWS + 2)
                link = chained(dve, chain)
                shape = [P, NB, EX]
                order_b = order[:].unsqueeze(1).to_broadcast(shape)
                link(nc.vector.tensor_reduce(best[:], logits[:], AX.X, ALU.max))
                nc.vector.tensor_tensor(logits[:], logits[:], best[:].unsqueeze(2).to_broadcast(shape), ALU.subtract).then_inc(shift_ready, 1)
                dve.wait_ge(exps_ready, 1)
                first_largest(nc, link, logits[:], pick[:], best[:], tmp[:], order_b, shape)
                link(nc.vector.tensor_reduce(tmp[:], logits[:], AX.X, ALU.add))
                link(nc.vector.reciprocal(share[:], tmp[:]))
                link(nc.vector.tensor_tensor(share[:], share[:], best[:], ALU.mult))


def routed_tiles(nc, st, rows_dram, y_dram, expert_of, w1_sb, b1_sb, wd_sb, bd_sb, loaded, ident):
    HC = b1_sb.shape[1]
    STEPS = T2 // 2
    PH = 2
    assert STEPS % 2 == 0
    with ExitStack() as ctx:
        def sb(name, shape, dt=F32):
            return ctx.enter_context(nc.sbuf_tensor(f"rt_{name}", shape, dt))

        rows = sb("rows", [P, 2, 2, D])
        xt = sb("xt", [P, 2, DC, 2 * P])
        hidden = sb("hidden", [P, HC, 2 * P])
        y = sb("y", [P, 2, 2, D])
        px = ctx.enter_context(nc.psum_tensor("rt_px", [P, DC, 2 * P], F32))
        ph = ctx.enter_context(nc.psum_tensor("rt_ph", [P, PH, 512], F32))
        py = ctx.enter_context(nc.psum_tensor("rt_py", [P, 2, 2, 512], F32))
        came = [st.sem(f"rt_came{u}") for u in range(2)]
        turned = st.sem("rt_turned")
        xt_ready = st.sem("rt_xt_ready")
        h_product = st.sem("rt_h_product")
        h_ready = st.sem("rt_h_ready")
        h_used = st.sem("rt_h_used")
        y_ready = st.sem("rt_y_ready")
        y_left = [st.sem(f"rt_y_left{u}") for u in range(2)]
        tiles = rows_dram.rearrange("(t p) d -> p t d", p=P)
        y_tiles = y_dram.rearrange("(t p) d -> p t d", p=P)
        with nc.Block() as block:
            @block.sync
            def _(sp):
                def fetch(s, u):
                    sp.dma_start(rows[:, u, :, :], tiles[:, bass.ds(s * 2, 2), :]).then_inc(came[u], 16)

                def step(s, u, more=True):
                    if more:
                        sp.wait_ge(turned, s + 1)
                        fetch(s + 2, u)
                    sp.wait_ge(y_ready, s * 2 + 6)
                    sp.dma_start(y_tiles[:, bass.ds(s * 2, 2), :], y[:, u, :, :]).then_inc(y_left[u], 16)

                for u in range(2):
                    fetch(u, u)
                with sp.Fori(0, STEPS // 2 - 1) as v:
                    for u in range(2):
                        step(v * 2 + u, u)
                for u in range(2):
                    step(STEPS - 2 + u, u, more=False)
                for u in range(2):
                    sp.wait_ge(y_left[u], 16 * (STEPS // 2))

            @block.tensor
            def _(pe):
                pe.sem_inc(h_used, HC)
                pe.wait_ge(loaded, 16 * (EX + 1))

                def turn_rows(s, u, v, first=False):
                    if not first:
                        pe.wait_ge(xt_ready, s)
                    pe.wait_ge(came[u], v * 16 + 16)
                    for c in range(DC):
                        for k in range(2):
                            last = nc.tensor.transpose(px[:, c, k * P:(k + 1) * P], rows[:, u, k, c * P:(c + 1) * P], ident[:])
                    last.then_inc(turned, 1)

                def step(s, u, v, more=True):
                    experts = load_experts(nc, expert_of, s * 2, mybir.EngineType.PE, many=2)

                    def y_part(hc):
                        pe.wait_ge(h_ready, s * HC + hc + PH + 1)
                        for k in range(2):
                            last = nc.tensor.matmul(py[:, u, k, 0:D], hidden[:, hc, k * P:(k + 1) * P],
                                                    wd_sb[:, bass.ds(experts[k], 1), hc, :].rearrange("p a d -> p (a d)"),
                                                    start=(hc == 0), stop=(hc == HC - 1))
                        last.then_inc(h_used, 1)

                    pe.wait_ge(xt_ready, s + 1)
                    pe.wait_ge(y_ready, s * 2 + 2)
                    for hc in range(HC):
                        pe.wait_ge(h_ready, s * HC + hc + 1)
                        for c in range(DC):
                            last = nc.tensor.matmul(ph[:, hc % PH, 0:2 * P], w1_sb[:, c, hc * P:(hc + 1) * P],
                                                    xt[:, u, c, :], start=(c == 0), stop=(c == DC - 1))
                        last.then_inc(h_product, 1)
                        if hc >= LAG:
                            y_part(hc - LAG)
                        if more and hc == HC // 2:
                            turn_rows(s + 1, 1 - u, v + u)
                    for hc in range(HC - LAG, HC):
                        y_part(hc)

                turn_rows(0, 0, 0, first=True)
                with pe.Fori(0, STEPS // 2 - 1) as v:
                    for u in range(2):
                        step(v * 2 + u, u, v)
                step(STEPS - 2, 0, STEPS // 2 - 1)
                step(STEPS - 1, 1, STEPS // 2 - 1, more=False)

            @block.scalar
            def _(act):
                act.sem_inc(h_ready, PH)
                with act.Fori(0, STEPS) as s:
                    for hc in range(HC):
                        act.wait_ge(h_used, s * HC + hc + 1)
                        act.wait_ge(h_product, s * HC + hc + 1)
                        nc.scalar.activation(hidden[:, hc, :], ph[:, hc % PH, 0:2 * P], ACT.Gelu, bias=b1_sb[:, hc:hc + 1]).then_inc(h_ready, 1)

            @block.vector
            def _(dve):
                dve.sem_inc(y_ready, 4)
                dve.wait_ge(loaded, 16 * (EX + 1))

                def copy_xt(s, u, first=False):
                    if not first:
                        dve.wait_ge(h_product, s * HC - HC)
                    dve.wait_ge(turned, s + 1)
                    nc.vector.tensor_copy(xt[:, u, :, :], px[:]).then_inc(xt_ready, 1)

                def step(s, u, v=None, first=False, more=True):
                    if more:
                        copy_xt(s + 1, 1 - u, first and s == 0)
                    experts = load_experts(nc, expert_of, s * 2, mybir.EngineType.DVE, many=2)
                    if not first:
                        dve.wait_ge(y_left[u], v * 16)
                    dve.wait_ge(h_used, s * HC + 2 * HC)
                    for k in range(2):
                        nc.vector.tensor_tensor(y[:, u, k, :], py[:, u, k, 0:D],
                                                bd_sb[:, bass.ds(experts[k], 1), :].rearrange("p a d -> p (a d)"),
                                                ALU.add).then_inc(y_ready, 1)

                copy_xt(0, 0, first=True)
                for u in range(2):
                    step(u, u, first=True)
                with dve.Fori(1, STEPS // 2 - 1) as v:
                    for u in range(2):
                        step(v * 2 + u, u, v)
                step(STEPS - 2, 0, STEPS // 2 - 1)
                step(STEPS - 1, 1, STEPS // 2 - 1, more=False)


def move(nc, st, name, pairs):
    moved = st.sem(f"{name}_moved")
    with nc.Block() as block:
        @block.sync
        def _(sp):
            for to, of in pairs:
                sp.dma_start(to, of).then_inc(moved, 16)
            sp.wait_ge(moved, 16 * len(pairs))


def load_columns(nc, st, name, pairs):
    moved = st.sem(f"{name}_moved")
    with nc.Block() as block:
        @block.sync
        def _(sp):
            for to, of in pairs:
                sp.dma_start(to, of.rearrange("(c p) -> p c", p=P), allow_slow_non_contiguous=True).then_inc(moved, 16)
            sp.wait_ge(moved, 16 * len(pairs))


def build(nc, a, out):
    st = Stage(nc)
    keep = st.keep

    def dram(name, shape, dt=F32):
        return nc.dram_tensor(name, shape, dt, kind="Internal").ap()

    q_dram, k_dram, v_dram = (dram(f"{n}_table", (NB * P, D)) for n in "qkv")
    scratch = {"rows": dram("edge_rows", (SL, P), I32), "cols": dram("edge_cols", (SL, P), I32),
               "item_block": dram("item_block", (NI,), I32), "keys": dram("item_keys", (NI, P), I16)}
    placed_dram = dram("placed_values", (P * SL, 1))
    bounce = [dram(f"bounce{n}", (P, 1)) for n in range(2)]
    h_dram, g_dram = dram("h_values", (NB * P, 1)), dram("g_values", (NB * P, 1))

    def sb(ctx, name, shape, dt=F32):
        return ctx.enter_context(nc.sbuf_tensor(name, shape, dt))

    ident, before = sb(keep, "ident", [P, P]), sb(keep, "before", [P, P])
    iota_free, iota_part = sb(keep, "iota_free", [P, P]), sb(keep, "iota_part", [P, 1])
    ones, order = sb(keep, "ones", [P, P]), sb(keep, "order", [P, EX])
    stats, tmp = sb(keep, "stats", [P, NB, 6]), sb(keep, "ln_tmp", [P, NB])
    mean, rstd = sb(keep, "mean", [P, NB]), sb(keep, "rstd", [P, NB])
    mean2, rstd2 = sb(keep, "mean2", [P, NB]), sb(keep, "rstd2", [P, NB])
    degree, row_edges = sb(keep, "degree", [P, NB]), sb(keep, "row_edges", [P, NB])
    zero = sb(keep, "zero", [P, D])
    constants(nc, st, ident, before, iota_free, iota_part, ones, zero, order)
    rows_dram = [dram("mixture_rows", ((T1 + 2) * P, D)), dram("routed_rows", ((T2 + 1) * P, D))]

    with ExitStack() as ctx:
        rel, col = sb(ctx, "rel", [P, NI + 2 * QUAD]), sb(ctx, "col", [P, NI + QUAD], I32)
        item_block = sb(ctx, "item_block_sb", [1, NI], I32)
        row_blocks = sb(ctx, "row_blocks", [P, SL], BF16)
        with ExitStack() as nodes:
            x, nshift = sb(nodes, "x_first", [P, NB, D]), sb(nodes, "nshift", [P, NB])
            load_x(nc, st, "x_first", a["x"], x)
            layernorm_stats(nc, st, "ln_attention", x, stats, mean, rstd, tmp)
            cleared = st.sem("cleared")
            clears = [*rows_dram, placed_dram.rearrange("(n d) a -> n (d a)", d=D)]
            clears = [(to.rearrange("(t p) d -> p t d", p=P), zero[:].unsqueeze(1).to_broadcast([P, to.shape[0] // P, D]))
                      for to in clears]
            shifted = st.sem("nshift_made")
            with nc.Block() as block:
                @block.vector
                def _(dve):
                    nc.vector.scalar_tensor_tensor(out=nshift[:], in0=mean[:], scalar=-1.0, in1=rstd[:],
                                                   op0=ALU.mult, op1=ALU.mult).then_inc(shifted, 1)
            projection = Projection(nc, st, nodes, x, nshift, rstd, ident, ones, [a[f"L0_gnn_W{n}"] for n in "qkv"],
                                    [a[f"L0_gnn_b{n}"] for n in "qkv"], (q_dram, k_dram, v_dram), clears, cleared)
            sort_edges(nc, st, a["src"], a["dst"], scratch, row_blocks, ident, iota_part, projection)
        scores = sb(ctx, "scores", [P, NI, HEADS])
        with ExitStack() as queries:
            q_all = sb(queries, "q_all", [P, NB, D])
            item_tables(nc, st, row_blocks, scratch, ident, ones, rel, col, q_all, q_dram, cleared)
            move(nc, st, "items", [(item_block[:], scratch["item_block"].rearrange("(a i) -> a i", a=1))])
            col_lo, col_hi = sb(queries, "col_lo", [P, NI]), sb(queries, "col_hi", [P, NI])
            split_columns(nc, st, "split", scratch["cols"], col_lo, col_hi)
            edge_scores(nc, st, q_all, k_dram, rel, col, col_lo, col_hi, item_block, iota_free, ident, scores, degree)
        softmax_over_rows(nc, st, scores, scratch["keys"], bounce, ident)
        acc = sb(ctx, "acc", [P, NB, AW])
        aggregate(nc, st, scores, v_dram, rel, col, item_block, iota_free, acc)
        copied = st.sem("row_edges_copied")
        with nc.Block() as block:
            @block.vector
            def _(dve):
                nc.vector.tensor_copy(row_edges[:], acc[:, :, AW - 1]).then_inc(copied, 1)
        x = sb(ctx, "x_second", [P, NB, D])
        load_x(nc, st, "x_second", a["x"], x)
        x_dram = dram("x_between", (P, NB, D))
        attention_output(nc, st, acc, x, a["L0_gnn_Wo"], a["L0_gnn_bo"], ident, ones, x_dram)
    st.hand_back()

    with ExitStack() as ctx:
        x = sb(ctx, "x", [P, NB, D])
        move(nc, st, "x_in", [(x[:], x_dram)])

        y_dram = dram("mixture_y", (T1 * P, D))
        with ExitStack() as ffn:
            share = [sb(ffn, f"share{k}", [P, NB]) for k in range(2)]
            scatter = [sb(ffn, f"scatter{k}", [P, NB], I32) for k in range(2)]
            gather = [sb(ffn, f"gather{k}", [P, NB], I32) for k in range(2)]
            expert_of = sb(ffn, "expert_of", [1, T1], I32)
            gamma, beta = sb(ffn, "gamma", [P, DC]), sb(ffn, "beta", [P, DC])
            load_columns(nc, st, "affine", [(gamma[:], a["L0_ffn_gamma"]), (beta[:], a["L0_ffn_beta"])])
            with ExitStack() as router:
                xt = sb(router, "xt_first", [P, DC, NB * P])
                lines = sb(router, "ln_lines", [P, UNROLL, D])
                pick = [sb(router, f"pick{k}", [P, NB, EX]) for k in range(2)]
                layernorm_stats(nc, st, "ln_outer", x, stats, mean, rstd, tmp)
                layernorm_stats(nc, st, "ln_inner", x, stats, mean2, rstd2, tmp, inner=(mean, rstd, lines))
                affine = ((mean, rstd), (mean2, rstd2))
                turn(nc, st, "turn_first", x, affine, xt, ident, gamma, beta)
                route_two(nc, st, xt, a["L0_ffn_Wr"], a["L0_ffn_br"], order, ident, pick, share)
                slots(nc, st, "mixture_slots", pick, scatter, gather, expert_of, ones, iota_part, before, T1)
            scatter_rows(nc, st, "mixture_scatter", x, affine, scatter, rows_dram[0])
            mixture_tiles(nc, st, rows_dram[0], y_dram, expert_of, a["L0_ffn_W1"], a["L0_ffn_b1"], a["L0_ffn_W2"],
                          a["L0_ffn_b2"], gamma, beta, ident)
            gather_rows(nc, st, "mixture_gather", y_dram, gather, share, x)
        st.hand_back()

        with ExitStack() as gnn:
            gate = sb(gnn, "gate", [P, D])
            h, dis, g = sb(gnn, "h", [P, NB]), sb(gnn, "dis", [P, NB]), sb(gnn, "g", [P, NB])
            sums = sb(gnn, "neighbour_sums", [P, NB])
            layernorm_stats(nc, st, "ln_gates", x, stats, mean, rstd, tmp)
            with ExitStack() as turned:
                xt = sb(turned, "xt_second", [P, DC, NB * P])
                turn(nc, st, "turn_second", x, ((mean, rstd),), xt, ident)
                gate_and_values(nc, st, xt, a["L1_gnn_w1"], a["L1_gnn_b1"], a["L1_gnn_w2"], a["L1_gnn_b2"],
                                a["L1_gnn_gcn_w"], h_dram, ident, gate, h)
            graph_values(nc, st, h, degree, dis, g, g_dram, ident)
            with ExitStack() as edges:
                col_lo, col_hi = sb(edges, "col_lo_again", [P, NI]), sb(edges, "col_hi_again", [P, NI])
                weight = sb(edges, "weight", [P, NI])
                split_columns(nc, st, "split_again", scratch["cols"], col_lo, col_hi)
                value_of_rows(nc, st, row_edges, g, g_dram, scratch["rows"], placed_dram, ones, before, weight)
                scatter_to_columns(nc, st, "neighbours", weight, col_lo, col_hi, iota_free, ident, sums)
            gated_update(nc, st, x, mean, rstd, dis, g, sums, a["L1_gnn_gcn_b"], gate)

        st.hand_back()

        with ExitStack() as ffn:
            hidden_channels = a["L1_ffn_W1"].shape[1]
            y_dram = dram("routed_y", (T2 * P, D))
            share = sb(ffn, "routed_share", [P, NB])
            scatter, gather = sb(ffn, "routed_scatter", [P, NB], I32), sb(ffn, "routed_gather", [P, NB], I32)
            expert_of = sb(ffn, "routed_expert_of", [1, T2], I32)
            w1_sb, b1_sb = sb(ffn, "routed_w1", [P, DC, hidden_channels]), sb(ffn, "routed_b1", [P, hidden_channels // P])
            move(nc, st, "routed_w1", [(w1_sb[:], a["L1_ffn_W1"].rearrange("(c p) n -> p c n", p=P))])
            load_columns(nc, st, "routed_b1", [(b1_sb[:], a["L1_ffn_b1"])])
            layernorm_stats(nc, st, "ln_routed", x, stats, mean, rstd, tmp)
            affine = ((mean, rstd),)
            wd, bd = a["L1_ffn_Wd"], a["L1_ffn_bd"]
            wd_sb, bd_sb = sb(ffn, "routed_wd", [P, EX, hidden_channels // P, D]), sb(ffn, "routed_bd", [P, EX, D])
            experts = [(wd_sb[:, e, :, :], wd[e].rearrange("(c p) d -> p c d", p=P)) for e in range(EX)]
            experts.append((bd_sb[:].rearrange("p e n -> p (e n)"),
                            bd.rearrange("e n -> (e n)").unsqueeze(0).to_broadcast([P, EX * D])))
            fetched = st.sem("routed_experts_fetched")
            with ExitStack() as router:
                xt = sb(router, "xt_third", [P, DC, NB * P])
                pick = sb(router, "routed_pick", [P, NB, EX])
                turn(nc, st, "turn_third", x, affine, xt, ident)
                route_one(nc, st, xt, w1_sb, b1_sb, a["L1_ffn_Wg"], a["L1_ffn_bg"], order, ident, pick, share, experts, fetched)
                slots(nc, st, "routed_slots", [pick], [scatter], [gather], expert_of, ones, iota_part, before, T2)
            scatter_rows(nc, st, "routed_scatter", x, affine, [scatter], rows_dram[1])
            routed_tiles(nc, st, rows_dram[1], y_dram, expert_of, w1_sb, b1_sb, wd_sb, bd_sb, fetched, ident)
            gather_rows(nc, st, "routed_gather", y_dram, [gather], [share], x)
        move(nc, st, "result", [(out[0:FULL * P, :].rearrange("(b p) d -> p b d", p=P), x[:, 0:FULL, :]),
                                (out[FULL * P:N, :], x[0:TAIL, FULL, :])])
    keep.close()


def kernel(**inputs):
    import numpy as _np
    import concourse.bacc as _bacc
    from concourse.bass_utils import run_bass_kernel_spmd as _run

    nc = _bacc.Bacc("TRN2", target_bir_lowering=False, num_devices=1)
    arrays, aps = {}, {}
    for name, value in inputs.items():
        value = _np.ascontiguousarray(value)
        arrays[f"in_{name}"] = value
        aps[name] = nc.dram_tensor(f"in_{name}", value.shape, mybir.dt.from_np(value.dtype), kind="ExternalInput").ap()
    out = nc.dram_tensor("out", (N, D), F32, kind="ExternalOutput").ap()
    build(nc, aps, out)
    result = _run(nc, [arrays], core_ids=[0])
    return result.results[0]["out"]
```
